# Optimizing a Trainium2 kernel written in Bass

```python
import numpy as np
import jax
import jax.numpy as jnp

def _softmax(x, axis=-1):
    return jax.nn.softmax(x, axis=axis)

def _gelu(x):
    return jax.nn.gelu(x, approximate=True)

def _silu(x):
    return jax.nn.silu(x)

def _sigmoid(x):
    return jax.nn.sigmoid(x)

def _layernorm(x, axis=-1, eps=1e-05):
    m = jnp.mean(x, axis=axis, keepdims=True)
    v = jnp.var(x, axis=axis, keepdims=True)
    return (x - m) / jnp.sqrt(v + eps)

def _scatter_add(tgt, idx, src, axis=0):
    return tgt.at[idx].add(src)

def _segment_sum(src, seg, n):
    return jax.ops.segment_sum(src, seg, n)
kernel_name = 'mk_vit_tower_postln_d1_tok_img2048_r4_b4a069'

def setup_inputs(seed: int=0):
    np.random.seed(seed)
    _w = jnp.asarray

    def _rec_inputs():
        import jax
        import jax.numpy as jnp
        _rk = jax.random.key(seed)
        x = -0.00178296 + 0.498989 * jax.random.normal(jax.random.fold_in(_rk, 1), (8, 256, 64, 2), jnp.float32)
        return x
    x = _rec_inputs()

    def _L0_tok_setup():
        import jax, jax.numpy as jnp
        import numpy as np
        H, N, CCH, LLEN = (256, 64, 1, 512)
        key = jax.random.key(seed)
        k1, k2 = jax.random.split(key, 2)
        log_dt = jax.random.uniform(k1, (H,), jnp.float32, float(np.log(0.001)), float(np.log(0.1)))
        C = 0.5 * jax.random.normal(k2, (CCH, H, N, 2), jnp.float32)
        log_w_real = jnp.full((H, N), float(np.log(0.5)), jnp.float32)
        w_imag = jnp.broadcast_to(np.pi * jnp.arange(N, dtype=jnp.float32), (H, N)) + jnp.zeros((H, N), jnp.float32)
        return {'C': C, 'log_dt': log_dt, 'log_w_real': log_w_real, 'w_imag': w_imag, 'L': LLEN}
    _L0_tok_all = _L0_tok_setup()
    _L0_tok_in = {k: v for k, v in _L0_tok_all.items() if k in ('log_dt', 'log_w_real', 'w_imag')}
    del _L0_tok_all

    def _L0_attn_setup():
        import jax, jax.numpy as jnp
        import numpy as np
        B, S, E, H = (2, 512, 512, 16)
        HD = E // H
        INIT_LAMBDA = 0.8

        def rope_cos_sin(seqlen, head_dim, dtype):
            inv = 1.0 / 10000.0 ** (jnp.arange(0, head_dim, 2, dtype=jnp.float32) / head_dim)
            ang = jnp.arange(seqlen, dtype=jnp.float32)[:, None] * inv[None, :]
            ang = jnp.concatenate([ang, ang], axis=-1)
            return (jnp.cos(ang).astype(dtype), jnp.sin(ang).astype(dtype))

        def apply_rope(x, cos, sin):
            d = x.shape[-1]
            x1, x2 = (x[..., :d // 2], x[..., d // 2:])
            rot = jnp.concatenate([-x2, x1], axis=-1)
            return x * cos + rot * sin
        key = jax.random.key(seed)
        ks = jax.random.split(key, 9)
        return {'x': jax.random.normal(ks[0], (B, S, E), jnp.float32), 'w_qkv': jax.random.normal(ks[1], (3 * E, E), jnp.float32) * 0.02, 'wo': jax.random.normal(ks[2], (E, E), jnp.float32) * 0.02, 'lambda_q1': jax.random.normal(ks[3], (HD,), jnp.float32) * 0.1, 'lambda_q2': jax.random.normal(ks[4], (HD,), jnp.float32) * 0.1, 'lambda_k1': jax.random.normal(ks[5], (HD,), jnp.float32) * 0.1, 'lambda_k2': jax.random.normal(ks[6], (HD,), jnp.float32) * 0.1, 'gamma': jnp.ones((E,), jnp.float32), 'beta': jnp.zeros((E,), jnp.float32)}
    _L0_attn_all = _L0_attn_setup()
    _L0_attn_in = {k: v for k, v in _L0_attn_all.items() if k in ('w_qkv', 'wo', 'lambda_q1', 'lambda_q2', 'lambda_k1', 'lambda_k2', 'gamma', 'beta')}
    del _L0_attn_all

    def _L0_ffn_setup():
        import jax, jax.numpy as jnp
        import numpy as np
        H = 512
        E = 64
        I = 128
        SI = 128
        TOP_K = 8
        B, T = (2, 128)
        key = jax.random.key(seed)
        ks = jax.random.split(key, 8)
        s = 0.02
        return {'h': jax.random.normal(ks[0], (B, T, H), jnp.float32), 'gate_w': jax.random.normal(ks[1], (E, H), jnp.float32) * s, 'gu_w': jax.random.normal(ks[2], (E, 2 * I, H), jnp.float32) * s, 'dp_w': jax.random.normal(ks[3], (E, H, I), jnp.float32) * s, 'sh_gate_w': jax.random.normal(ks[4], (SI, H), jnp.float32) * s, 'sh_up_w': jax.random.normal(ks[5], (SI, H), jnp.float32) * s, 'sh_down_w': jax.random.normal(ks[6], (H, SI), jnp.float32) * s, 'sh_gate1_w': jax.random.normal(ks[7], (1, H), jnp.float32) * s}
    _L0_ffn_all = _L0_ffn_setup()
    _L0_ffn_in = {k: v for k, v in _L0_ffn_all.items() if k in ('gate_w', 'gu_w', 'dp_w', 'sh_gate_w', 'sh_up_w', 'sh_down_w', 'sh_gate1_w')}
    del _L0_ffn_all
    return {'x': x, 'L0_tok_log_dt': _L0_tok_in['log_dt'], 'L0_tok_log_w_real': _L0_tok_in['log_w_real'], 'L0_tok_w_imag': _L0_tok_in['w_imag'], 'L0_attn_w_qkv': _L0_attn_in['w_qkv'], 'L0_attn_wo': _L0_attn_in['wo'], 'L0_attn_lambda_q1': _L0_attn_in['lambda_q1'], 'L0_attn_lambda_q2': _L0_attn_in['lambda_q2'], 'L0_attn_lambda_k1': _L0_attn_in['lambda_k1'], 'L0_attn_lambda_k2': _L0_attn_in['lambda_k2'], 'L0_attn_gamma': _L0_attn_in['gamma'], 'L0_attn_beta': _L0_attn_in['beta'], 'L0_ffn_gate_w': _L0_ffn_in['gate_w'], 'L0_ffn_gu_w': _L0_ffn_in['gu_w'], 'L0_ffn_dp_w': _L0_ffn_in['dp_w'], 'L0_ffn_sh_gate_w': _L0_ffn_in['sh_gate_w'], 'L0_ffn_sh_up_w': _L0_ffn_in['sh_up_w'], 'L0_ffn_sh_down_w': _L0_ffn_in['sh_down_w'], 'L0_ffn_sh_gate1_w': _L0_ffn_in['sh_gate1_w']}

def reference(x, L0_tok_log_dt, L0_tok_log_w_real, L0_tok_w_imag, L0_attn_w_qkv, L0_attn_wo, L0_attn_lambda_q1, L0_attn_lambda_q2, L0_attn_lambda_k1, L0_attn_lambda_k2, L0_attn_gamma, L0_attn_beta, L0_ffn_gate_w, L0_ffn_gu_w, L0_ffn_dp_w, L0_ffn_sh_gate_w, L0_ffn_sh_up_w, L0_ffn_sh_down_w, L0_ffn_sh_gate1_w):
    import jax
    import jax.numpy as jnp

    def _L0_tok_ref(C, log_dt, log_w_real, w_imag, L):
        import jax, jax.numpy as jnp
        import numpy as np
        H, N, CCH, LLEN = (256, 64, 1, 512)
        dt = jnp.exp(log_dt)
        Cc = C[..., 0] + 1j * C[..., 1]
        w = -jnp.exp(log_w_real) + 1j * w_imag
        dtA = w * dt[:, None]
        K = dtA[:, :, None] * jnp.arange(L)
        Cm = Cc * (jnp.exp(dtA) - 1.0) / w
        K = jnp.einsum('chn,hnl->chl', Cm, jnp.exp(K))
        return 2 * K.real

    def _L0_attn_ref(x, w_qkv, wo, lambda_q1, lambda_q2, lambda_k1, lambda_k2, gamma, beta):
        import jax, jax.numpy as jnp
        import numpy as np
        B, S, E, H = (2, 512, 512, 16)
        HD = E // H
        INIT_LAMBDA = 0.8

        def rope_cos_sin(seqlen, head_dim, dtype):
            inv = 1.0 / 10000.0 ** (jnp.arange(0, head_dim, 2, dtype=jnp.float32) / head_dim)
            ang = jnp.arange(seqlen, dtype=jnp.float32)[:, None] * inv[None, :]
            ang = jnp.concatenate([ang, ang], axis=-1)
            return (jnp.cos(ang).astype(dtype), jnp.sin(ang).astype(dtype))

        def apply_rope(x, cos, sin):
            d = x.shape[-1]
            x1, x2 = (x[..., :d // 2], x[..., d // 2:])
            rot = jnp.concatenate([-x2, x1], axis=-1)
            return x * cos + rot * sin
        b, s, e = x.shape
        hd = e // H
        scaler = hd ** (-0.5)
        qkv = x @ w_qkv.T
        q, k, v = jnp.split(qkv, 3, axis=-1)
        to_heads = lambda t: t.reshape(b, s, H, hd).transpose(0, 2, 1, 3)
        q, k, v = (to_heads(q), to_heads(k), to_heads(v))
        cos, sin = rope_cos_sin(s, hd, x.dtype)
        q = apply_rope(q, cos, sin)
        k = apply_rope(k, cos, sin)
        q1, q2 = jnp.split(q, 2, axis=-1)
        k1, k2 = jnp.split(k, 2, axis=-1)
        lam = (jnp.exp(jnp.sum(lambda_q1 * lambda_k1)) - jnp.exp(jnp.sum(lambda_q2 * lambda_k2)) + INIT_LAMBDA).astype(x.dtype)
        add_mask = jnp.triu(jnp.ones((s, s), x.dtype), k=1)

        def sdpa(qh, kh):
            scores = jnp.einsum('bhqd,bhkd->bhqk', qh, kh) * scaler + add_mask
            p = jax.nn.softmax(scores, axis=-1)
            return jnp.einsum('bhqk,bhkd->bhqd', p, v)
        out = sdpa(q1, k1) - lam * sdpa(q2, k2)
        y = out.transpose(0, 2, 1, 3).reshape(b, e, s)
        yg = y.reshape(b, H, e // H * s)
        mean = jnp.mean(yg, axis=-1, keepdims=True)
        var = jnp.var(yg, axis=-1, keepdims=True)
        yn = ((yg - mean) * jax.lax.rsqrt(var + 1e-05)).reshape(b, e, s)
        yn = yn * gamma[None, :, None] + beta[None, :, None]
        y = (yn * (1.0 - INIT_LAMBDA)).reshape(b, s, e)
        return y @ wo.T

    def _L0_ffn_ref(h, gate_w, gu_w, dp_w, sh_gate_w, sh_up_w, sh_down_w, sh_gate1_w):
        import jax, jax.numpy as jnp
        import numpy as np
        H = 512
        E = 64
        I = 128
        SI = 128
        TOP_K = 8
        B, T = (2, 128)
        Bb, Tt, Hh = h.shape
        x = h.reshape(Bb * Tt, Hh)
        N = x.shape[0]
        logits = x @ gate_w.T
        topv, topi = jax.lax.top_k(logits, TOP_K)
        rw = jax.nn.softmax(topv.astype(jnp.float32), axis=-1).astype(x.dtype)
        W = jnp.zeros((N, E), x.dtype).at[jnp.arange(N)[:, None], topi].set(rw)
        gu = jnp.einsum('nh,eih->nei', x, gu_w)
        gate, up = (gu[..., :I], gu[..., I:])
        inter = jax.nn.silu(gate) * up
        inter_w = inter * W[:, :, None]
        out = jnp.einsum('nei,ehi->nh', inter_w, dp_w)
        sh_inter = jax.nn.silu(x @ sh_gate_w.T) * (x @ sh_up_w.T)
        sh_out = sh_inter @ sh_down_w.T
        sh_g = jax.nn.sigmoid(x @ sh_gate1_w.T)
        out = out + sh_g * sh_out
        return out.reshape(Bb, Tt, Hh)
    h = _L0_tok_ref(x, L0_tok_log_dt, L0_tok_log_w_real, L0_tok_w_imag, 512)
    h = _layernorm(h + _L0_attn_ref(h, L0_attn_w_qkv, L0_attn_wo, L0_attn_lambda_q1, L0_attn_lambda_q2, L0_attn_lambda_k1, L0_attn_lambda_k2, L0_attn_gamma, L0_attn_beta), axis=-1)
    h = _layernorm(h + _L0_ffn_ref(h, L0_ffn_gate_w, L0_ffn_gu_w, L0_ffn_dp_w, L0_ffn_sh_gate_w, L0_ffn_sh_up_w, L0_ffn_sh_down_w, L0_ffn_sh_gate1_w), axis=-1)
    return h

_drawn_inputs = setup_inputs


def setup_inputs(seed=0):
    import zlib

    import numpy as np

    out = dict(_drawn_inputs(seed))
    spreads = {'L0_tok_log_w_real': (-0.6931471824645996, 0.2),
     'L0_attn_gamma': (1.0, 0.6),
     'L0_attn_beta': (0.0, 0.1)}
    factors = {'L0_ffn_gate_w': 6.873,
     'L0_ffn_gu_w': 6.46,
     'L0_ffn_dp_w': 6.465,
     'L0_ffn_sh_gate_w': 4.648,
     'L0_ffn_sh_up_w': 4.51,
     'L0_ffn_sh_down_w': 4.528,
     'L0_ffn_sh_gate1_w': 8.0}
    for name, (base, spread) in spreads.items():
        noise = np.random.default_rng([zlib.crc32(name.encode()), seed]).standard_normal(out[name].shape)
        drawn = base * np.exp(spread * noise) if base else spread * noise
        out[name] = jnp.asarray(drawn.astype(out[name].dtype))
    for name, factor in factors.items():
        out[name] = (out[name] * factor).astype(out[name].dtype)
    return out
```

```python
import concourse.bass as bass
from concourse import mybir
from contextlib import ExitStack
import math
import numpy as np

F32 = mybir.dt.float32
F32R = mybir.dt.float32r
BF16 = mybir.dt.bfloat16
I32 = mybir.dt.int32
U32 = mybir.dt.uint32
ACT = mybir.ActivationFunctionType
ALU = mybir.AluOpType
AX = mybir.AxisListType

P = 128
BATCH, SEQ, MODES, LEN = 8, 256, 64, 512
TOK = BATCH * SEQ
TILES = TOK // P
FCH = LEN // P
FINE = 64
COARSE = LEN // FINE
ROUND = 1.5 * 2.0 ** 23
TURN = 6.2831845
INV_TURN = 1.0 / (2.0 * math.pi)

CONST = {}


def const_table():
    parts = {}
    p = np.arange(P)
    parts["ident"] = np.eye(P)
    parts["before"] = (p[:, None] < p[None, :]) * 1.0
    parts["ones"] = np.ones((P, P))
    parts["group"] = (p[:, None] // 16 == p[None, :] // 16) * (1.0 / 16)
    tri = (p[None, :] > p[:, None]) * 1.0
    one, zero = np.ones((P, P)), np.zeros((P, P))
    parts["mask"] = np.concatenate([tri, one, zero, tri], 1)
    inv = np.float32(1.0) / np.power(np.float32(10000.0), np.arange(0, 32, 2, dtype=np.float32) / np.float32(32))
    ang = np.arange(SEQ, dtype=np.float32)[:, None] * inv[None, :].astype(np.float32)
    cos, sin = np.cos(ang), np.sin(ang)
    scaler = np.float32(32) ** np.float32(-0.5)
    for name, f in (("q", scaler), ("k", np.float32(1))):
        c = np.concatenate([cos, cos], 1) * f
        s = np.concatenate([-sin, sin], 1) * f
        for u in range(2):
            parts[f"cos_{name}{u}"] = c[u * P:(u + 1) * P]
            parts[f"sin_{name}{u}"] = s[u * P:(u + 1) * P]
    row = lambda v: np.broadcast_to(np.asarray(v, np.float64), (P, len(v)))
    parts["fine"] = row(np.arange(FINE))
    parts["coarse"] = row(np.arange(COARSE) * FINE)
    parts["experts"] = row(np.arange(64))
    parts["tiles128"] = row(np.arange(16) * 128)
    half = (p >= 64) * 1.0
    parts["phase_v"] = (0.25 - 0.25 * half)[:, None]
    parts["phase_a"] = (0.25 + 0.25 * half)[:, None]
    parts["phase_b"] = (0.50 + 0.25 * half)[:, None]
    parts["minus_half"] = np.full((P, 1), -0.5)
    parts["eps"] = np.full((P, 1), 1e-5)
    parts["lane"] = p[:, None] * 1.0
    at = 0
    for name, a in parts.items():
        CONST[name] = (at, a.shape[1])
        at += a.shape[1]
    return np.ascontiguousarray(np.concatenate(list(parts.values()), 1).astype(np.float32))


class Steps:

    def __init__(self, sem):
        self.sem, self.start, self.n = sem, 0, 0

    def inc(self, ins):
        ins.then_inc(self.sem, 1)
        self.n += 1
        return self.n

    def wait(self, engine, n=None):
        engine.wait_ge(self.sem, self.start + (self.n if n is None else n))


def bc(ap, axis, n):
    a = ap.unsqueeze(axis)
    shape = list(a.shape)
    shape[axis] = n
    return a.to_broadcast(shape)


def tok_phase(nc, c_in, log_dt, lwr, wim, consts, hT):
    HB = 16
    NB = SEQ // HB
    with ExitStack() as ctx:
        sb = lambda n, s, d=F32: ctx.enter_context(nc.sbuf_tensor("a_" + n, s, d))
        sem = lambda n: ctx.enter_context(nc.semaphore("a_" + n))
        C = sb("C", [P, 2, SEQ, BATCH])
        ldt, lw, wi = sb("ldt", [P, SEQ]), sb("lw", [P, SEQ]), sb("wi", [P, SEQ])
        sm = sb("small", [P, 14, SEQ])
        dt, ew, dr, di, ti, e, th, rs, rc, s_, c_, qr, qi, tmp = [sm[:, i, :] for i in range(14)]
        tmpb, er, ei = ldt[:], th, dt
        U = sb("U", [P, 4, SEQ, COARSE])
        mag, ta, tb, work = [U[:, i] for i in range(4)]
        A, B = sb("A", [P, SEQ, COARSE]), sb("B", [P, SEQ, COARSE])
        EV = sb("EV", [P, SEQ, FINE])
        tT, t2, kk, V = [U[:, i].rearrange("p (t h x) a -> p t h (x a)", t=2, h=HB) for i in range(4)]
        G = sb("G", [P, 2, HB, COARSE, BATCH])
        G2 = sb("G2", [P, 2, HB, COARSE, BATCH])
        ps = ctx.enter_context(nc.psum_tensor("a_ps", [P, 2, HB, FCH, BATCH], F32))
        loaded = sem("loaded")
        dve_s, act_s, pool_s = sem("dve"), sem("act"), sem("pool")
        angle, phased, rounded, residue, sine = sem("angle"), sem("phased"), sem("rounded"), sem("residue"), sem("sine")
        v_ready, g2_ready, g_ready, products, evac = sem("v"), sem("g2"), sem("g"), sem("products"), sem("evac")
        exps_in, exps = sem("exps_in"), sem("exps")
        g1_free = sem("g1")
        cst = lambda n: consts[:, CONST[n][0]:CONST[n][0] + CONST[n][1]]
        EB = 32
        with nc.Block() as block:
            @block.sync
            def _(sp):
                sp.dma_start(ldt[:], log_dt.partition_broadcast(P)).then_inc(loaded, 16)
                for h in range(2):
                    lo, hi = 64 * h, 64 * h + 64
                    sp.dma_start(lw[lo:hi, :], lwr).then_inc(loaded, 16)
                    sp.dma_start(wi[lo:hi, :], wim).then_inc(loaded, 16)
                    for r in range(2):
                        sp.dma_start(C[lo:hi, r], c_in[r]).then_inc(loaded, 16)
                sp.wait_ge(loaded, 16 * 9)

            @block.gpsimd
            def _(pool):
                pool.wait_ge(dve_s, 3)
                for i in range(SEQ // EB):
                    hs = slice(i * EB, (i + 1) * EB)
                    nc.gpsimd.tensor_tensor(EV[:, hs], bc(dr[:, hs], 2, FINE), bc(cst("fine"), 1, EB), ALU.mult).then_inc(exps_in, 1)
                pool.wait_ge(dve_s, TABLES)
                with nc.gpsimd.Fori(0, NB // 2) as i:
                    for par in range(2):
                        n = i * 2 + par
                        hs = bass.ds(n * HB, HB)
                        pool.wait_ge(phased, n + 1)
                        nc.gpsimd.tensor_tensor(tT[:, par], bc(di[:, hs], 2, FINE), bc(cst("fine"), 1, HB), ALU.mult).then_inc(angle, 1)
                        pool.wait_ge(g_ready, n + 1)
                        nc.gpsimd.tensor_tensor(G2[:, par], bc(C[:, 1, hs], 2, COARSE), bc(B[:, hs], 3, BATCH), ALU.mult).then_inc(g2_ready, 1)

            @block.vector
            def _(dve):
                st = Steps(dve_s)
                V_ = nc.vector

                def do(ins, wait=True):
                    st.inc(ins)
                    if wait:
                        st.wait(dve)

                dve.wait_ge(act_s, 2)
                do(V_.tensor_tensor(dr, ew, dt, ALU.mult), False)
                dve.wait_ge(loaded, 16 * 9)
                do(V_.tensor_tensor(di, wi[:], dt, ALU.mult))
                do(V_.tensor_scalar(di, di, INV_TURN, None, ALU.mult))
                do(V_.tensor_tensor(mag, bc(dr, 2, COARSE), bc(cst("coarse"), 1, SEQ), ALU.mult))
                do(V_.tensor_tensor(ta, bc(di, 2, COARSE), bc(cst("coarse"), 1, SEQ), ALU.mult))
                do(V_.tensor_scalar(ti, di, 0.5, None, ALU.mult))
                do(V_.tensor_scalar(tmp, ti, ROUND, ROUND, ALU.add, ALU.subtract))
                do(V_.tensor_tensor(rs, tmp, ti, ALU.subtract))
                do(V_.tensor_scalar(ti, ti, 0.25, None, ALU.add))
                do(V_.tensor_scalar(tmp, ti, ROUND, ROUND, ALU.add, ALU.subtract))
                do(V_.tensor_tensor(rc, tmp, ti, ALU.subtract))
                do(V_.tensor_scalar(tb, ta, cst("phase_b"), None, ALU.add))
                do(V_.tensor_scalar(ta, ta, cst("phase_a"), None, ALU.add))
                do(V_.tensor_scalar(work, ta, ROUND, ROUND, ALU.add, ALU.subtract))
                do(V_.tensor_tensor(ta, work, ta, ALU.subtract))
                do(V_.tensor_scalar(work, tb, ROUND, ROUND, ALU.add, ALU.subtract))
                do(V_.tensor_tensor(tb, work, tb, ALU.subtract))
                assert st.n == ANGLES
                dve.wait_ge(act_s, 2 + 3)
                do(V_.scalar_tensor_tensor(th, e, 1.0, th, ALU.add, ALU.mult))
                dve.wait_ge(act_s, 2 + 3 + 2)
                do(V_.tensor_tensor(tmp, s_, s_, ALU.mult), False)
                do(V_.tensor_tensor(tmpb, s_, c_, ALU.mult))
                do(V_.scalar_tensor_tensor(tmp, tmp, -2.0, e, ALU.mult, ALU.mult), False)
                do(V_.scalar_tensor_tensor(ei, tmpb, 2.0, e, ALU.mult, ALU.mult))
                do(V_.tensor_tensor(er, th, tmp, ALU.add))
                do(V_.tensor_tensor(tmp, ew, ew, ALU.mult), False)
                do(V_.tensor_tensor(tmpb, wi[:], wi[:], ALU.mult))
                do(V_.tensor_tensor(tmp, tmp, tmpb, ALU.add))
                do(V_.reciprocal(tmp, tmp))
                do(V_.tensor_tensor(qr, ei, wi[:], ALU.mult), False)
                do(V_.tensor_tensor(tmpb, er, ew, ALU.mult))
                do(V_.tensor_tensor(qr, qr, tmpb, ALU.subtract))
                do(V_.tensor_tensor(qr, qr, tmp, ALU.mult))
                do(V_.tensor_tensor(qi, er, wi[:], ALU.mult), False)
                do(V_.tensor_tensor(tmpb, ei, ew, ALU.mult))
                do(V_.tensor_tensor(qi, qi, tmpb, ALU.add))
                do(V_.scalar_tensor_tensor(qi, qi, -1.0, tmp, ALU.mult, ALU.mult))
                dve.wait_ge(act_s, 2 + 3 + 2 + 2)
                do(V_.tensor_tensor(ta, ta, mag, ALU.mult), False)
                do(V_.tensor_tensor(tb, tb, mag, ALU.mult))
                do(V_.tensor_tensor(A[:], ta, bc(qr, 2, COARSE), ALU.mult), False)
                do(V_.tensor_tensor(work, tb, bc(qi, 2, COARSE), ALU.mult))
                do(V_.tensor_tensor(A[:], A[:], work, ALU.add), False)
                do(V_.tensor_tensor(B[:], tb, bc(qr, 2, COARSE), ALU.mult), False)
                do(V_.tensor_tensor(mag, ta, bc(qi, 2, COARSE), ALU.mult))
                do(V_.tensor_tensor(B[:], B[:], mag, ALU.subtract))
                assert st.n == TABLES, st.n
                V_.tensor_copy(tmp, tmp).then_inc(g_ready, 1)
                V_.tensor_copy(tmpb, tmpb).then_inc(v_ready, 1)
                dve.wait_ge(exps, SEQ // EB)
                with V_.Fori(0, NB // 2) as i:
                    for par in range(2):
                        n = i * 2 + par
                        hs = bass.ds(n * HB, HB)
                        dve.wait_ge(rounded, n + 1)
                        V_.scalar_tensor_tensor(kk[:, par], kk[:, par], ROUND, t2[:, par], ALU.subtract, ALU.subtract).then_inc(residue, 1)
                        dve.wait_ge(products, n)
                        V_.tensor_tensor(G[:, par], bc(C[:, 0, hs], 2, COARSE), bc(A[:, hs], 3, BATCH), ALU.mult).then_inc(g1_free, 1)
                        dve.wait_ge(g1_free, n + 1)
                        dve.wait_ge(g2_ready, n + 1)
                        V_.tensor_tensor(G[:, par], G[:, par], G2[:, par], ALU.add).then_inc(g_ready, 1)
                        dve.wait_ge(sine, n + 1)
                        V_.tensor_tensor(V[:, par], kk[:, par], EV[:, hs], ALU.mult).then_inc(v_ready, 1)

            @block.scalar
            def _(act):
                A_ = nc.scalar
                act.wait_ge(loaded, 16 * 9)
                A_.activation(dt, ldt[:], ACT.Exp).then_inc(act_s, 1)
                A_.activation(ew, lw[:], ACT.Exp).then_inc(act_s, 1)
                act.wait_ge(dve_s, 1)
                A_.activation(e, dr, ACT.Exp, scale=-1.0).then_inc(act_s, 1)
                A_.activation(th, dr, ACT.Tanh, scale=-0.5).then_inc(act_s, 1)
                act.wait_ge(dve_s, 4)
                A_.activation(mag, mag, ACT.Exp, scale=-1.0).then_inc(act_s, 1)
                for i in range(SEQ // EB):
                    act.wait_ge(exps_in, i + 1)
                    A_.activation(EV[:, i * EB:(i + 1) * EB], EV[:, i * EB:(i + 1) * EB], ACT.Exp, scale=-1.0).then_inc(exps, 1)
                act.wait_ge(dve_s, ANGLES)
                A_.activation(s_, rs, ACT.Sin, scale=-TURN).then_inc(act_s, 1)
                A_.activation(c_, rc, ACT.Sin, scale=-TURN).then_inc(act_s, 1)
                A_.activation(ta, ta, ACT.Sin, scale=-TURN).then_inc(act_s, 1)
                A_.activation(tb, tb, ACT.Sin, scale=-TURN).then_inc(act_s, 1)
                A_.copy(rs, rs).then_inc(phased, 1)

                def sines(n, par):
                    act.wait_ge(angle, n + 1)
                    A_.activation(t2[:, par], tT[:, par], ACT.Identity, bias=cst("phase_v")).then_inc(phased, 1)
                    act.wait_ge(phased, n + 2)
                    act.wait_ge(v_ready, n)
                    A_.activation(kk[:, par], t2[:, par], ACT.Copy, bias=ROUND).then_inc(rounded, 1)
                    act.wait_ge(residue, n + 1)
                    A_.activation(kk[:, par], kk[:, par], ACT.Sin, scale=-TURN).then_inc(sine, 1)

                def evacuate(n, par):
                    act.wait_ge(products, n + 2)
                    out = hT[:].rearrange("p j (c s) -> p j c s", c=BATCH)[:, :, :, bass.ds(n * HB, HB)]
                    A_.activation(out, ps[:, par].rearrange("p h j c -> p j c h"), ACT.Copy, scale=2.0).then_inc(evac, 1)

                sines(0, 0)
                with A_.Fori(0, NB // 2 - 1) as i:
                    for par in range(2):
                        sines(i * 2 + par + 1, 1 - par)
                        evacuate(i * 2 + par, par)
                sines(NB - 1, 1)
                evacuate(NB - 2, 0)
                evacuate(NB - 1, 1)

            @block.tensor
            def _(pe):
                pe.sem_inc(products, 1)
                pe.sem_inc(evac, 1)
                with nc.tensor.Fori(0, NB // 2) as i:
                    for par in range(2):
                        n = i * 2 + par
                        pe.wait_ge(g_ready, n + 2)
                        pe.wait_ge(v_ready, n + 2)
                        pe.wait_ge(evac, n)
                        for h in range(HB):
                            for odd in range(2):
                                ins = nc.tensor.matmul(ps[64 * odd:64 * odd + 64, par, h], V[:, par, h],
                                                       G[:, par, h].rearrange("p (j o) c -> p o j c", o=2)[:, odd],
                                                       start=True, stop=True)
                        ins.then_inc(products, 1)


ANGLES, TABLES = 17, 43



HEADS, HD = 16, 32
INIT_LAMBDA = 0.8


def attention_phase(nc, hT, y, w_qkv, lambdas, consts):
    UN = 2 * HEADS
    with ExitStack() as ctx:
        sb = lambda n, s, d=F32: ctx.enter_context(nc.sbuf_tensor("b_" + n, s, d))
        sem = lambda n: ctx.enter_context(nc.semaphore("b_" + n))
        pb = lambda n, s: ctx.enter_context(nc.psum_tensor("b_" + n, s, F32))
        cst = lambda n: consts[:, CONST[n][0]:CONST[n][0] + CONST[n][1]]
        W = sb("W", [P, FCH, 3 * LEN])
        hc = sb("hc", [P, FCH, SEQ])
        mulc, muls = sb("mulc", [P, LEN]), sb("muls", [P, LEN])
        xr = sb("xr", [P, 2, LEN])
        stack = sb("stack", [P, 2, UN, 4, 16])
        qk = [sb(f"qk{i}", [P, 2, HEADS, SEQ], F32R) for i in range(2)]
        Vb = sb("Vb", [P, 2, 2, LEN])
        E = sb("E", [P, 2, 2, SEQ])
        D = sb("D", [P, 2, SEQ])
        DT = sb("DT", [P, 2, 2, P])
        negmax, sums, mixw = sb("negmax", [P, 2, 2]), sb("sums", [P, 2, 2]), sb("mixw", [P, 2])
        recips = sb("recips", [P, 2, HEADS, 2])
        maskb, identb = sb("maskb", [P, 2, SEQ], BF16), sb("identb", [P, P], BF16)
        lam = sb("lam", [P, 4, HD])
        lamw = sb("lamw", [P, 2, HD])
        lams = sb("lams", [P, 4])
        pq = pb("pq", [P, 2, LEN])
        pS = pb("pS", [P, 2, 2, SEQ])
        pT = pb("pT", [P, 2, 4, P])
        pK = pb("pK", [P, 4, P])
        pO = pb("pO", [P, LEN])

        loaded, setup = sem("loaded"), sem("setup")
        s_hc, s_qkv, s_rm, s_xr, s_hi, s_lo = (sem(n) for n in ("hc", "qkv", "rope_mul", "roped", "hi", "lo"))
        s_qkb, s_qke, s_v = sem("qk_transposed"), sem("qk_evac"), sem("v_evac")
        s_scores, s_max, s_exp, s_small, s_d = (sem(n) for n in ("scores", "max", "exp", "small", "mixed"))
        s_t, s_dt, s_pv, s_y = (sem(n) for n in ("mixed_t", "mixed_t_evac", "pv", "y"))


        with nc.Block() as block:
            @block.sync
            def _(sp):
                for i, l in enumerate(lambdas):
                    sp.dma_start(lam[:, i, :], l.partition_broadcast(P)).then_inc(loaded, 16)
                sp.dma_start(W[:], w_qkv.rearrange("(j p) n -> p j n", p=P)).then_inc(loaded, 16)

            @block.gpsimd
            def _(pool):
                def prepare(b, t):
                    for x in range(2):
                        r = b * 4 + (2 * t + x)
                        pool.wait_ge(s_rm, r + 2)
                        nc.gpsimd.tensor_tensor(xr[:, x], mulc[:], muls[:], ALU.add).then_inc(s_xr, 1)
                        pool.wait_ge(s_hi, r + 1)
                        hi, lo = (0, 1) if x == 0 else (slice(0, 2), slice(2, 4))
                        src = xr[:, x].rearrange("p (m d) -> p m d", d=16)
                        if x == 0:
                            out = stack[:, x].rearrange("p m (a r) d -> p m a r d", r=2)[:, :, :, 1]
                        else:
                            out = stack[:, x, :, 2:4]
                        nc.gpsimd.tensor_tensor(out, bc(src, 2, 2), bc(stack[:, x, :, 0], 2, 2), ALU.subtract).then_inc(s_lo, 1)

                def batch(c, more):
                    if more:
                        prepare(c + 1, 0)
                        prepare(c + 1, 1)
                prepare(0, 0)
                prepare(0, 1)
                with nc.gpsimd.Fori(0, BATCH // 2 - 1) as i:
                    batch(i * 2, True)
                    batch(i * 2 + 1, True)
                batch(BATCH - 2, True)

            @block.vector
            def _(dve):
                V_ = nc.vector
                V_.tensor_copy(maskb[:], cst("mask")).then_inc(setup, 1)
                V_.tensor_copy(identb[:], cst("ident")).then_inc(setup, 1)
                dve.wait_ge(loaded, 80)
                V_.tensor_tensor(lamw[:], lam[:, 0:2], lam[:, 2:4], ALU.mult).then_inc(setup, 1)
                dve.wait_ge(setup, 3)
                V_.reduce_sum(lams[:, 0:2], lamw[:], AX.X).then_inc(setup, 1)
                dve.wait_ge(setup, 5)
                V_.tensor_tensor(lams[:, 2:3], lams[:, 1:2], lams[:, 0:1], ALU.subtract).then_inc(setup, 1)
                dve.wait_ge(setup, 6)
                V_.tensor_scalar(lams[:, 3:4], lams[:, 2:3], -INIT_LAMBDA, None, ALU.add).then_inc(setup, 1)
                dve.wait_ge(setup, 7)
                dve.sem_inc(s_rm, 1)
                dve.sem_inc(s_d, 2)

                def rope(b, t, x):
                    r = b * 4 + (2 * t + x)
                    name = "qk"[x]
                    dve.wait_ge(s_qkv, b * 6 + (3 * t + x + 1))
                    dve.wait_ge(s_xr, r)
                    src = pq[:, (3 * t + x) % 2].rearrange("p (h s d) -> p s h d", s=2, d=16)
                    cos = cst(f"cos_{name}{t}")[:, 0:16]
                    sin = cst(f"sin_{name}{t}")
                    V_.tensor_tensor(mulc[:].rearrange("p (s h d) -> p s h d", s=2, d=16), src,
                                     bc(bc(cos, 1, HEADS), 1, 2), ALU.mult)
                    ms = muls[:].rearrange("p (s h d) -> p s h d", s=2, d=16)
                    V_.tensor_tensor(ms[:, 0], src[:, 1], bc(sin[:, 0:16], 1, HEADS), ALU.mult)
                    V_.tensor_tensor(ms[:, 1], src[:, 0], bc(sin[:, 16:32], 1, HEADS), ALU.mult).then_inc(s_rm, 1)

                def evac(b, t, x, i, par):
                    w = b * 16 + (8 * t + 4 * x + i)
                    dve.wait_ge(s_qkb, w + 1 + 4)
                    V_.tensor_copy(qk[par][:, x, 4 * i:4 * i + 4, t * P:(t + 1) * P], pK[:]).then_inc(s_qke, 1)

                def negmax_of(n, k):
                    dve.wait_ge(s_scores, n + 1)
                    V_.tensor_reduce(negmax[:, k % 2], pS[:, k % 2], AX.X, ALU.max, negate=True).then_inc(s_max, 1)

                def mix(n, k):
                    u, h = divmod(k, HEADS)
                    dve.wait_ge(s_exp, n + 3)
                    V_.reciprocal(recips[:, u, h], sums[:, k % 2]).then_inc(s_small, 1)
                    dve.wait_ge(s_small, n * 2 + 1)
                    V_.scalar_tensor_tensor(mixw[:, k % 2:k % 2 + 1], sums[:, k % 2, 0:1], lams[:, 3:4], recips[:, u, h, 1:2],
                                            ALU.mult, ALU.mult).then_inc(s_small, 1)
                    dve.wait_ge(s_small, n * 2 + 2)
                    dve.wait_ge(s_t, n + 1)
                    V_.scalar_tensor_tensor(D[:, k % 2], E[:, k % 2, 1], mixw[:, k % 2:k % 2 + 1], E[:, k % 2, 0],
                                            ALU.mult, ALU.add).then_inc(s_d, 1)

                def finish(c, u):
                    dve.wait_ge(s_pv, c * UN + (HEADS * (u + 1) + 2))
                    V_.tensor_tensor(y[:, bass.ds(c * 2 + u, 1)].rearrange("p o (h d) -> p (o h) d", d=HD),
                                     pO[:].rearrange("p (h d) -> p h d", d=HD),
                                     bc(recips[:, u, :, 0], 2, HD), ALU.mult).then_inc(s_y, 1)

                def batch(c, par, more):
                    for k in range(UN):
                        n = c * UN + k
                        negmax_of(n, k)
                        if k >= 1:
                            mix(n - 1, k - 1)
                        if k == HEADS + 3:
                            finish(c, 0)
                        if more:
                            for piece in DVE_PIECES.get(k, ()):
                                (rope if piece[0] == "rope" else evac)(c + 1, *piece[1:], *(() if piece[0] == "rope" else (1 - par,)))
                    mix(c * UN + (UN - 1), UN - 1)
                    finish(c, 1)

                for t in range(2):
                    for x in range(2):
                        rope(0, t, x)
                    for x in range(2):
                        for i in range(4):
                            evac(0, t, x, i, 0)
                with V_.Fori(0, BATCH // 2 - 1) as i:
                    batch(i * 2, 0, True)
                    batch(i * 2 + 1, 1, True)
                batch(BATCH - 2, 0, True)
                batch(BATCH - 1, 1, False)

            @block.scalar
            def _(act):
                A_ = nc.scalar
                act.wait_ge(setup, 4)
                A_.activation(lams[:, 0:2], lams[:, 0:2], ACT.Exp).then_inc(setup, 1)
                act.sem_inc(s_exp, 2)
                act.sem_inc(s_dt, 2)

                def take(b):
                    act.wait_ge(s_qkv, b * 6)
                    A_.activation(hc[:], hT[:, :, bass.ds(b * SEQ, SEQ)], ACT.Copy).then_inc(s_hc, 1)

                def high(b, t, x):
                    r = b * 4 + (2 * t + x)
                    act.wait_ge(s_xr, r + 1)
                    act.wait_ge(s_qkb, r * 4)
                    if x == 0:
                        out = stack[:, x].rearrange("p m (a r) d -> p m a r d", r=2)[:, :, :, 0]
                    else:
                        out = stack[:, x, :, 0:2]
                    A_.activation(out.bitcast(F32R), bc(xr[:, x].rearrange("p (m d) -> p m d", d=16), 2, 2), ACT.Copy).then_inc(s_hi, 1)

                def values(b, t, par):
                    act.wait_ge(s_qkv, b * 6 + (3 * t + 3))
                    A_.activation(Vb[:, par, t], pq[:, (3 * t + 2) % 2], ACT.Copy).then_inc(s_v, 1)

                def exps(n, k):
                    act.wait_ge(s_max, n + 1)
                    act.wait_ge(s_d, n + 1)
                    for s in range(2):
                        ins = A_.activation(E[:, k % 2, s], pS[:, k % 2, s], ACT.Exp, bias=negmax[:, k % 2, s:s + 1],
                                            accum_out=sums[:, k % 2, s:s + 1])
                    ins.then_inc(s_exp, 1)

                def evac(n, k):
                    act.wait_ge(s_t, n + 3)
                    act.wait_ge(s_pv, n + 1)
                    A_.activation(DT[:, k % 2], pT[:, k % 2, 0:2], ACT.Copy).then_inc(s_dt, 1)

                def batch(c, par, more):
                    for k in range(UN):
                        n = c * UN + k
                        exps(n, k)
                        if k >= 2:
                            evac(n - 2, k - 2)
                        if more:
                            for piece in ACT_PIECES.get(k, ()):
                                if piece[0] == "take":
                                    take(c + 1)
                                elif piece[0] == "high":
                                    high(c + 1, *piece[1:])
                                else:
                                    values(c + 1, piece[1], 1 - par)
                    for k in (UN - 2, UN - 1):
                        evac(c * UN + k, k)

                take(0)
                for t in range(2):
                    high(0, t, 0)
                    high(0, t, 1)
                    values(0, t, 0)
                with A_.Fori(0, BATCH // 2 - 1) as i:
                    batch(i * 2, 0, True)
                    batch(i * 2 + 1, 1, True)
                batch(BATCH - 2, 0, True)
                batch(BATCH - 1, 1, False)

            @block.tensor
            def _(pe):
                T_ = nc.tensor
                pe.wait_ge(loaded, 80)
                pe.wait_ge(setup, 2)
                pe.sem_inc(s_qkb, 4)
                pe.sem_inc(s_t, 2)
                pe.sem_inc(s_pv, 2)

                def project(b, t, x):
                    pe.wait_ge(s_hc, b + 1)
                    if x == 0:
                        pe.wait_ge(s_rm, b * 4 + (2 * t + 1))
                    elif x == 1:
                        pe.wait_ge(s_v, b * 2 + t)
                    else:
                        pe.wait_ge(s_rm, b * 4 + (2 * t + 2))
                    for j in range(FCH):
                        ins = T_.matmul(pq[:, (3 * t + x) % 2], hc[:, j, t * P:(t + 1) * P], W[:, j, x * LEN:(x + 1) * LEN],
                                        start=(j == 0), stop=(j == FCH - 1))
                    ins.then_inc(s_qkv, 1)

                def turn(b, t, x, i):
                    w = b * 16 + (8 * t + 4 * x + i)
                    pe.wait_ge(s_lo, b * 4 + (2 * t + x + 1))
                    pe.wait_ge(s_qke, w)
                    for q in range(4):
                        m = (4 * i + q) * 2
                        ins = T_.transpose(pK[:, q], stack[:, x, m:m + 2].rearrange("p m r d -> p (m r d)"), cst("ident"))
                    ins.then_inc(s_qkb, 1)

                def scores(c, n, k, par):
                    u, h = divmod(k, HEADS)
                    hh, hp = h % 2, h // 2
                    pe.wait_ge(s_exp, n + 1)
                    if k == 0:
                        pe.wait_ge(s_qke, c * 16 + 16)
                    T_.matmul(pS[:, hh], identb[:], bc(maskb[:, u], 1, 2), start=True, stop=False, skip_group_check=True)
                    for s in range(2):
                        rows = slice(64 * hh, 64 * hh + 64)
                        ins = T_.matmul(pS[:, hh, s], qk[par][rows, 0, s * 8 + hp, u * P:(u + 1) * P],
                                        qk[par][rows, 1, s * 8 + hp, :], start=False, stop=True, skip_group_check=True)
                    ins.then_inc(s_scores, 1)

                def turn_mixed(n, k):
                    pe.wait_ge(s_d, n + 3)
                    pe.wait_ge(s_dt, n + 1)
                    for kt in range(2):
                        ins = T_.transpose(pT[:, k % 2, kt], D[:, k % 2, kt * P:(kt + 1) * P], cst("ident"))
                    ins.then_inc(s_t, 1)

                def values(c, n, k, par):
                    u, h = divmod(k, HEADS)
                    pe.wait_ge(s_dt, n + 3)
                    if k == 0:
                        pe.wait_ge(s_v, c * 2 + 2)
                    if h == 0:
                        pe.wait_ge(s_y, c * 2 + u)
                    for kt in range(2):
                        ins = T_.matmul(pO[:, h * HD:(h + 1) * HD], DT[:, k % 2, kt], Vb[:, par, kt, h * HD:(h + 1) * HD],
                                        start=(kt == 0), stop=(kt == 1))
                    ins.then_inc(s_pv, 1)

                def batch(c, par, more):
                    for k in range(UN + 3):
                        n = c * UN + k
                        if k < UN:
                            scores(c, n, k, par)
                        if 2 <= k < UN + 2:
                            turn_mixed(n - 2, k - 2)
                        if k >= 3:
                            values(c, n - 3, k - 3, par)
                        if more:
                            for piece in PE_PIECES.get(k, ()):
                                (project if piece[0] == "project" else turn)(c + 1, *piece[1:])

                for t in range(2):
                    for x in range(3):
                        project(0, t, x)
                    for x in range(2):
                        for i in range(4):
                            turn(0, t, x, i)
                with T_.Fori(0, BATCH // 2 - 1) as i:
                    batch(i * 2, 0, True)
                    batch(i * 2 + 1, 1, True)
                batch(BATCH - 2, 0, True)
                batch(BATCH - 1, 1, False)


PE_PIECES, DVE_PIECES, ACT_PIECES = {}, {}, {}
for _t, _at in ((0, 1), (1, 9)):
    for _x in range(3):
        PE_PIECES.setdefault(_at + 2 * _x, []).append(("project", _t, _x))
    for _x in range(2):
        DVE_PIECES.setdefault(_at + 2 * _x + 1, []).append(("rope", _t, _x))
        ACT_PIECES.setdefault(_at + 2 * _x + 3, []).append(("high", _t, _x))
    ACT_PIECES.setdefault(_at + 6, []).append(("values", _t))
ACT_PIECES.setdefault(0, []).append(("take",))
for _t, _at in ((0, 7), (1, 19)):
    for _x in range(2):
        for _i in range(4):
            PE_PIECES.setdefault(_at + 4 * _x + _i, []).append(("turn", _t, _x, _i))
            DVE_PIECES.setdefault(_at + 4 * _x + _i, []).append(("evac", _t, _x, _i))



EXPERTS, TOPK, INTER = 64, 8, 128
EPS = 1e-5
UP, GATE, GATE1 = 64, 192, 320
JOINT = 321


def mix_phase(nc, hT, y, keep, d, consts):
    with ExitStack() as ctx:
        sb = lambda n, s, dt=F32: ctx.enter_context(nc.sbuf_tensor("c_" + n, s, dt))
        sem = lambda n: ctx.enter_context(nc.semaphore("c_" + n))
        pb = lambda n, s: ctx.enter_context(nc.psum_tensor("c_" + n, s, F32))
        cst = lambda n: consts[:, CONST[n][0]:CONST[n][0] + CONST[n][1]]
        Wo = sb("Wo", [P, FCH, LEN])
        Wj = sb("Wj", [P, FCH, JOINT])
        Wd = sb("Wd", [P, LEN])
        gb = sb("gb", [P, 2, 2, 2])
        hs = sb("hs", [P, FCH, P])
        z = sb("z", [P, 2, LEN // 2])
        zT = sb("zT", [P, FCH, P])
        h1 = sb("h1", [P, 2, LEN])
        h1T = sb("h1T", [P, FCH, P])
        bn = sb("bn", [P, 6])
        mark = sb("mark", [P, 1])
        sta = sb("sta", [P, 16])
        stb = sb("stb", [P, 6])
        ab = sb("ab", [P, 2, 2])
        top, topi, topf = sb("top", [P, TOPK]), sb("topi", [P, TOPK], U32), sb("topf", [P, TOPK])
        negtop, wsum = sb("negtop", [P, 1]), sb("wsum", [P, 2])
        onehot, picked = sb("onehot", [P, TOPK, EXPERTS]), sb("picked", [P, TOPK, EXPERTS])
        chosen = sb("chosen", [P, EXPERTS], BF16)
        R = sb("R", [P, EXPERTS])
        posf, pos = sb("posf", [P, TOPK]), sb("pos", [P, 2, TOPK], I32)
        tok = sb("tok", [P, TILES], I32)
        tokc = sb("tokc", [P, 2, 1], I32)
        ex, rc, inter = sb("ex", [P, INTER + 1]), sb("rc", [P, INTER + 1]), sb("inter", [P, INTER])
        interT = sb("interT", [P, INTER])
        beforeb, onesb = sb("beforeb", [P, P], BF16), sb("onesb", [P, P], BF16)
        zero = sb("zero", [P, EXPERTS * TOK // P], I32)
        pG, pZ, pA, pX = pb("pG", [P, 2, 256]), pb("pZ", [P, LEN]), pb("pA", [P, LEN]), pb("pX", [P, LEN])
        pR, pC, pI, pD = pb("pR", [P, LEN]), pb("pC", [P, LEN]), pb("pI", [P, LEN]), pb("pD", [P, LEN])
        rw, ranks, experts, carry = keep["rw"], keep["ranks"], keep["experts"], keep["counts"]

        loaded, setup = sem("loaded"), sem("setup")
        listed0 = sem("list_zero")
        sA, sB = sem("dve_a"), sem("dve_b")
        group, s_hs, zt, zte, joined = sem("group"), sem("hs"), sem("zt"), sem("zt_evac"), sem("wo")
        h1t, h1te, joint, s_ex, s_w8 = sem("h1t"), sem("h1t_evac"), sem("joint"), sem("ex"), sem("w8")
        rank, it, ite, down = sem("rank"), sem("it"), sem("it_evac"), sem("down")
        h1_ready, h1_out, posr = sem("h1_ready"), [sem("h1_out0"), sem("h1_out1")], sem("pos_ready")
        listed = [sem("listed0"), sem("listed1")]
        zeroed, passed, passed_p, roots = sem("zeroed"), sem("passed"), sem("passed_pool"), sem("roots")
        LOADS = 16 * 7
        PA, PB = 13, 17

        with nc.Block() as block:
            @block.sync
            def _(sp):
                sp.dma_start(Wo[:], d["wo"].rearrange("(j p) n -> p j n", p=P)).then_inc(loaded, 16)
                sp.dma_start(Wj[:], d["w_joint"].rearrange("(j p) n -> p j n", p=P)).then_inc(loaded, 16)
                sp.dma_start(Wd[:], d["sh_down"]).then_inc(loaded, 16)
                for i, n in enumerate(("gamma", "beta")):
                    for u in range(2):
                        sp.dma_start(gb[:, i, u], d[n].rearrange("(u p a) -> u p a", p=P, a=2)[u]).then_inc(loaded, 16)
                sp.wait_ge(zeroed, 1)
                sp.dma_start(d["lists"].rearrange("(p n) a -> p (n a)", p=P), zero[:]).then_inc(listed0, 16)
                sp.wait_ge(listed0, 16)
                with nc.sync.Fori(0, TILES // 2) as i:
                    for par in range(2):
                        n = i * 2 + par
                        sp.wait_ge(h1_ready, n + 1)
                        sp.dma_start(d["h1"].rearrange("(t p) n -> p t n", p=P)[:, bass.ds(n, 1)], h1[:, par:par + 1]).then_inc(h1_out[par], 16)
                for par in range(2):
                    sp.wait_ge(h1_out[par], 16 * TILES // 2)

            @block.gpsimd
            def _(pool):
                nc.gpsimd.memset(zero[:], 0).then_inc(zeroed, 1)
                pool.wait_ge(listed0, 16)
                def root(n, which):
                    pool.wait_ge(sA, n * PA + (6 if which == 0 else 12))
                    src, dst = ((5, 12), (9, 13))[which]
                    nc.gpsimd.tensor_tensor(sta[:, dst:dst + 1], sta[:, src:src + 1], cst("eps"), ALU.add).then_inc(roots, 1)
                    pool.wait_ge(roots, n * 4 + (2 * which + 1))
                    nc.gpsimd.tensor_tensor(sta[:, dst:dst + 1], sta[:, dst:dst + 1], cst("minus_half"), ALU.pow).then_inc(roots, 1)

                def both(n, par, more):
                    if more:
                        root(n + 1, 0)
                        root(n + 1, 1)
                    pool.wait_ge(posr, n + 1)
                    pool.sem_inc(passed_p, 1)
                    for k in range(TOPK):
                        nc.gpsimd.indirect_dma_start(
                            d["lists"], bass.IndirectOffsetOnAxis(ap=pos[:, par, k:k + 1], axis=0),
                            tokc[:, par], None).then_inc(listed[par], 16)

                root(0, 0)
                root(0, 1)
                with nc.gpsimd.Fori(0, TILES // 2 - 1) as i:
                    both(i * 2, 0, True)
                    both(i * 2 + 1, 1, True)
                both(TILES - 2, 0, True)
                both(TILES - 1, 1, False)
                for par in range(2):
                    pool.wait_ge(listed[par], 16 * TOPK * TILES // 2)

            @block.vector
            def _(dve):
                V_ = nc.vector
                V_.tensor_copy(beforeb[:], cst("before")).then_inc(setup, 1)
                V_.tensor_copy(onesb[:], cst("ones")).then_inc(setup, 1)
                V_.memset(carry, 0.0).then_inc(setup, 1)
                V_.memset(ranks[:, TILES * TOPK:], 0.0)
                V_.memset(experts[:, TILES * TOPK:], 0.0)
                for t in range(TILES):
                    V_.tensor_scalar(tok[:, t:t + 1], cst("lane"), float(P * t), None, ALU.add).then_inc(setup, 1)
                dve.wait_ge(setup, 3 + TILES)
                dve.wait_ge(loaded, LOADS)
                a, b = Steps(sA), Steps(sB)

                def do(st, ins, wait=True, alone=False):
                    st.inc(ins)
                    if wait:
                        st.wait(dve)
                    if alone:
                        dve.sem_inc(passed, 1)

                def first(n, par):
                    a.start, a.n = n * PA, 0
                    yt = y[:, bass.ds(n, 1)].rearrange("p o n -> p (o n)")
                    do(a, V_.bn_stats(bn[:], yt), alone=True)
                    do(a, V_.bn_aggr(sta[:, 0:2], bn[:]))
                    yield
                    dve.wait_ge(group, n * 2 + 1)
                    do(a, V_.tensor_copy(sta[:, 2:3], pG[:, 0, 0:1]))
                    do(a, V_.tensor_tensor(sta[:, 3:4], sta[:, 0:1], sta[:, 2:3], ALU.subtract))
                    do(a, V_.scalar_tensor_tensor(sta[:, 4:5], sta[:, 3:4], sta[:, 3:4], sta[:, 1:2], ALU.mult, ALU.add))
                    yield
                    dve.wait_ge(group, n * 2 + 2)
                    do(a, V_.tensor_copy(sta[:, 5:6], pG[:, 0, 1:2]), False)
                    dve.wait_ge(roots, n * 4 + 2)
                    do(a, V_.tensor_scalar(ab[:, 0], gb[:, 0, par], sta[:, 12:13], 1.0 - INIT_LAMBDA, ALU.mult, ALU.mult))
                    do(a, V_.tensor_scalar(sta[:, 6:8], ab[:, 0], sta[:, 2:3], None, ALU.mult))
                    do(a, V_.scalar_tensor_tensor(ab[:, 1], gb[:, 1, par], 1.0 - INIT_LAMBDA, sta[:, 6:8], ALU.mult, ALU.subtract))
                    dve.wait_ge(zt, n)
                    for f in range(2):
                        ins = V_.tensor_scalar(z[:, f], yt[:, f * 256:(f + 1) * 256], ab[:, 0, f:f + 1], ab[:, 1, f:f + 1], ALU.mult, ALU.add)
                    do(a, ins)
                    yield
                    dve.wait_ge(joined, n + 1)
                    do(a, V_.bn_stats(bn[:], pA[:]), alone=True)
                    do(a, V_.bn_aggr(sta[:, 8:10], bn[:]), False)
                    dve.wait_ge(roots, n * 4 + 4)
                    if LATE[0]:
                        dve.wait_ge(h1_out[par], (n - par) * 8)
                    do(a, V_.tensor_scalar(h1[:, par], pA[:], sta[:, 8:9], sta[:, 13:14], ALU.subtract, ALU.mult), False)
                    assert a.n == PA
                    V_.tensor_copy(mark[:], cst("lane")).then_inc(h1_ready, 1)
                    yield

                def second(n, par):
                    b.start, b.n = n * PB, 0
                    dve.wait_ge(joint, n + 1)
                    dve.sem_inc(passed, 1)
                    logits = pR[:, 0:EXPERTS]
                    do(b, V_.max(top[:], logits), alone=True)
                    do(b, V_.max_index(topi[:], top[:], logits), False)
                    do(b, V_.tensor_scalar(negtop[:], top[:, 0:1], -1.0, None, ALU.mult))
                    do(b, V_.tensor_copy(topf[:], topi[:]))
                    do(b, V_.tensor_tensor(onehot[:], bc(cst("experts"), 1, TOPK), bc(topf[:], 2, EXPERTS), ALU.is_equal))
                    with nc.allow_low_precision(reason="zeros and ones"):
                        do(b, V_.tensor_reduce(chosen[:], onehot[:].rearrange("p k e -> p e k"), AX.X, ALU.add))
                    yield
                    dve.wait_ge(s_ex, n + 1)
                    do(b, V_.tensor_scalar(rc[:], ex[:], 1.0, None, ALU.add))
                    do(b, V_.reciprocal(rc[:], rc[:]))
                    dve.wait_ge(it, n)
                    do(b, V_.tensor_tensor(inter[:], rc[:, 0:INTER], pR[:, GATE:GATE1], ALU.mult))
                    do(b, V_.tensor_tensor(inter[:], inter[:], pR[:, UP:GATE], ALU.mult))
                    yield
                    dve.wait_ge(rank, n + 1)
                    do(b, V_.tensor_tensor(R[:], pC[:, 0:EXPERTS], carry, ALU.add))
                    do(b, V_.tensor_tensor(carry, pC[:, EXPERTS:2 * EXPERTS], carry, ALU.add), False)
                    do(b, V_.tensor_tensor(picked[:], onehot[:], bc(R[:], 1, TOPK), ALU.mult))
                    kept = lambda x: x[:, bass.ds(n * TOPK, TOPK)]
                    do(b, V_.tensor_reduce(posf[:], picked[:], AX.X, ALU.add))
                    V_.tensor_copy(kept(ranks), posf[:])
                    V_.tensor_copy(kept(experts), topf[:])
                    dve.wait_ge(listed[par], (n - par) * 8 * TOPK) if LATE[0] else None
                    V_.tensor_copy(tokc[:, par], tok[:, bass.ds(n, 1)])
                    do(b, V_.scalar_tensor_tensor(pos[:, par], topf[:], float(TOK), posf[:], ALU.mult, ALU.add))
                    V_.tensor_copy(mark[:], cst("lane")).then_inc(posr, 1)
                    dve.wait_ge(s_w8, n + 1)
                    do(b, V_.reciprocal(wsum[:, 1:2], wsum[:, 0:1]))
                    V_.tensor_scalar(kept(rw), kept(rw), wsum[:, 1:2], None, ALU.mult)
                    yield
                    dve.wait_ge(down, n + 1)
                    do(b, V_.scalar_tensor_tensor(y[:, bass.ds(n, 1)].rearrange("p o n -> p (o n)"), pD[:], rc[:, INTER:INTER + 1], h1[:, par],
                                                  ALU.mult, ALU.add))
                    assert b.n == PB, b.n
                    yield

                LATE = [False]

                def both(n, par, more):
                    f = first(n + 1, 1 - par) if more else iter([None] * 4)
                    s = second(n, par)
                    next(f)
                    next(s)
                    next(f)
                    next(s)
                    next(f)
                    next(s)
                    next(s)
                    next(f)

                for _ in first(0, 0):
                    pass
                both(0, 0, True)
                LATE[0] = True
                both(1, 1, True)
                with V_.Fori(1, TILES // 2 - 1) as i:
                    both(i * 2, 0, True)
                    both(i * 2 + 1, 1, True)
                both(TILES - 2, 0, True)
                both(TILES - 1, 1, False)

            @block.scalar
            def _(act):
                A_ = nc.scalar
                kept = lambda x, n: x[:, bass.ds(n * TOPK, TOPK)]

                def residual(n):
                    act.wait_ge(joined, n)
                    A_.activation(hs[:], hT[:, :, bass.ds(n * P, P)], ACT.Copy).then_inc(s_hs, 1)

                def z_evac(n):
                    act.wait_ge(zt, n + 1)
                    A_.activation(zT[:].rearrange("p j n -> p (j n)"), pZ[:], ACT.Copy).then_inc(zte, 1)

                def second_a(n):
                    act.wait_ge(h1t, n + 1)
                    A_.activation(h1T[:].rearrange("p j n -> p (j n)"), pX[:], ACT.Copy).then_inc(h1te, 1)

                def second_b(n):
                    act.wait_ge(joint, n + 1)
                    act.wait_ge(sB, n * PB + 6)
                    A_.activation(ex[:], pR[:, GATE:JOINT], ACT.Exp, scale=-1.0).then_inc(s_ex, 1)
                    A_.activation(kept(rw, n), top[:], ACT.Exp, bias=negtop[:], accum_out=wsum[:, 0:1]).then_inc(s_w8, 1)

                def second_c(n):
                    act.wait_ge(it, n + 1)
                    A_.activation(interT[:], pI[:, 0:P], ACT.Copy).then_inc(ite, 1)

                def both(n, more):
                    second_a(n)
                    if more:
                        residual(n + 1)
                    second_b(n)
                    second_c(n)
                    if more:
                        z_evac(n + 1)

                residual(0)
                z_evac(0)
                with A_.Fori(0, TILES - 1) as i:
                    both(i, True)
                both(TILES - 1, False)

            @block.tensor
            def _(pe):
                T_ = nc.tensor
                pe.wait_ge(setup, 3 + TILES)
                pe.wait_ge(loaded, LOADS)
                ident = cst("ident")

                def means(n, which):
                    pe.wait_ge(sA, n * PA + (2 if which == 0 else 5))
                    src = sta[:, 0:1] if which == 0 else sta[:, 4:5]
                    T_.matmul(pG[:, 0, which:which + 1], cst("group"), src, start=True, stop=True).then_inc(group, 1)

                def z_turn(n):
                    pe.wait_ge(sA, n * PA + 10)
                    pe.wait_ge(zte, n)
                    for j in range(FCH):
                        ins = T_.transpose(pZ[:, j * P:(j + 1) * P], z[:].rearrange("p a n -> p (a n)")[:, j * P:(j + 1) * P], ident)
                    ins.then_inc(zt, 1)

                def project(n):
                    pe.wait_ge(zte, n + 1)
                    pe.wait_ge(s_hs, n + 1)
                    pe.wait_ge(sA, n * PA)
                    for j in range(FCH):
                        T_.matmul(pA[:], zT[:, j], Wo[:, j], start=(j == 0), stop=False, skip_group_check=True)
                    for j in range(FCH):
                        ins = T_.matmul(pA[:, j * P:(j + 1) * P], hs[:, j], ident, start=False, stop=True, skip_group_check=True)
                    ins.then_inc(joined, 1)

                def h1_turn(n, par):
                    pe.wait_ge(h1_ready, n + 1)
                    pe.wait_ge(h1te, n)
                    for j in range(FCH):
                        ins = T_.transpose(pX[:, j * P:(j + 1) * P], h1[:, par, j * P:(j + 1) * P], ident)
                    ins.then_inc(h1t, 1)

                def joint_product(n):
                    pe.wait_ge(h1te, n + 1)
                    pe.wait_ge(sB, n * PB)
                    for j in range(FCH):
                        ins = T_.matmul(pR[:, 0:JOINT], h1T[:, j], Wj[:, j], start=(j == 0), stop=(j == FCH - 1))
                    ins.then_inc(joint, 1)

                def count(n):
                    pe.wait_ge(sB, n * PB + 6)
                    T_.matmul(pC[:, 0:EXPERTS], beforeb[:], chosen[:], start=True, stop=True)
                    T_.matmul(pC[:, EXPERTS:2 * EXPERTS], onesb[:], chosen[:], start=True, stop=True).then_inc(rank, 1)

                def shared(n):
                    pe.wait_ge(sB, n * PB + 10)
                    pe.wait_ge(ite, n)
                    T_.transpose(pI[:, 0:P], inter[:], ident).then_inc(it, 1)

                def shared_down(n):
                    pe.wait_ge(ite, n + 1)
                    T_.matmul(pD[:], interT[:], Wd[:], start=True, stop=True).then_inc(down, 1)

                def both(n, par, more):
                    h1_turn(n, par)
                    joint_product(n)
                    if more:
                        means(n + 1, 0)
                    count(n)
                    if more:
                        means(n + 1, 1)
                    shared(n)
                    if more:
                        z_turn(n + 1)
                    shared_down(n)
                    if more:
                        project(n + 1)

                means(0, 0)
                means(0, 1)
                z_turn(0)
                project(0)
                with T_.Fori(0, TILES // 2 - 1) as i:
                    both(i * 2, 0, True)
                    both(i * 2 + 1, 1, True)
                both(TILES - 2, 0, True)
                both(TILES - 1, 1, False)


def keeps(nc, ctx):
    sb = lambda n, s, dt=F32: ctx.enter_context(nc.sbuf_tensor("k_" + n, s, dt))
    return dict(rw=sb("rw", [P, TILES * TOPK])[:], ranks=sb("ranks", [P, 144])[:],
                experts=sb("experts", [P, 144])[:], slots=sb("slots", [P, 144])[:], counts=sb("counts", [P, EXPERTS])[:])



MAX_TILES = TOK * TOPK // P + EXPERTS
RING = 4
PAIRS = 144
WCOLS = FCH * 2 * INTER + LEN


def expert_phase(nc, keep, d, consts):
    NT = MAX_TILES
    with ExitStack() as ctx:
        sb = lambda n, s, dt=F32: ctx.enter_context(nc.sbuf_tensor("d_" + n, s, dt))
        sem = lambda n: ctx.enter_context(nc.semaphore("d_" + n))
        pb = lambda n, s: ctx.enter_context(nc.psum_tensor("d_" + n, s, F32))
        cst = lambda n: consts[:, CONST[n][0]:CONST[n][0] + CONST[n][1]]
        ident = cst("ident")
        more_than = sb("more_than", [P, EXPERTS, 16])
        nt, cum, first = sb("nt", [P, EXPERTS]), sb("cum", [P, 2, EXPERTS]), sb("first", [P, EXPERTS])
        behind = sb("behind", [P, 2, EXPERTS])
        et, bt, tt, rowf, rowi = (sb(n, [P, 2]) for n in ("et", "bt", "tt", "rowf", "rowi_f"))
        rowi = sb("rowi", [P, 2], I32)
        rows = sb("rows", [P, 2, P], I32)
        rowsf = sb("rowsf", [P, 2, P])
        idx = sb("idx", [P, 2 * P], I32)
        idxc = sb("idxc", [P, 2, RING], I32)
        erow = sb("erow", [1, 2 * P])
        turn = sb("turn", [1, 2, 2 * P])
        tab = sb("tab", [1, 3, 2 * P], I32)
        W = sb("W", [P, RING, WCOLS])
        X = sb("X", [P, RING, LEN])
        XT = sb("XT", [P, 2, LEN])
        ex, inter = sb("ex", [P, INTER]), sb("inter", [P, 2, INTER])
        interT = sb("interT", [P, 2, INTER])
        Y = sb("Y", [P, RING, LEN])
        oneh = sb("oneh", [P, 3, EXPERTS])
        base3 = sb("base3", [P, 3])
        pX, pG, pY = pb("pX", [P, 2, LEN]), pb("pG", [P, 2, LEN]), pb("pY", [P, 2, LEN])
        pI = pb("pI", [P, LEN])
        st_s = sem("setup")
        listg, turned, tabbed, ready = sem("list_rows"), sem("rows_turned"), sem("erow"), sem("tables")
        wl = [sem(f"weights{u}") for u in range(RING)]
        xl = [sem(f"gathered{u}") for u in range(RING)]
        yl = [sem(f"stored{u}") for u in range(RING)]
        xt, xte, gu, s_ex, s_r, s_in = sem("xt"), sem("xt_evac"), sem("gate_up"), sem("ex"), sem("rc"), sem("inter")
        it, ite, dn, yr = sem("it"), sem("it_evac"), sem("down"), sem("y_ready")
        idxs, passed, s_pos = sem("idx_copied"), sem("passed"), sem("positions")
        LOOPS = NT // RING

        with nc.Block() as block:
            @block.vector
            def _(dve):
                V_ = nc.vector
                st = Steps(st_s)

                def do(ins, wait=True):
                    st.inc(ins)
                    if wait:
                        st.wait(dve)
                do(V_.tensor_tensor(more_than[:], bc(keep["counts"], 2, 16), bc(cst("tiles128"), 1, EXPERTS), ALU.is_gt))
                do(V_.tensor_reduce(nt[:], more_than[:], AX.X, ALU.add))
                do(V_.tensor_copy(cum[:, 0], nt[:]))
                a, s = 0, 1
                while s < EXPERTS:
                    do(V_.tensor_copy(cum[:, 1 - a, 0:s], cum[:, a, 0:s]), False)
                    do(V_.tensor_tensor(cum[:, 1 - a, s:], cum[:, a, s:], cum[:, a, 0:EXPERTS - s], ALU.add))
                    a, s = 1 - a, 2 * s
                incl = cum[:, a]
                do(V_.tensor_tensor(first[:], incl, nt[:], ALU.subtract))
                do(V_.tensor_scalar(first[:], first[:], float(P), None, ALU.mult))
                for g in range(2):
                    do(V_.tensor_scalar(tt[:, g:g + 1], cst("lane"), float(P * g), None, ALU.add))
                    do(V_.tensor_scalar(behind[:, g], incl, tt[:, g:g + 1], None, ALU.is_le))
                    do(V_.tensor_reduce(et[:, g:g + 1], behind[:, g], AX.X, ALU.add), False)
                    do(V_.tensor_tensor(behind[:, g], behind[:, g], nt[:], ALU.mult))
                    do(V_.tensor_reduce(bt[:, g:g + 1], behind[:, g], AX.X, ALU.add))
                do(V_.tensor_scalar(et[:], et[:], float(EXPERTS - 1), None, ALU.min))
                do(V_.tensor_tensor(tt[:], tt[:], bt[:], ALU.subtract))
                do(V_.scalar_tensor_tensor(rowf[:], et[:], 16.0, tt[:], ALU.mult, ALU.add))
                do(V_.tensor_scalar(rowi[:], rowf[:], float(EXPERTS * 16 - 1), None, ALU.min))
                assert st.n == ROWS, st.n
                for g in range(2):
                    dve.wait_ge(listg, 16 * (g + 1))
                    do(V_.tensor_copy(rowsf[:, g], rows[:, g]))
                assert st.n == ROWS + 2
                dve.wait_ge(turned, 2)
                do(V_.tensor_copy(idx[:], pX[:, 0, 0:2 * P]))
                do(V_.tensor_copy(erow[:], pG[0:1, 0, 0:2 * P]))
                do(V_.memset(turn[:, 0, 0:1], 1.0), False)
                do(V_.tensor_tensor(turn[:, 0, 1:], erow[:, 1:], erow[:, 0:2 * P - 1], ALU.not_equal))
                do(V_.tensor_copy(tab[:, 1], turn[:, 0]), False)
                do(V_.tensor_copy(tab[:, 0], erow[:]))
                a, s = 0, 1
                while s < 2 * P:
                    do(V_.tensor_copy(turn[:, 1 - a, 0:s], turn[:, a, 0:s]), False)
                    do(V_.tensor_tensor(turn[:, 1 - a, s:], turn[:, a, s:], turn[:, a, 0:2 * P - s], ALU.add))
                    a, s = 1 - a, 2 * s
                do(V_.tensor_scalar(turn[:, 1 - a], turn[:, a], 1.0 / RING, -0.375, ALU.mult, ALU.add))
                do(V_.tensor_scalar(turn[:, 1 - a], turn[:, 1 - a], ROUND, ROUND, ALU.add, ALU.subtract))
                do(V_.scalar_tensor_tensor(tab[:, 2], turn[:, 1 - a], -float(RING), turn[:, a], ALU.mult, ALU.add))
                V_.tensor_copy(tt[:, 0:1], tt[:, 1:2]).then_inc(ready, 1)

                def silu(t, u):
                    w = u % 2
                    dve.wait_ge(s_ex, t + 1)
                    if not (isinstance(t, int) and t < 2):
                        dve.wait_ge(it, t - 1)
                    V_.tensor_scalar(inter[:, w], ex[:], 1.0, None, ALU.add).then_inc(s_r, 1)
                    dve.wait_ge(s_r, t * 3 + 1)
                    V_.reciprocal(inter[:, w], inter[:, w]).then_inc(s_r, 1)
                    dve.wait_ge(s_r, t * 3 + 2)
                    V_.tensor_tensor(inter[:, w], inter[:, w], pG[:, w, 0:INTER], ALU.mult).then_inc(s_r, 1)
                    dve.wait_ge(s_r, t * 3 + 3)
                    V_.tensor_tensor(inter[:, w], inter[:, w], pG[:, w, INTER:2 * INTER], ALU.mult).then_inc(s_in, 1)

                def out(t, u, late=True):
                    dve.wait_ge(dn, t + (1 + RING))
                    if late:
                        dve.wait_ge(yl[u], (t - u) * 4)
                    V_.tensor_copy(Y[:, u], pY[:, u % 2]).then_inc(yr, 1)

                def place(i):
                    pairs = bass.ds(i * 3, 3)
                    V_.tensor_tensor(oneh[:], bc(cst("experts"), 1, 3), bc(keep["experts"][:, pairs], 2, EXPERTS), ALU.is_equal).then_inc(s_pos, 1)
                    dve.wait_ge(s_pos, i * 4 + 1)
                    V_.tensor_tensor(oneh[:], oneh[:], bc(first[:], 1, 3), ALU.mult).then_inc(s_pos, 1)
                    dve.wait_ge(s_pos, i * 4 + 2)
                    V_.tensor_reduce(base3[:], oneh[:], AX.X, ALU.add).then_inc(s_pos, 1)
                    dve.wait_ge(s_pos, i * 4 + 3)
                    V_.tensor_tensor(keep["slots"][:, pairs], keep["ranks"][:, pairs], base3[:], ALU.add).then_inc(s_pos, 1)

                def four(i, head=False):
                    for u in range(RING):
                        t = i * RING + u
                        silu(t, u)
                        if not (head and u < 2):
                            out(t - 2, (u - 2) % RING, late=not head)
                    place(i)

                four(0, True)
                with V_.Fori(1, LOOPS) as i:
                    four(i)
                for t in (NT - 2, NT - 1):
                    out(t, t % RING)

            @block.gpsimd
            def _(pool):
                G_ = nc.gpsimd
                pool.wait_ge(st_s, ROWS)
                rows_view = d["lists"].rearrange("(r n) a -> r (n a)", n=P)
                for g in range(2):
                    G_.indirect_dma_start(rows[:, g], None, rows_view,
                                          bass.IndirectOffsetOnAxis(ap=rowi[:, g:g + 1], axis=0)).then_inc(listg, 16)
                    pool.wait_ge(listg, 16 * (g + 1))
                pool.wait_ge(ready, 1)

                def four(i, par, head=False):
                    G_.tensor_copy(idxc[:, par], idx[:, bass.ds(i * RING, RING)]).then_inc(idxs, 1)
                    pool.wait_ge(idxs, i + 1)
                    pool.sem_inc(passed, 1)
                    for u in range(RING):
                        t = i * RING + u
                        if not head:
                            pool.wait_ge(xt, t - (RING - 1))
                            pool.sem_inc(passed, 1)
                        G_.indirect_dma_start(X[:, u], None, d["h1"],
                                              bass.IndirectOffsetOnAxis(ap=idxc[:, par, u:u + 1], axis=0)).then_inc(xl[u], 16)

                four(0, 0, True)
                four(1, 1)
                with G_.Fori(1, LOOPS // 2) as i:
                    four(i * 2, 0)
                    four(i * 2 + 1, 1)

            @block.sync
            def _(sp):
                sp.wait_ge(ready, 1)
                yv = d["slots"].rearrange("(t p) n -> p t n", p=P)

                def four(i, head=False):
                    for u in range(RING):
                        t = i * RING + u
                        e = sp.value_load(tab[0:1, 0, bass.ds(t, 1)], min_val=0, max_val=EXPERTS - 1)
                        new = sp.value_load(tab[0:1, 1, bass.ds(t, 1)], min_val=0, max_val=1)
                        at = sp.value_load(tab[0:1, 2, bass.ds(t, 1)], min_val=0, max_val=RING - 1)
                        if not head:
                            sp.wait_ge(dn, t + 1)
                        sp.dma_start(W[:, bass.ds(at, 1)].rearrange("p o n -> p (o n)"),
                                     d["w_experts"][bass.ds(e, 1)].rearrange("o p n -> p (o n)"), cond=new).then_inc(wl[u], 16)
                        if not head:
                            store(t - RING, u)

                def store(t, u):
                    sp.wait_ge(yr, t + 1)
                    sp.dma_start(yv[:, bass.ds(t, 1)].rearrange("p o n -> p (o n)"), Y[:, u]).then_inc(yl[u], 16)

                four(0, True)
                with nc.sync.Fori(1, LOOPS) as i:
                    four(i)
                for t in range(NT - RING, NT):
                    store(t, t % RING)
                for u in range(RING):
                    sp.wait_ge(yl[u], 16 * LOOPS)

            @block.scalar
            def _(act):
                A_ = nc.scalar

                def x_evac(t, u):
                    act.wait_ge(xt, t + 1)
                    A_.activation(XT[:, u % 2], pX[:, u % 2], ACT.Copy).then_inc(xte, 1)

                def exps(t, u):
                    act.wait_ge(gu, t + 1)
                    act.wait_ge(s_in, t)
                    A_.activation(ex[:], pG[:, u % 2, 0:INTER], ACT.Exp, scale=-1.0).then_inc(s_ex, 1)

                def i_evac(t, u):
                    act.wait_ge(it, t + 1)
                    A_.activation(interT[:, u % 2], pI[:, 0:P], ACT.Copy).then_inc(ite, 1)

                def four(i, head=False, tail=False):
                    for u in range(RING):
                        t = i * RING + u
                        if not (tail and u == RING - 1):
                            x_evac(t + 1, (u + 1) % RING)
                        exps(t, u)
                        if not (head and u == 0):
                            i_evac(t - 1, (u - 1) % RING)

                x_evac(0, 0)
                four(0, head=True)
                with A_.Fori(1, LOOPS - 1) as i:
                    four(i)
                four(LOOPS - 1, tail=True)
                i_evac(NT - 1, RING - 1)

            @block.tensor
            def _(pe):
                T_ = nc.tensor
                for g in range(2):
                    pe.wait_ge(st_s, ROWS + 1 + g)
                    T_.transpose(pX[:, 0, g * P:(g + 1) * P], rowsf[:, g], ident)
                    T_.matmul(pG[0:1, 0, g * P:(g + 1) * P], et[:, g:g + 1], ident, start=True, stop=True).then_inc(turned, 1)
                pe.wait_ge(ready, 1)
                pe.sem_inc(dn, RING)

                def x_turn(t, u):
                    pe.wait_ge(xl[u], ((t - u) * 4 + 16))
                    if not (isinstance(t, int) and t < 2):
                        pe.wait_ge(xte, t - 1)
                    for j in range(FCH):
                        ins = T_.transpose(pX[:, u % 2, j * P:(j + 1) * P], X[:, u, j * P:(j + 1) * P], ident)
                    ins.then_inc(xt, 1)

                def gate_up(t, u, at):
                    pe.wait_ge(xte, t + 1)
                    pe.wait_ge(wl[u], (t - u) * 4 + 16)
                    if not (isinstance(t, int) and t < 2):
                        pe.wait_ge(s_in, t - 1)
                    for j in range(FCH):
                        ins = T_.matmul(pG[:, u % 2, 0:2 * INTER], XT[:, u % 2, j * P:(j + 1) * P],
                                        W[:, bass.ds(at, 1), j * 2 * INTER:(j + 1) * 2 * INTER].rearrange("p o n -> p (o n)"),
                                        start=(j == 0), stop=(j == FCH - 1))
                    ins.then_inc(gu, 1)

                def i_turn(t, u):
                    pe.wait_ge(s_in, t + 1)
                    pe.wait_ge(ite, t)
                    T_.transpose(pI[:, 0:P], inter[:, u % 2], ident).then_inc(it, 1)

                def down(t, u, at):
                    pe.wait_ge(ite, t + 1)
                    if not (isinstance(t, int) and t < 2):
                        pe.wait_ge(yr, t - 1)
                    T_.matmul(pY[:, u % 2], interT[:, u % 2],
                              W[:, bass.ds(at, 1), FCH * 2 * INTER:WCOLS].rearrange("p o n -> p (o n)"), start=True, stop=True).then_inc(dn, 1)

                def place(t):
                    return pe.value_load(tab[0:1, 2, bass.ds(t, 1)], min_val=0, max_val=RING - 1)

                def four(i, head=False, tail=False):
                    for u in range(RING):
                        t = i * RING + u
                        if not (tail and u == RING - 1):
                            x_turn(t + 1, (u + 1) % RING)
                        gate_up(t, u, place(t))
                        if not (head and u < 2):
                            down(t - 2, (u - 2) % RING, place(t - 2))
                        if not (head and u == 0):
                            i_turn(t - 1, (u - 1) % RING)

                x_turn(0, 0)
                four(0, head=True)
                with T_.Fori(1, LOOPS - 1) as i:
                    four(i)
                four(LOOPS - 1, tail=True)
                down(NT - 2, RING - 2, place(NT - 2))
                i_turn(NT - 1, RING - 1)
                down(NT - 1, RING - 1, place(NT - 1))


ROWS = 3 + 12 + 2 + 10 + 4


def combine_phase(nc, y, keep, d, out, consts):
    with ExitStack() as ctx:
        sb = lambda n, s, dt=F32: ctx.enter_context(nc.sbuf_tensor("e_" + n, s, dt))
        sem = lambda n: ctx.enter_context(nc.semaphore("e_" + n))
        Gt = sb("G", [P, 2, TOPK, LEN])
        posi = sb("posi", [P, TILES * TOPK], I32)
        posc = sb("posc", [P, 2, TOPK], I32)
        rwc = sb("rwc", [P, 2, TOPK])
        acc = sb("acc", [P, 2, LEN])
        o = sb("o", [P, 2, LEN])
        bn, sta = sb("bn", [P, 6]), sb("sta", [P, 2, 6])
        s_posi, s_posc, passed, passed_v = sem("posi"), sem("posc"), sem("passed"), sem("passed_v")
        got = [sem(f"got{i}") for i in range(2 * TOPK)]
        sv, root, outr = sem("steps"), sem("root"), sem("out_ready")
        stored = [sem("stored0"), sem("stored1")]
        used = sem("used")
        PE_ = TOPK + 6
        with nc.Block() as block:
            @block.gpsimd
            def _(pool):
                G_ = nc.gpsimd
                pool.wait_ge(s_posi, 1)

                def tile(n, par, head):
                    if not head:
                        pool.wait_ge(used, n - 1)
                        pool.sem_inc(passed, 1)
                    G_.tensor_copy(posc[:, par], posi[:, bass.ds(n * TOPK, TOPK)]).then_inc(s_posc, 1)
                    pool.wait_ge(s_posc, n + 1)
                    pool.sem_inc(passed, 1)
                    for k in range(TOPK):
                        G_.indirect_dma_start(Gt[:, par, k], None, d["slots"],
                                              bass.IndirectOffsetOnAxis(ap=posc[:, par, k:k + 1], axis=0)).then_inc(got[par * TOPK + k], 16)
                tile(0, 0, True)
                tile(1, 1, True)
                with G_.Fori(1, TILES // 2) as i:
                    tile(i * 2, 0, False)
                    tile(i * 2 + 1, 1, False)

            @block.vector
            def _(dve):
                V_ = nc.vector
                V_.tensor_copy(posi[:], keep["slots"][:, 0:TILES * TOPK]).then_inc(s_posi, 1)
                st = Steps(sv)

                def do(ins, wait=True):
                    st.inc(ins)
                    if wait:
                        st.wait(dve)

                def tile(n, par, head):
                    st.start, st.n = n * PE_, 0
                    do(V_.tensor_copy(rwc[:, par], keep["rw"][:, bass.ds(n * TOPK, TOPK)]))
                    for k in range(TOPK):
                        dve.wait_ge(got[par * TOPK + k], (n - par) * 8 + 16)
                        before = y[:, bass.ds(n, 1)].rearrange("p o n -> p (o n)") if k == 0 else acc[:, par]
                        do(V_.scalar_tensor_tensor(acc[:, par], Gt[:, par, k], rwc[:, par, k:k + 1], before,
                                                   ALU.mult, ALU.add))
                    V_.tensor_copy(sta[:, par, 5:6], acc[:, par, 0:1]).then_inc(used, 1)
                    do(V_.bn_stats(bn[:], acc[:, par]))
                    dve.sem_inc(passed_v, 1)
                    do(V_.bn_aggr(sta[:, par, 0:2], bn[:]))
                    do(V_.tensor_scalar(sta[:, par, 2:3], sta[:, par, 1:2], EPS, None, ALU.add))
                    do(V_.reciprocal(sta[:, par, 3:4], sta[:, par, 2:3]))
                    dve.wait_ge(root, n + 1)
                    do(V_.scalar_tensor_tensor(sta[:, par, 5:6], sta[:, par, 0:1], -1.0, sta[:, par, 4:5], ALU.mult, ALU.mult), False)
                    assert st.n == PE_
                tile(0, 0, True)
                tile(1, 1, True)
                with V_.Fori(1, TILES // 2) as i:
                    tile(i * 2, 0, False)
                    tile(i * 2 + 1, 1, False)

            @block.scalar
            def _(act):
                def tile(n, par, head):
                    act.wait_ge(sv, n * PE_ + (TOPK + 5))
                    nc.scalar.activation(sta[:, par, 4:5], sta[:, par, 3:4], ACT.Sqrt).then_inc(root, 1)
                    act.wait_ge(sv, n * PE_ + PE_)
                    if not head:
                        act.wait_ge(stored[par], (n - par) * 8)
                    nc.scalar.activation(o[:, par], acc[:, par], ACT.Identity, bias=sta[:, par, 5:6], scale=sta[:, par, 4:5]).then_inc(outr, 1)
                tile(0, 0, True)
                tile(1, 1, True)
                with nc.scalar.Fori(1, TILES // 2) as i:
                    tile(i * 2, 0, False)
                    tile(i * 2 + 1, 1, False)

            @block.sync
            def _(sp):
                ov = out.rearrange("b (u p) n -> p (b u) n", p=P)
                with nc.sync.Fori(0, TILES // 2) as i:
                    for par in range(2):
                        n = i * 2 + par
                        sp.wait_ge(outr, n + 1)
                        sp.dma_start(ov[:, bass.ds(n, 1)].rearrange("p o n -> p (o n)"), o[:, par]).then_inc(stored[par], 16)
                for par in range(2):
                    sp.wait_ge(stored[par], 16 * TILES // 2)


def build(nc, d, out):
    with ExitStack() as ctx:
        consts_sb = ctx.enter_context(nc.sbuf_tensor("consts_sb", [P, d["consts"].shape[1]], F32))
        keep = keeps(nc, ctx)
        d["lists"] = nc.dram_tensor("lists", (EXPERTS * TOK, 1), I32, kind="Internal").ap()
        d["h1"] = nc.dram_tensor("h1", (TOK, LEN), F32, kind="Internal").ap()
        d["slots"] = nc.dram_tensor("slots", (MAX_TILES * P, LEN), F32, kind="Internal").ap()
        consts_loaded = ctx.enter_context(nc.semaphore("consts_loaded"))
        with nc.Block() as block:
            @block.sync
            def _(sp):
                sp.dma_start(consts_sb[:], d["consts"]).then_inc(consts_loaded, 16)
                sp.wait_ge(consts_loaded, 16)
        hT = ctx.enter_context(nc.sbuf_tensor("hT", [P, FCH, TOK], F32))
        tok_phase(nc, d["c"], d["log_dt"], d["log_w_real"], d["w_imag"], consts_sb, hT)
        y = ctx.enter_context(nc.sbuf_tensor("y", [P, TILES, LEN], F32))
        attention_phase(nc, hT, y, d["w_qkv"], [d["lq1"], d["lq2"], d["lk1"], d["lk2"]], consts_sb)
        mix_phase(nc, hT, y, keep, d, consts_sb)
        expert_phase(nc, keep, d, consts_sb)
        combine_phase(nc, y, keep, d, out, consts_sb)


def kernel(x, L0_tok_log_dt, L0_tok_log_w_real, L0_tok_w_imag, L0_attn_w_qkv, L0_attn_wo, L0_attn_lambda_q1,
           L0_attn_lambda_q2, L0_attn_lambda_k1, L0_attn_lambda_k2, L0_attn_gamma, L0_attn_beta, L0_ffn_gate_w,
           L0_ffn_gu_w, L0_ffn_dp_w, L0_ffn_sh_gate_w, L0_ffn_sh_up_w, L0_ffn_sh_down_w, L0_ffn_sh_gate1_w):
    import numpy as _np
    import concourse.bacc as _bacc
    from concourse import mybir as _mybir
    from concourse.bass_utils import run_bass_kernel_spmd as _run

    lay = _np.ascontiguousarray
    gu = _np.asarray(L0_ffn_gu_w).transpose(0, 2, 1).reshape(EXPERTS, FCH, P, 2 * INTER).transpose(0, 2, 1, 3)
    w_experts = _np.concatenate([gu.reshape(EXPERTS, P, FCH * 2 * INTER), _np.asarray(L0_ffn_dp_w).transpose(0, 2, 1)], 2)
    w_joint = _np.concatenate([_np.asarray(a) for a in (L0_ffn_gate_w, L0_ffn_sh_up_w, L0_ffn_sh_gate_w, L0_ffn_sh_gate1_w)], 0).T
    arrays = {
        "c": _np.asarray(x).transpose(3, 2, 1, 0), "log_dt": L0_tok_log_dt,
        "log_w_real": _np.asarray(L0_tok_log_w_real).T, "w_imag": _np.asarray(L0_tok_w_imag).T,
        "w_qkv": _np.asarray(L0_attn_w_qkv).T, "wo": _np.asarray(L0_attn_wo).T,
        "lq1": L0_attn_lambda_q1, "lq2": L0_attn_lambda_q2, "lk1": L0_attn_lambda_k1, "lk2": L0_attn_lambda_k2,
        "gamma": L0_attn_gamma, "beta": L0_attn_beta, "w_joint": w_joint, "sh_down": _np.asarray(L0_ffn_sh_down_w).T,
        "w_experts": w_experts, "consts": const_table(),
    }
    arrays = {"in_" + n: lay(_np.asarray(a)) for n, a in arrays.items()}
    nc = _bacc.Bacc("TRN2", target_bir_lowering=False, num_devices=1)
    d = {n[3:]: nc.dram_tensor(n, a.shape, _mybir.dt.from_np(a.dtype), kind="ExternalInput").ap() for n, a in arrays.items()}
    out = nc.dram_tensor("out", (BATCH, SEQ, LEN), _mybir.dt.float32, kind="ExternalOutput").ap()
    build(nc, d, out)
    r = _run(nc, [arrays], core_ids=[0])
    return r.results[0]["out"]
```

```python
import concourse.bass as bass
from concourse import mybir
from contextlib import ExitStack
import math
import numpy as np

F32 = mybir.dt.float32
F32R = mybir.dt.float32r
BF16 = mybir.dt.bfloat16
I32 = mybir.dt.int32
U32 = mybir.dt.uint32
ACT = mybir.ActivationFunctionType
ALU = mybir.AluOpType
AX = mybir.AxisListType

P = 128
BATCH, SEQ, MODES, LEN = 8, 256, 64, 512
TOK = BATCH * SEQ
TILES = TOK // P
FCH = LEN // P
FINE = 64
COARSE = LEN // FINE
ROUND = 1.5 * 2.0 ** 23
TURN = 6.2831845
INV_TURN = 1.0 / (2.0 * math.pi)

CONST = {}


def const_table():
    parts = {}
    p = np.arange(P)
    parts["ident"] = np.eye(P)
    parts["before"] = (p[:, None] < p[None, :]) * 1.0
    parts["ones"] = np.ones((P, P))
    parts["group"] = (p[:, None] // 16 == p[None, :] // 16) * (1.0 / 16)
    inv = np.float32(1.0) / np.power(np.float32(10000.0), np.arange(0, 32, 2, dtype=np.float32) / np.float32(32))
    ang = np.arange(SEQ, dtype=np.float32)[:, None] * inv[None, :].astype(np.float32)
    cos, sin = np.cos(ang), np.sin(ang)
    scaler = np.float32(32) ** np.float32(-0.5)
    for name, f in (("q", scaler), ("k", np.float32(1))):
        c = np.concatenate([cos, cos], 1) * f
        s = np.concatenate([-sin, sin], 1) * f
        for u in range(2):
            parts[f"cos_{name}{u}"] = c[u * P:(u + 1) * P]
            parts[f"sin_{name}{u}"] = s[u * P:(u + 1) * P]
    row = lambda v: np.broadcast_to(np.asarray(v, np.float64), (P, len(v)))
    parts["fine"] = row(np.arange(FINE))
    parts["coarse"] = row(np.arange(COARSE) * FINE)
    parts["experts"] = row(np.arange(64))
    parts["tiles128"] = row(np.arange(16) * 128)
    half = (p >= 64) * 1.0
    parts["phase_v"] = (0.25 - 0.25 * half)[:, None]
    parts["phase_a"] = (0.25 + 0.25 * half)[:, None]
    parts["phase_b"] = (0.50 + 0.25 * half)[:, None]
    parts["minus_half"] = np.full((P, 1), -0.5)
    parts["eps"] = np.full((P, 1), 1e-5)
    parts["lane"] = p[:, None] * 1.0
    at = 0
    for name, a in parts.items():
        CONST[name] = (at, a.shape[1])
        at += a.shape[1]
    return np.ascontiguousarray(np.concatenate(list(parts.values()), 1).astype(np.float32))


class Steps:

    def __init__(self, sem):
        self.sem, self.start, self.n = sem, 0, 0

    def inc(self, ins):
        ins.then_inc(self.sem, 1)
        self.n += 1
        return self.n

    def wait(self, engine, n=None):
        engine.wait_ge(self.sem, self.start + (self.n if n is None else n))


def bc(ap, axis, n):
    a = ap.unsqueeze(axis)
    shape = list(a.shape)
    shape[axis] = n
    return a.to_broadcast(shape)


def tok_phase(nc, c_in, log_dt, lwr, wim, consts, hT):
    HB = 16
    NB = SEQ // HB
    with ExitStack() as ctx:
        sb = lambda n, s, d=F32: ctx.enter_context(nc.sbuf_tensor("a_" + n, s, d))
        sem = lambda n: ctx.enter_context(nc.semaphore("a_" + n))
        C = sb("C", [P, 2, SEQ, BATCH])
        ldt, lw, wi = sb("ldt", [P, SEQ]), sb("lw", [P, SEQ]), sb("wi", [P, SEQ])
        sm = sb("small", [P, 14, SEQ])
        dt, ew, dr, di, ti, e, th, rs, rc, s_, c_, qr, qi, tmp = [sm[:, i, :] for i in range(14)]
        tmpb, er, ei = ldt[:], th, dt
        U = sb("U", [P, 4, SEQ, COARSE])
        mag, ta, tb, work = [U[:, i] for i in range(4)]
        A, B = sb("A", [P, SEQ, COARSE]), sb("B", [P, SEQ, COARSE])
        EV = sb("EV", [P, SEQ, FINE])
        tT, t2, kk, V = [U[:, i].rearrange("p (t h x) a -> p t h (x a)", t=2, h=HB) for i in range(4)]
        G = sb("G", [P, 2, HB, COARSE, BATCH])
        G2 = sb("G2", [P, 2, HB, COARSE, BATCH])
        ps = ctx.enter_context(nc.psum_tensor("a_ps", [P, 2, HB, FCH, BATCH], F32))
        loaded = sem("loaded")
        dve_s, act_s, pool_s = sem("dve"), sem("act"), sem("pool")
        angle, phased, rounded, residue, sine = sem("angle"), sem("phased"), sem("rounded"), sem("residue"), sem("sine")
        v_ready, g2_ready, g_ready, products, evac = sem("v"), sem("g2"), sem("g"), sem("products"), sem("evac")
        exps_in, exps = sem("exps_in"), sem("exps")
        g1_free = sem("g1")
        cst = lambda n: consts[:, CONST[n][0]:CONST[n][0] + CONST[n][1]]
        EB = 32
        with nc.Block() as block:
            @block.sync
            def _(sp):
                sp.dma_start(ldt[:], log_dt.partition_broadcast(P)).then_inc(loaded, 16)
                for h in range(2):
                    lo, hi = 64 * h, 64 * h + 64
                    sp.dma_start(lw[lo:hi, :], lwr).then_inc(loaded, 16)
                    sp.dma_start(wi[lo:hi, :], wim).then_inc(loaded, 16)
                    for r in range(2):
                        sp.dma_start(C[lo:hi, r], c_in[r]).then_inc(loaded, 16)
                sp.wait_ge(loaded, 16 * 9)

            @block.gpsimd
            def _(pool):
                pool.wait_ge(dve_s, 3)
                for i in range(SEQ // EB):
                    hs = slice(i * EB, (i + 1) * EB)
                    nc.gpsimd.tensor_tensor(EV[:, hs], bc(dr[:, hs], 2, FINE), bc(cst("fine"), 1, EB), ALU.mult).then_inc(exps_in, 1)
                pool.wait_ge(dve_s, TABLES)
                with nc.gpsimd.Fori(0, NB // 2) as i:
                    for par in range(2):
                        n = i * 2 + par
                        hs = bass.ds(n * HB, HB)
                        pool.wait_ge(phased, n + 1)
                        nc.gpsimd.tensor_tensor(tT[:, par], bc(di[:, hs], 2, FINE), bc(cst("fine"), 1, HB), ALU.mult).then_inc(angle, 1)
                        pool.wait_ge(g_ready, n + 1)
                        nc.gpsimd.tensor_tensor(G2[:, par], bc(C[:, 1, hs], 2, COARSE), bc(B[:, hs], 3, BATCH), ALU.mult).then_inc(g2_ready, 1)

            @block.vector
            def _(dve):
                st = Steps(dve_s)
                V_ = nc.vector

                def do(ins, wait=True):
                    st.inc(ins)
                    if wait:
                        st.wait(dve)

                dve.wait_ge(act_s, 2)
                do(V_.tensor_tensor(dr, ew, dt, ALU.mult), False)
                dve.wait_ge(loaded, 16 * 9)
                do(V_.tensor_tensor(di, wi[:], dt, ALU.mult))
                do(V_.tensor_scalar(di, di, INV_TURN, None, ALU.mult))
                do(V_.tensor_tensor(mag, bc(dr, 2, COARSE), bc(cst("coarse"), 1, SEQ), ALU.mult))
                do(V_.tensor_tensor(ta, bc(di, 2, COARSE), bc(cst("coarse"), 1, SEQ), ALU.mult))
                do(V_.tensor_scalar(ti, di, 0.5, None, ALU.mult))
                do(V_.tensor_scalar(tmp, ti, ROUND, ROUND, ALU.add, ALU.subtract))
                do(V_.tensor_tensor(rs, tmp, ti, ALU.subtract))
                do(V_.tensor_scalar(ti, ti, 0.25, None, ALU.add))
                do(V_.tensor_scalar(tmp, ti, ROUND, ROUND, ALU.add, ALU.subtract))
                do(V_.tensor_tensor(rc, tmp, ti, ALU.subtract))
                do(V_.tensor_scalar(tb, ta, cst("phase_b"), None, ALU.add))
                do(V_.tensor_scalar(ta, ta, cst("phase_a"), None, ALU.add))
                do(V_.tensor_scalar(work, ta, ROUND, ROUND, ALU.add, ALU.subtract))
                do(V_.tensor_tensor(ta, work, ta, ALU.subtract))
                do(V_.tensor_scalar(work, tb, ROUND, ROUND, ALU.add, ALU.subtract))
                do(V_.tensor_tensor(tb, work, tb, ALU.subtract))
                assert st.n == ANGLES
                dve.wait_ge(act_s, 2 + 3)
                do(V_.scalar_tensor_tensor(th, e, 1.0, th, ALU.add, ALU.mult))
                dve.wait_ge(act_s, 2 + 3 + 2)
                do(V_.tensor_tensor(tmp, s_, s_, ALU.mult), False)
                do(V_.tensor_tensor(tmpb, s_, c_, ALU.mult))
                do(V_.scalar_tensor_tensor(tmp, tmp, -2.0, e, ALU.mult, ALU.mult), False)
                do(V_.scalar_tensor_tensor(ei, tmpb, 2.0, e, ALU.mult, ALU.mult))
                do(V_.tensor_tensor(er, th, tmp, ALU.add))
                do(V_.tensor_tensor(tmp, ew, ew, ALU.mult), False)
                do(V_.tensor_tensor(tmpb, wi[:], wi[:], ALU.mult))
                do(V_.tensor_tensor(tmp, tmp, tmpb, ALU.add))
                do(V_.reciprocal(tmp, tmp))
                do(V_.tensor_tensor(qr, ei, wi[:], ALU.mult), False)
                do(V_.tensor_tensor(tmpb, er, ew, ALU.mult))
                do(V_.tensor_tensor(qr, qr, tmpb, ALU.subtract))
                do(V_.tensor_tensor(qr, qr, tmp, ALU.mult))
                do(V_.tensor_tensor(qi, er, wi[:], ALU.mult), False)
                do(V_.tensor_tensor(tmpb, ei, ew, ALU.mult))
                do(V_.tensor_tensor(qi, qi, tmpb, ALU.add))
                do(V_.scalar_tensor_tensor(qi, qi, -1.0, tmp, ALU.mult, ALU.mult))
                dve.wait_ge(act_s, 2 + 3 + 2 + 2)
                do(V_.tensor_tensor(ta, ta, mag, ALU.mult), False)
                do(V_.tensor_tensor(tb, tb, mag, ALU.mult))
                do(V_.tensor_tensor(A[:], ta, bc(qr, 2, COARSE), ALU.mult), False)
                do(V_.tensor_tensor(work, tb, bc(qi, 2, COARSE), ALU.mult))
                do(V_.tensor_tensor(A[:], A[:], work, ALU.add), False)
                do(V_.tensor_tensor(B[:], tb, bc(qr, 2, COARSE), ALU.mult), False)
                do(V_.tensor_tensor(mag, ta, bc(qi, 2, COARSE), ALU.mult))
                do(V_.tensor_tensor(B[:], B[:], mag, ALU.subtract))
                assert st.n == TABLES, st.n
                V_.tensor_copy(tmp, tmp).then_inc(g_ready, 1)
                V_.tensor_copy(tmpb, tmpb).then_inc(v_ready, 1)
                dve.wait_ge(exps, SEQ // EB)
                with V_.Fori(0, NB // 2) as i:
                    for par in range(2):
                        n = i * 2 + par
                        hs = bass.ds(n * HB, HB)
                        dve.wait_ge(rounded, n + 1)
                        V_.scalar_tensor_tensor(kk[:, par], kk[:, par], ROUND, t2[:, par], ALU.subtract, ALU.subtract).then_inc(residue, 1)
                        dve.wait_ge(products, n)
                        V_.tensor_tensor(G[:, par], bc(C[:, 0, hs], 2, COARSE), bc(A[:, hs], 3, BATCH), ALU.mult).then_inc(g1_free, 1)
                        dve.wait_ge(g1_free, n + 1)
                        dve.wait_ge(g2_ready, n + 1)
                        V_.tensor_tensor(G[:, par], G[:, par], G2[:, par], ALU.add).then_inc(g_ready, 1)
                        dve.wait_ge(sine, n + 1)
                        V_.tensor_tensor(V[:, par], kk[:, par], EV[:, hs], ALU.mult).then_inc(v_ready, 1)

            @block.scalar
            def _(act):
                A_ = nc.scalar
                act.wait_ge(loaded, 16 * 9)
                A_.activation(dt, ldt[:], ACT.Exp).then_inc(act_s, 1)
                A_.activation(ew, lw[:], ACT.Exp).then_inc(act_s, 1)
                act.wait_ge(dve_s, 1)
                A_.activation(e, dr, ACT.Exp, scale=-1.0).then_inc(act_s, 1)
                A_.activation(th, dr, ACT.Tanh, scale=-0.5).then_inc(act_s, 1)
                act.wait_ge(dve_s, 4)
                A_.activation(mag, mag, ACT.Exp, scale=-1.0).then_inc(act_s, 1)
                for i in range(SEQ // EB):
                    act.wait_ge(exps_in, i + 1)
                    A_.activation(EV[:, i * EB:(i + 1) * EB], EV[:, i * EB:(i + 1) * EB], ACT.Exp, scale=-1.0).then_inc(exps, 1)
                act.wait_ge(dve_s, ANGLES)
                A_.activation(s_, rs, ACT.Sin, scale=-TURN).then_inc(act_s, 1)
                A_.activation(c_, rc, ACT.Sin, scale=-TURN).then_inc(act_s, 1)
                A_.activation(ta, ta, ACT.Sin, scale=-TURN).then_inc(act_s, 1)
                A_.activation(tb, tb, ACT.Sin, scale=-TURN).then_inc(act_s, 1)
                A_.copy(rs, rs).then_inc(phased, 1)

                def sines(n, par):
                    act.wait_ge(angle, n + 1)
                    A_.activation(t2[:, par], tT[:, par], ACT.Identity, bias=cst("phase_v")).then_inc(phased, 1)
                    act.wait_ge(phased, n + 2)
                    act.wait_ge(v_ready, n)
                    A_.activation(kk[:, par], t2[:, par], ACT.Copy, bias=ROUND).then_inc(rounded, 1)
                    act.wait_ge(residue, n + 1)
                    A_.activation(kk[:, par], kk[:, par], ACT.Sin, scale=-TURN).then_inc(sine, 1)

                def evacuate(n, par):
                    act.wait_ge(products, n + 2)
                    out = hT[:].rearrange("p j (c s) -> p j c s", c=BATCH)[:, :, :, bass.ds(n * HB, HB)]
                    A_.activation(out, ps[:, par].rearrange("p h j c -> p j c h"), ACT.Copy, scale=2.0).then_inc(evac, 1)

                sines(0, 0)
                with A_.Fori(0, NB // 2 - 1) as i:
                    for par in range(2):
                        sines(i * 2 + par + 1, 1 - par)
                        evacuate(i * 2 + par, par)
                sines(NB - 1, 1)
                evacuate(NB - 2, 0)
                evacuate(NB - 1, 1)

            @block.tensor
            def _(pe):
                pe.sem_inc(products, 1)
                pe.sem_inc(evac, 1)
                with nc.tensor.Fori(0, NB // 2) as i:
                    for par in range(2):
                        n = i * 2 + par
                        pe.wait_ge(g_ready, n + 2)
                        pe.wait_ge(v_ready, n + 2)
                        pe.wait_ge(evac, n)
                        for h in range(HB):
                            for odd in range(2):
                                ins = nc.tensor.matmul(ps[64 * odd:64 * odd + 64, par, h], V[:, par, h],
                                                       G[:, par, h].rearrange("p (j o) c -> p o j c", o=2)[:, odd],
                                                       start=True, stop=True)
                        ins.then_inc(products, 1)


ANGLES, TABLES = 17, 43



HEADS, HD = 16, 32
INIT_LAMBDA = 0.8


def attention_phase(nc, hT, y, w_qkv, lambdas, consts):
    UN = 2 * HEADS
    with ExitStack() as ctx:
        sb = lambda n, s, d=F32: ctx.enter_context(nc.sbuf_tensor("b_" + n, s, d))
        sem = lambda n: ctx.enter_context(nc.semaphore("b_" + n))
        pb = lambda n, s: ctx.enter_context(nc.psum_tensor("b_" + n, s, F32))
        cst = lambda n: consts[:, CONST[n][0]:CONST[n][0] + CONST[n][1]]
        W = sb("W", [P, FCH, 3 * LEN])
        hc = sb("hc", [P, FCH, SEQ])
        mulc, muls = sb("mulc", [P, LEN]), sb("muls", [P, LEN])
        xr = sb("xr", [P, 2, LEN])
        stack = sb("stack", [P, UN, 4, 16], F32R)
        qk = [sb(f"qk{i}", [P, 2, HEADS, SEQ], F32R) for i in range(2)]
        Vb = sb("Vb", [P, 2, 2, LEN])
        E = sb("E", [P, 2, 2, 2, SEQ])
        D = sb("D", [P, 2, 2, SEQ])
        DT = sb("DT", [P, 2, 2, 2, P])
        negmax, sums, mixw = sb("negmax", [P, 2, 2, 2]), sb("sums", [P, 2, 2, 2]), sb("mixw", [P, 2, 2])
        recips = sb("recips", [P, 2, HEADS, 2])
        maskb, identb = sb("maskb", [P, SEQ], BF16), sb("identb", [P, P], BF16)
        identr = sb("identr", [P, P], F32R)
        lam = sb("lam", [P, 4, HD])
        lamw = sb("lamw", [P, 2, HD])
        lams = sb("lams", [P, 4])
        pq = pb("pq", [P, LEN])
        pS = pb("pS", [P, 2, 2, 2, SEQ])
        pT = pb("pT", [P, 2, 2, P])
        pK = ctx.enter_context(nc.psum_tensor("b_pK", [P, 4, P], F32R))
        pO = pb("pO", [P, LEN])

        loaded, lam_loaded, setup = sem("loaded"), sem("lam_loaded"), sem("setup")
        s_hc, s_qkv, s_rm, s_xr, s_hi, s_lo = (sem(n) for n in ("hc", "qkv", "rope_mul", "roped", "hi", "lo"))
        s_qkb, s_qke, s_v = sem("qk_transposed"), sem("qk_evac"), sem("v_evac")
        s_scores, s_max, s_exp, s_small, s_d = (sem(n) for n in ("scores", "max", "exp", "small", "mixed"))
        s_t, s_dt, s_pv, s_y = (sem(n) for n in ("mixed_t", "mixed_t_evac", "pv", "y"))


        def walk(engine, slot):
            for j in range(LAG):
                slot(0, 0, j)
            with engine.Fori(0, BATCH // 2 - 1) as i:
                for j in range(LAG, PAIRS_):
                    slot(i * 2, 0, j)
                for j in range(PAIRS_):
                    slot(i * 2 + 1, 1, j)
                for j in range(LAG):
                    slot(i * 2 + 2, 0, j)
            for j in range(LAG, PAIRS_):
                slot(BATCH - 2, 0, j)
            for j in range(PAIRS_ + LAG):
                slot(BATCH - 1, 1, j)

        def behind(c, par, j, lag):
            j -= lag
            if j < 0:
                if isinstance(c, int) and c == 0:
                    return None
                c, par, j = c - 1, 1 - par, j + PAIRS_
            return (c, par, j, c * PAIRS_ + j) if j < PAIRS_ else None

        def pieces(table, c, j):
            more = j < PAIRS_ and not (isinstance(c, int) and c == BATCH - 1)
            return [table.get((j, place), ()) if more else () for place in (START, MID, END)]

        with nc.Block() as block:
            @block.sync
            def _(sp):
                for x in range(3):
                    cols = slice(x * LEN, (x + 1) * LEN)
                    sp.dma_start(W[:, :, cols], w_qkv.rearrange("(j p) n -> p j n", p=P)[:, :, cols]).then_inc(loaded, 16)
                    sp.wait_ge(loaded, 16 * (x + 1))
                    if x == 0:
                        for i, l in enumerate(lambdas):
                            sp.dma_start(lam[:, i, :], l.partition_broadcast(P)).then_inc(lam_loaded, 16)

            @block.gpsimd
            def _(pool):
                def prepare(b, t):
                    for x in range(2):
                        r = b * 4 + (2 * t + x)
                        pool.wait_ge(s_rm, r + 1)
                        nc.gpsimd.tensor_tensor(xr[:, x], mulc[:], muls[:], ALU.add).then_inc(s_xr, 1)
                        pool.wait_ge(s_hi, r + 1)
                        src = xr[:, x].rearrange("p (m d) -> p m d", d=16)
                        for half in range(2):
                            ms = slice(half * HEADS, (half + 1) * HEADS)
                            if x == 0:
                                out = stack[:].rearrange("p m (a r) d -> p m a r d", r=2)[:, ms, :, 1]
                            else:
                                out = stack[:, ms, 2:4]
                            nc.gpsimd.tensor_tensor(out, bc(src[:, ms], 2, 2), bc(stack[:, ms, 0].bitcast(F32), 2, 2),
                                                    ALU.subtract).then_inc(s_lo, 1)

                prepare(0, 0)
                prepare(0, 1)
                with nc.gpsimd.Fori(1, BATCH) as b:
                    prepare(b, 0)
                    prepare(b, 1)

            @block.vector
            def _(dve):
                V_ = nc.vector
                V_.tensor_copy(maskb[:, 0:P], cst("before")).then_inc(setup, 1)
                V_.tensor_copy(maskb[:, P:SEQ], cst("ones")).then_inc(setup, 1)
                V_.tensor_copy(identb[:], cst("ident")).then_inc(setup, 1)
                V_.tensor_copy(identr[:], cst("ident")).then_inc(setup, 1)
                dve.wait_ge(lam_loaded, 64)
                V_.tensor_tensor(lamw[:], lam[:, 0:2], lam[:, 2:4], ALU.mult).then_inc(setup, 1)
                dve.wait_ge(setup, 5)
                V_.reduce_sum(lams[:, 0:2], lamw[:], AX.X).then_inc(setup, 1)
                dve.wait_ge(setup, 7)
                V_.tensor_tensor(lams[:, 2:3], lams[:, 1:2], lams[:, 0:1], ALU.subtract).then_inc(setup, 1)
                dve.wait_ge(setup, 8)
                V_.tensor_scalar(lams[:, 3:4], lams[:, 2:3], -INIT_LAMBDA, None, ALU.add).then_inc(setup, 1)
                dve.wait_ge(setup, 9)
                dve.sem_inc(s_d, 4)

                def rope(b, t, x):
                    r = b * 4 + (2 * t + x)
                    name = "qk"[x]
                    dve.wait_ge(s_qkv, b * 6 + (3 * t + x + 1))
                    dve.wait_ge(s_xr, r)
                    src = pq[:].rearrange("p (h s d) -> p s h d", s=2, d=16)
                    cos = cst(f"cos_{name}{t}")[:, 0:16]
                    sin = cst(f"sin_{name}{t}")
                    V_.tensor_tensor(mulc[:].rearrange("p (s h d) -> p s h d", s=2, d=16), src,
                                     bc(bc(cos, 1, HEADS), 1, 2), ALU.mult)
                    ms = muls[:].rearrange("p (s h d) -> p s h d", s=2, d=16)
                    V_.tensor_tensor(ms[:, 0], src[:, 1], bc(sin[:, 0:16], 1, HEADS), ALU.mult)
                    V_.tensor_tensor(ms[:, 1], src[:, 0], bc(sin[:, 16:32], 1, HEADS), ALU.mult).then_inc(s_rm, 1)

                def evac(b, t, x, i, par):
                    w = b * 16 + (8 * t + 4 * x + i)
                    dve.wait_ge(s_qkb, w + 1)
                    V_.tensor_copy(qk[par][:, x, 4 * i:4 * i + 4, t * P:(t + 1) * P], pK[:]).then_inc(s_qke, 1)

                def negmax_of(m, j, g):
                    dve.wait_ge(s_scores, m * 2 + (g + 1))
                    V_.tensor_reduce(negmax[:, j % 2, g], pS[:, j % 2, g], AX.X, ALU.max, negate=True).then_inc(s_max, 1)

                def slot(c, par, j):
                    now, last = behind(c, par, j, 0), behind(c, par, j, 1)
                    begin, mid, _ = pieces(DVE_PIECES, c, j)

                    def piece(p):
                        rope(c + 1, *p[1:]) if p[0] == "rope" else evac(c + 1, *p[1:], 1 - par)
                    for p in begin:
                        piece(p)
                    if now:
                        negmax_of(now[3], j, 0)
                    if last:
                        _, _, jl, ml = last
                        u, h = divmod(2 * jl, HEADS)
                        l2 = jl % 2
                        dve.wait_ge(s_exp, ml * 2 + 6)
                        V_.reciprocal(recips[:, u, h:h + 2], sums[:, l2]).then_inc(s_small, 1)
                    if now:
                        negmax_of(now[3], j, 1)
                    for p in mid:
                        piece(p)
                    if last:
                        dve.wait_ge(s_small, ml * 2 + 1)
                        V_.scalar_tensor_tensor(mixw[:, l2], sums[:, l2, :, 0], lams[:, 3:4], recips[:, u, h:h + 2, 1],
                                                ALU.mult, ALU.mult).then_inc(s_small, 1)
                        dve.wait_ge(s_small, ml * 2 + 2)
                        dve.wait_ge(s_t, ml + 1)
                        for g in range(2):
                            V_.scalar_tensor_tensor(D[:, l2, g], E[:, l2, g, 1], mixw[:, l2, g:g + 1], E[:, l2, g, 0],
                                                    ALU.mult, ALU.add).then_inc(s_d, 1)
                    done = behind(c, par, j, LAG)
                    if done and done[2] % (PAIRS_ // 2) == PAIRS_ // 2 - 1:
                        cd, _, jd, md = done
                        u = jd // (PAIRS_ // 2)
                        dve.wait_ge(s_pv, md + (1 + 2))
                        V_.tensor_tensor(y[:, bass.ds(cd * 2 + u, 1)].rearrange("p o (h d) -> p (o h) d", d=HD),
                                         pO[:].rearrange("p (h d) -> p h d", d=HD),
                                         bc(recips[:, u, :, 0], 2, HD), ALU.mult).then_inc(s_y, 1)

                rope(0, 0, 0)
                for t, x in ((0, 0), (0, 1), (1, 0), (1, 1)):
                    if (t, x) != (1, 1):
                        rope(0, *((t, 1) if x == 0 else (1, 0)))
                    for i in range(4):
                        evac(0, t, x, i, 0)
                walk(V_, slot)

            @block.scalar
            def _(act):
                A_ = nc.scalar
                act.wait_ge(setup, 6)
                A_.activation(lams[:, 0:2], lams[:, 0:2], ACT.Exp).then_inc(setup, 1)
                act.sem_inc(s_exp, 4)

                def take(b):
                    act.wait_ge(s_qkv, b * 6)
                    A_.activation(hc[:], hT[:, :, bass.ds(b * SEQ, SEQ)], ACT.Copy).then_inc(s_hc, 1)

                def high(b, t, x):
                    r = b * 4 + (2 * t + x)
                    act.wait_ge(s_xr, r + 1)
                    act.wait_ge(s_qkb, r * 4)
                    if x == 0:
                        out = stack[:].rearrange("p m (a r) d -> p m a r d", r=2)[:, :, :, 0]
                    else:
                        out = stack[:, :, 0:2]
                    A_.activation(out, bc(xr[:, x].rearrange("p (m d) -> p m d", d=16), 2, 2), ACT.Copy).then_inc(s_hi, 1)

                def values(b, t, par):
                    act.wait_ge(s_qkv, b * 6 + (3 * t + 3))
                    A_.activation(Vb[:, par, t], pq[:], ACT.Copy).then_inc(s_v, 1)

                def slot(c, par, j):
                    now, turned = behind(c, par, j, 0), behind(c, par, j, 2)
                    begin, mid, _ = pieces(ACT_PIECES, c, j)

                    def piece(p):
                        if p[0] == "take":
                            take(c + 1)
                        elif p[0] == "high":
                            high(c + 1, *p[1:])
                        else:
                            values(c + 1, p[1], 1 - par)
                    for p in begin:
                        piece(p)
                    if now:
                        for g in range(2):
                            act.wait_ge(s_max, now[3] * 2 + (g + 1))
                            act.wait_ge(s_d, now[3] * 2 + (g + 1))
                            for s in range(2):
                                ins = A_.activation(E[:, j % 2, g, s], pS[:, j % 2, g, s], ACT.Exp,
                                                    bias=negmax[:, j % 2, g, s:s + 1], accum_out=sums[:, j % 2, g, s:s + 1])
                            ins.then_inc(s_exp, 1)
                    for p in mid:
                        piece(p)
                    if turned:
                        _, _, jt, mt = turned
                        act.wait_ge(s_t, mt + 3)
                        act.wait_ge(s_pv, mt + 1)
                        A_.activation(DT[:, jt % 2], pT[:], ACT.Copy).then_inc(s_dt, 1)

                take(0)
                for t in range(2):
                    high(0, t, 0)
                    values(0, t, 0)
                    high(0, t, 1)
                walk(A_, slot)

            @block.tensor
            def _(pe):
                T_ = nc.tensor
                pe.wait_ge(setup, 4)
                pe.sem_inc(s_t, 2)
                pe.sem_inc(s_pv, 2)

                def project(b, t, x, f):
                    if f in (0, None):
                        pe.wait_ge(s_hc, b + 1)
                        if x == 0:
                            pe.wait_ge(s_v, b * 2 + t)
                        else:
                            pe.wait_ge(s_rm, b * 4 + (2 * t + x))
                    for f in (range(FCH) if f is None else (f,)):
                        ins = T_.matmul(pq[:], hc[:, f, t * P:(t + 1) * P], W[:, f, x * LEN:(x + 1) * LEN],
                                        start=(f == 0), stop=(f == FCH - 1))
                    if f == FCH - 1:
                        ins.then_inc(s_qkv, 1)

                def turn(b, t, x, i):
                    w = b * 16 + (8 * t + 4 * x + i)
                    pe.wait_ge(s_lo, b * 8 + (2 * (2 * t + x) + i // 2 + 1))
                    pe.wait_ge(s_qke, w)
                    for q in range(4):
                        m = (4 * i + q) * 2
                        ins = T_.transpose(pK[:, q], stack[:, m:m + 2].rearrange("p m r d -> p (m r d)"), identr[:])
                    ins.then_inc(s_qkb, 1)

                def scores(m, j, g, par):
                    u, h = divmod(2 * j + g, HEADS)
                    hp = h // 2
                    pe.wait_ge(s_exp, m * 2 + (g + 1))
                    rows = slice(64 * g, 64 * g + 64)
                    for s in range(2):
                        T_.matmul(pS[:, j % 2, g, s], qk[par][rows, 0, s * 8 + hp, u * P:(u + 1) * P],
                                  qk[par][rows, 1, s * 8 + hp, :], start=(s == 0), stop=False, skip_group_check=True)
                    out, mask = (pS[:, j % 2, g], maskb[:]) if u == 0 else (pS[:, j % 2, g, :, P:SEQ], maskb[:, 0:P])
                    T_.matmul(out, identb[:], bc(mask, 1, 2), start=False, stop=True, skip_group_check=True).then_inc(s_scores, 1)

                def slot(c, par, j):
                    now, mixed, turned = behind(c, par, j, 0), behind(c, par, j, 2), behind(c, par, j, LAG)
                    begin, mid, end = pieces(PE_PIECES, c, j)

                    def piece(p):
                        (project if p[0] == "project" else turn)(c + 1, *p[1:])
                    for p in begin:
                        piece(p)
                    if now:
                        if j == 0:
                            pe.wait_ge(s_qke, c * 16 + 16)
                        for g in range(2):
                            scores(now[3], j, g, par)
                    if mixed:
                        _, _, jm, mm = mixed
                        pe.wait_ge(s_d, mm * 2 + 6)
                        pe.wait_ge(s_dt, mm)
                        for g in range(2):
                            for kt in range(2):
                                ins = T_.transpose(pT[:, g, kt], D[:, jm % 2, g, kt * P:(kt + 1) * P], cst("ident"))
                        ins.then_inc(s_t, 1)
                    for p in mid:
                        piece(p)
                    if turned:
                        ct, pt, jt, mt = turned
                        u, h = divmod(2 * jt, HEADS)
                        pe.wait_ge(s_dt, mt + 1)
                        if jt == 0:
                            pe.wait_ge(s_v, ct * 2 + 2)
                        if h == 0:
                            pe.wait_ge(s_y, ct * 2 + u)
                        for g in range(2):
                            for kt in range(2):
                                cols = slice((h + g) * HD, (h + g + 1) * HD)
                                ins = T_.matmul(pO[:, cols], DT[:, jt % 2, g, kt], Vb[:, pt, kt, cols],
                                                start=(kt == 0), stop=(kt == 1))
                        ins.then_inc(s_pv, 1)
                    for p in end:
                        piece(p)

                pe.wait_ge(loaded, 16)
                project(0, 0, 0, None)
                pe.wait_ge(loaded, 32)
                project(0, 0, 1, None)
                for i in range(4):
                    turn(0, 0, 0, i)
                pe.wait_ge(loaded, 48)
                project(0, 0, 2, None)
                project(0, 1, 0, None)
                for i in range(4):
                    turn(0, 0, 1, i)
                project(0, 1, 1, None)
                project(0, 1, 2, None)
                for x in range(2):
                    for i in range(4):
                        turn(0, 1, x, i)
                walk(T_, slot)


LAG, PAIRS_ = 3, HEADS
START, MID, END = 0, 1, 2
PE_PIECES, DVE_PIECES, ACT_PIECES = {}, {}, {(0, START): [("take",)]}
FIRST_SLOT = (0, 2, 5, 7, 9, 11)
for _t in range(2):
    for _x in range(3):
        _s = FIRST_SLOT[3 * _t + _x]
        for _f, _at in enumerate(((_s, END), (_s + 1, MID), (_s + 1, END), (_s + 2, START))):
            PE_PIECES.setdefault(_at, []).append(("project", _t, _x, _f))
        if _x < 2:
            DVE_PIECES.setdefault((_s + 2, START), []).append(("rope", _t, _x))
        else:
            ACT_PIECES.setdefault((_s + 2, START), []).append(("values", _t))
for _t, _x, _high, _turn in ((0, 0, (3, START), 4), (0, 1, (6, START), 7), (1, 0, (10, START), 10), (1, 1, (12, START), 13)):
    ACT_PIECES.setdefault(_high, []).append(("high", _t, _x))
    for _i in range(4):
        PE_PIECES.setdefault((_turn + (_i + 1) // 2, (END, MID)[_i % 2]), []).append(("turn", _t, _x, _i))
        DVE_PIECES.setdefault((_turn + 1 + _i // 2, (START, MID)[_i % 2]), []).append(("evac", _t, _x, _i))



EXPERTS, TOPK, INTER = 64, 8, 128
EPS = 1e-5
UP, GATE, GATE1 = 64, 192, 320
JOINT = 321


def mix_phase(nc, hT, y, keep, d, consts):
    with ExitStack() as ctx:
        sb = lambda n, s, dt=F32: ctx.enter_context(nc.sbuf_tensor("c_" + n, s, dt))
        sem = lambda n: ctx.enter_context(nc.semaphore("c_" + n))
        pb = lambda n, s: ctx.enter_context(nc.psum_tensor("c_" + n, s, F32))
        cst = lambda n: consts[:, CONST[n][0]:CONST[n][0] + CONST[n][1]]
        Wo = sb("Wo", [P, FCH, LEN])
        Wj = sb("Wj", [P, FCH, JOINT])
        Wd = sb("Wd", [P, LEN])
        gb = sb("gb", [P, 2, 2, 2])
        hs = sb("hs", [P, FCH, P])
        z = sb("z", [P, 2, LEN // 2])
        zT = sb("zT", [P, FCH, P])
        h1 = sb("h1", [P, 2, LEN])
        h1T = sb("h1T", [P, FCH, P])
        bn = sb("bn", [P, 6])
        mark = sb("mark", [P, 1])
        sta = sb("sta", [P, 16])
        stb = sb("stb", [P, 6])
        ab = sb("ab", [P, 2, 2])
        top, topi, topf = sb("top", [P, TOPK]), sb("topi", [P, TOPK], U32), sb("topf", [P, TOPK])
        negtop, wsum = sb("negtop", [P, 1]), sb("wsum", [P, 2])
        onehot, picked = sb("onehot", [P, TOPK, EXPERTS]), sb("picked", [P, TOPK, EXPERTS])
        chosen = sb("chosen", [P, EXPERTS], BF16)
        R = sb("R", [P, EXPERTS])
        posf, pos = sb("posf", [P, TOPK]), sb("pos", [P, 2, TOPK], I32)
        tok = sb("tok", [P, TILES], I32)
        tokc = sb("tokc", [P, 2, 1], I32)
        ex, rc, inter = sb("ex", [P, INTER + 1]), sb("rc", [P, INTER + 1]), sb("inter", [P, INTER])
        interT = sb("interT", [P, INTER])
        beforeb, onesb = sb("beforeb", [P, P], BF16), sb("onesb", [P, P], BF16)
        zero = sb("zero", [P, EXPERTS * TOK // P], I32)
        pG, pZ, pA, pX = pb("pG", [P, 2, 256]), pb("pZ", [P, LEN]), pb("pA", [P, LEN]), pb("pX", [P, LEN])
        pR, pC, pI, pD = pb("pR", [P, LEN]), pb("pC", [P, LEN]), pb("pI", [P, LEN]), pb("pD", [P, LEN])
        rw, ranks, experts, carry = keep["rw"], keep["ranks"], keep["experts"], keep["counts"]

        loaded, setup = sem("loaded"), sem("setup")
        listed0, spared = sem("list_zero"), sem("spare_zero")
        sA, sB = sem("dve_a"), sem("dve_b")
        group, s_hs, zt, zte, joined = sem("group"), sem("hs"), sem("zt"), sem("zt_evac"), sem("wo")
        h1t, h1te, joint, s_ex, s_w8 = sem("h1t"), sem("h1t_evac"), sem("joint"), sem("ex"), sem("w8")
        rank, it, ite, down = sem("rank"), sem("it"), sem("it_evac"), sem("down")
        h1_ready, h1_out, posr = sem("h1_ready"), [sem("h1_out0"), sem("h1_out1")], sem("pos_ready")
        listed = [sem("listed0"), sem("listed1")]
        zeroed, passed, passed_p, roots = sem("zeroed"), sem("passed"), sem("passed_pool"), sem("roots")
        LOADS = 16 * 7
        PA, PB = 13, 17

        with nc.Block() as block:
            @block.sync
            def _(sp):
                sp.dma_start(Wo[:], d["wo"].rearrange("(j p) n -> p j n", p=P)).then_inc(loaded, 16)
                sp.dma_start(Wj[:], d["w_joint"].rearrange("(j p) n -> p j n", p=P)).then_inc(loaded, 16)
                sp.dma_start(Wd[:], d["sh_down"]).then_inc(loaded, 16)
                for i, n in enumerate(("gamma", "beta")):
                    for u in range(2):
                        sp.dma_start(gb[:, i, u], d[n].rearrange("(u p a) -> u p a", p=P, a=2)[u]).then_inc(loaded, 16)
                sp.wait_ge(zeroed, 1)
                sp.dma_start(d["lists"].rearrange("(p n) a -> p (n a)", p=P), zero[:]).then_inc(listed0, 16)
                sp.wait_ge(listed0, 16)
                spare = d["slots"].rearrange("(t p) n -> p t n", p=P)[:, TOK * TOPK // P:]
                sp.dma_start(spare, bc(zero[:, 0:LEN].bitcast(F32), 1, EXPERTS)).then_inc(spared, 16)
                with nc.sync.Fori(0, TILES // 2) as i:
                    for par in range(2):
                        n = i * 2 + par
                        sp.wait_ge(h1_ready, n + 1)
                        sp.dma_start(d["h1"].rearrange("(t p) n -> p t n", p=P)[:, bass.ds(n, 1)], h1[:, par:par + 1]).then_inc(h1_out[par], 16)
                for par in range(2):
                    sp.wait_ge(h1_out[par], 16 * TILES // 2)
                sp.wait_ge(spared, 16)

            @block.gpsimd
            def _(pool):
                nc.gpsimd.memset(zero[:], 0).then_inc(zeroed, 1)
                pool.wait_ge(listed0, 16)
                def root(n, which):
                    pool.wait_ge(sA, n * PA + (6 if which == 0 else 12))
                    src, dst = ((5, 12), (9, 13))[which]
                    nc.gpsimd.tensor_tensor(sta[:, dst:dst + 1], sta[:, src:src + 1], cst("eps"), ALU.add).then_inc(roots, 1)
                    pool.wait_ge(roots, n * 4 + (2 * which + 1))
                    nc.gpsimd.tensor_tensor(sta[:, dst:dst + 1], sta[:, dst:dst + 1], cst("minus_half"), ALU.pow).then_inc(roots, 1)

                def both(n, par, more):
                    if more:
                        root(n + 1, 0)
                        root(n + 1, 1)
                    pool.wait_ge(posr, n + 1)
                    pool.sem_inc(passed_p, 1)
                    for k in range(TOPK):
                        nc.gpsimd.indirect_dma_start(
                            d["lists"], bass.IndirectOffsetOnAxis(ap=pos[:, par, k:k + 1], axis=0),
                            tokc[:, par], None).then_inc(listed[par], 16)

                root(0, 0)
                root(0, 1)
                with nc.gpsimd.Fori(0, TILES // 2 - 1) as i:
                    both(i * 2, 0, True)
                    both(i * 2 + 1, 1, True)
                both(TILES - 2, 0, True)
                both(TILES - 1, 1, False)
                for par in range(2):
                    pool.wait_ge(listed[par], 16 * TOPK * TILES // 2)

            @block.vector
            def _(dve):
                V_ = nc.vector
                V_.tensor_copy(beforeb[:], cst("before")).then_inc(setup, 1)
                V_.tensor_copy(onesb[:], cst("ones")).then_inc(setup, 1)
                V_.memset(carry, 0.0).then_inc(setup, 1)
                V_.memset(ranks[:, TILES * TOPK:], 0.0)
                V_.memset(experts[:, TILES * TOPK:], 0.0)
                for t in range(TILES):
                    V_.tensor_scalar(tok[:, t:t + 1], cst("lane"), float(P * t), None, ALU.add).then_inc(setup, 1)
                dve.wait_ge(setup, 3 + TILES)
                dve.wait_ge(loaded, LOADS)
                a, b = Steps(sA), Steps(sB)

                def do(st, ins, wait=True, alone=False):
                    st.inc(ins)
                    if wait:
                        st.wait(dve)
                    if alone:
                        dve.sem_inc(passed, 1)

                def first(n, par):
                    a.start, a.n = n * PA, 0
                    yt = y[:, bass.ds(n, 1)].rearrange("p o n -> p (o n)")
                    do(a, V_.bn_stats(bn[:], yt), alone=True)
                    do(a, V_.bn_aggr(sta[:, 0:2], bn[:]))
                    yield
                    dve.wait_ge(group, n * 2 + 1)
                    do(a, V_.tensor_copy(sta[:, 2:3], pG[:, 0, 0:1]))
                    do(a, V_.tensor_tensor(sta[:, 3:4], sta[:, 0:1], sta[:, 2:3], ALU.subtract))
                    do(a, V_.scalar_tensor_tensor(sta[:, 4:5], sta[:, 3:4], sta[:, 3:4], sta[:, 1:2], ALU.mult, ALU.add))
                    yield
                    dve.wait_ge(group, n * 2 + 2)
                    do(a, V_.tensor_copy(sta[:, 5:6], pG[:, 0, 1:2]), False)
                    dve.wait_ge(roots, n * 4 + 2)
                    do(a, V_.tensor_scalar(ab[:, 0], gb[:, 0, par], sta[:, 12:13], 1.0 - INIT_LAMBDA, ALU.mult, ALU.mult))
                    do(a, V_.tensor_scalar(sta[:, 6:8], ab[:, 0], sta[:, 2:3], None, ALU.mult))
                    do(a, V_.scalar_tensor_tensor(ab[:, 1], gb[:, 1, par], 1.0 - INIT_LAMBDA, sta[:, 6:8], ALU.mult, ALU.subtract))
                    dve.wait_ge(zt, n)
                    for f in range(2):
                        ins = V_.tensor_scalar(z[:, f], yt[:, f * 256:(f + 1) * 256], ab[:, 0, f:f + 1], ab[:, 1, f:f + 1], ALU.mult, ALU.add)
                    do(a, ins)
                    yield
                    dve.wait_ge(joined, n + 1)
                    do(a, V_.bn_stats(bn[:], pA[:]), alone=True)
                    do(a, V_.bn_aggr(sta[:, 8:10], bn[:]), False)
                    dve.wait_ge(roots, n * 4 + 4)
                    if LATE[0]:
                        dve.wait_ge(h1_out[par], (n - par) * 8)
                    do(a, V_.tensor_scalar(h1[:, par], pA[:], sta[:, 8:9], sta[:, 13:14], ALU.subtract, ALU.mult), False)
                    assert a.n == PA
                    V_.tensor_copy(mark[:], cst("lane")).then_inc(h1_ready, 1)
                    yield

                def second(n, par):
                    b.start, b.n = n * PB, 0
                    dve.wait_ge(joint, n + 1)
                    dve.sem_inc(passed, 1)
                    logits = pR[:, 0:EXPERTS]
                    do(b, V_.max(top[:], logits), alone=True)
                    do(b, V_.max_index(topi[:], top[:], logits), False)
                    do(b, V_.tensor_scalar(negtop[:], top[:, 0:1], -1.0, None, ALU.mult))
                    do(b, V_.tensor_copy(topf[:], topi[:]))
                    do(b, V_.tensor_tensor(onehot[:], bc(cst("experts"), 1, TOPK), bc(topf[:], 2, EXPERTS), ALU.is_equal))
                    with nc.allow_low_precision(reason="zeros and ones"):
                        do(b, V_.tensor_reduce(chosen[:], onehot[:].rearrange("p k e -> p e k"), AX.X, ALU.add))
                    yield
                    dve.wait_ge(s_ex, n + 1)
                    do(b, V_.tensor_scalar(rc[:], ex[:], 1.0, None, ALU.add))
                    do(b, V_.reciprocal(rc[:], rc[:]))
                    dve.wait_ge(it, n)
                    do(b, V_.tensor_tensor(inter[:], rc[:, 0:INTER], pR[:, GATE:GATE1], ALU.mult))
                    do(b, V_.tensor_tensor(inter[:], inter[:], pR[:, UP:GATE], ALU.mult))
                    yield
                    dve.wait_ge(rank, n + 1)
                    do(b, V_.tensor_tensor(R[:], pC[:, 0:EXPERTS], carry, ALU.add))
                    do(b, V_.tensor_tensor(carry, pC[:, EXPERTS:2 * EXPERTS], carry, ALU.add), False)
                    do(b, V_.tensor_tensor(picked[:], onehot[:], bc(R[:], 1, TOPK), ALU.mult))
                    kept = lambda x: x[:, bass.ds(n * TOPK, TOPK)]
                    do(b, V_.tensor_reduce(posf[:], picked[:], AX.X, ALU.add))
                    V_.tensor_copy(kept(ranks), posf[:])
                    V_.tensor_copy(kept(experts), topf[:])
                    dve.wait_ge(listed[par], (n - par) * 8 * TOPK) if LATE[0] else None
                    V_.tensor_copy(tokc[:, par], tok[:, bass.ds(n, 1)])
                    do(b, V_.scalar_tensor_tensor(pos[:, par], topf[:], float(TOK), posf[:], ALU.mult, ALU.add))
                    V_.tensor_copy(mark[:], cst("lane")).then_inc(posr, 1)
                    dve.wait_ge(s_w8, n + 1)
                    do(b, V_.reciprocal(wsum[:, 1:2], wsum[:, 0:1]))
                    V_.tensor_scalar(kept(rw), kept(rw), wsum[:, 1:2], None, ALU.mult)
                    yield
                    dve.wait_ge(down, n + 1)
                    do(b, V_.scalar_tensor_tensor(y[:, bass.ds(n, 1)].rearrange("p o n -> p (o n)"), pD[:], rc[:, INTER:INTER + 1], h1[:, par],
                                                  ALU.mult, ALU.add))
                    assert b.n == PB, b.n
                    yield

                LATE = [False]

                def both(n, par, more):
                    f = first(n + 1, 1 - par) if more else iter([None] * 4)
                    s = second(n, par)
                    next(f)
                    next(s)
                    next(f)
                    next(s)
                    next(f)
                    next(s)
                    next(s)
                    next(f)

                for _ in first(0, 0):
                    pass
                both(0, 0, True)
                LATE[0] = True
                both(1, 1, True)
                with V_.Fori(1, TILES // 2 - 1) as i:
                    both(i * 2, 0, True)
                    both(i * 2 + 1, 1, True)
                both(TILES - 2, 0, True)
                both(TILES - 1, 1, False)

            @block.scalar
            def _(act):
                A_ = nc.scalar
                kept = lambda x, n: x[:, bass.ds(n * TOPK, TOPK)]

                def residual(n):
                    act.wait_ge(joined, n)
                    A_.activation(hs[:], hT[:, :, bass.ds(n * P, P)], ACT.Copy).then_inc(s_hs, 1)

                def z_evac(n):
                    act.wait_ge(zt, n + 1)
                    A_.activation(zT[:].rearrange("p j n -> p (j n)"), pZ[:], ACT.Copy).then_inc(zte, 1)

                def second_a(n):
                    act.wait_ge(h1t, n + 1)
                    A_.activation(h1T[:].rearrange("p j n -> p (j n)"), pX[:], ACT.Copy).then_inc(h1te, 1)

                def second_b(n):
                    act.wait_ge(joint, n + 1)
                    act.wait_ge(sB, n * PB + 6)
                    A_.activation(ex[:], pR[:, GATE:JOINT], ACT.Exp, scale=-1.0).then_inc(s_ex, 1)
                    A_.activation(kept(rw, n), top[:], ACT.Exp, bias=negtop[:], accum_out=wsum[:, 0:1]).then_inc(s_w8, 1)

                def second_c(n):
                    act.wait_ge(it, n + 1)
                    A_.activation(interT[:], pI[:, 0:P], ACT.Copy).then_inc(ite, 1)

                def both(n, more):
                    second_a(n)
                    if more:
                        residual(n + 1)
                    second_b(n)
                    second_c(n)
                    if more:
                        z_evac(n + 1)

                residual(0)
                z_evac(0)
                with A_.Fori(0, TILES - 1) as i:
                    both(i, True)
                both(TILES - 1, False)

            @block.tensor
            def _(pe):
                T_ = nc.tensor
                pe.wait_ge(setup, 3 + TILES)
                pe.wait_ge(loaded, LOADS)
                ident = cst("ident")

                def means(n, which):
                    pe.wait_ge(sA, n * PA + (2 if which == 0 else 5))
                    src = sta[:, 0:1] if which == 0 else sta[:, 4:5]
                    T_.matmul(pG[:, 0, which:which + 1], cst("group"), src, start=True, stop=True).then_inc(group, 1)

                def z_turn(n):
                    pe.wait_ge(sA, n * PA + 10)
                    pe.wait_ge(zte, n)
                    for j in range(FCH):
                        ins = T_.transpose(pZ[:, j * P:(j + 1) * P], z[:].rearrange("p a n -> p (a n)")[:, j * P:(j + 1) * P], ident)
                    ins.then_inc(zt, 1)

                def project(n):
                    pe.wait_ge(zte, n + 1)
                    pe.wait_ge(s_hs, n + 1)
                    pe.wait_ge(sA, n * PA)
                    for j in range(FCH):
                        T_.matmul(pA[:], zT[:, j], Wo[:, j], start=(j == 0), stop=False, skip_group_check=True)
                    for j in range(FCH):
                        ins = T_.matmul(pA[:, j * P:(j + 1) * P], hs[:, j], ident, start=False, stop=True, skip_group_check=True)
                    ins.then_inc(joined, 1)

                def h1_turn(n, par):
                    pe.wait_ge(h1_ready, n + 1)
                    pe.wait_ge(h1te, n)
                    for j in range(FCH):
                        ins = T_.transpose(pX[:, j * P:(j + 1) * P], h1[:, par, j * P:(j + 1) * P], ident)
                    ins.then_inc(h1t, 1)

                def joint_product(n):
                    pe.wait_ge(h1te, n + 1)
                    pe.wait_ge(sB, n * PB)
                    for j in range(FCH):
                        ins = T_.matmul(pR[:, 0:JOINT], h1T[:, j], Wj[:, j], start=(j == 0), stop=(j == FCH - 1))
                    ins.then_inc(joint, 1)

                def count(n):
                    pe.wait_ge(sB, n * PB + 6)
                    T_.matmul(pC[:, 0:EXPERTS], beforeb[:], chosen[:], start=True, stop=True)
                    T_.matmul(pC[:, EXPERTS:2 * EXPERTS], onesb[:], chosen[:], start=True, stop=True).then_inc(rank, 1)

                def shared(n):
                    pe.wait_ge(sB, n * PB + 10)
                    pe.wait_ge(ite, n)
                    T_.transpose(pI[:, 0:P], inter[:], ident).then_inc(it, 1)

                def shared_down(n):
                    pe.wait_ge(ite, n + 1)
                    T_.matmul(pD[:], interT[:], Wd[:], start=True, stop=True).then_inc(down, 1)

                def both(n, par, more):
                    h1_turn(n, par)
                    joint_product(n)
                    if more:
                        means(n + 1, 0)
                    count(n)
                    if more:
                        means(n + 1, 1)
                    shared(n)
                    if more:
                        z_turn(n + 1)
                    shared_down(n)
                    if more:
                        project(n + 1)

                means(0, 0)
                means(0, 1)
                z_turn(0)
                project(0)
                with T_.Fori(0, TILES // 2 - 1) as i:
                    both(i * 2, 0, True)
                    both(i * 2 + 1, 1, True)
                both(TILES - 2, 0, True)
                both(TILES - 1, 1, False)


def keeps(nc, ctx):
    sb = lambda n, s, dt=F32: ctx.enter_context(nc.sbuf_tensor("k_" + n, s, dt))
    return dict(rw=sb("rw", [P, TILES * TOPK])[:], ranks=sb("ranks", [P, 144])[:],
                experts=sb("experts", [P, 144])[:], slots=sb("slots", [P, 144])[:], counts=sb("counts", [P, EXPERTS])[:])



MAX_TILES = TOK * TOPK // P + EXPERTS
RING = 8
PAIRS = 144
WCOLS = FCH * 2 * INTER + LEN


def expert_phase(nc, keep, d, consts):
    NT = MAX_TILES
    with ExitStack() as ctx:
        sb = lambda n, s, dt=F32: ctx.enter_context(nc.sbuf_tensor("d_" + n, s, dt))
        sem = lambda n: ctx.enter_context(nc.semaphore("d_" + n))
        pb = lambda n, s: ctx.enter_context(nc.psum_tensor("d_" + n, s, F32))
        cst = lambda n: consts[:, CONST[n][0]:CONST[n][0] + CONST[n][1]]
        ident = cst("ident")
        more_than = sb("more_than", [P, EXPERTS, 16])
        nt, cum, first = sb("nt", [P, EXPERTS]), sb("cum", [P, 2, EXPERTS]), sb("first", [P, EXPERTS])
        behind = sb("behind", [P, 2, EXPERTS])
        et, bt, tt, rowf, rowi = (sb(n, [P, 2]) for n in ("et", "bt", "tt", "rowf", "rowi_f"))
        rowi = sb("rowi", [P, 2], I32)
        rows = sb("rows", [P, 2, P], I32)
        rowsf = sb("rowsf", [P, 2, P])
        idx = sb("idx", [P, 2 * P], I32)
        idxc = sb("idxc", [P, 2, RING], I32)
        erow = sb("erow", [1, 2 * P])
        turn = sb("turn", [1, 2, 2 * P])
        livef, live = sb("livef", [1, 2]), sb("live", [1, 1], I32)
        tab = sb("tab", [1, 3, 2 * P], I32)
        W = sb("W", [P, RING, WCOLS])
        X = sb("X", [P, RING, LEN])
        XT = sb("XT", [P, 2, LEN])
        ex, inter = sb("ex", [P, INTER]), sb("inter", [P, 2, INTER])
        interT = sb("interT", [P, 2, INTER])
        Y = sb("Y", [P, RING, LEN])
        oneh = sb("oneh", [P, 3, EXPERTS])
        base3 = sb("base3", [P, 3])
        pX, pG, pY = pb("pX", [P, 2, LEN]), pb("pG", [P, 2, LEN]), pb("pY", [P, 2, LEN])
        pI = pb("pI", [P, LEN])
        st_s = sem("setup")
        listg, turned, tabbed, ready = sem("list_rows"), sem("rows_turned"), sem("erow"), sem("tables")
        wl = [sem(f"weights{u}") for u in range(RING)]
        xl = [sem(f"gathered{u}") for u in range(RING)]
        yl = [sem(f"stored{u}") for u in range(RING)]
        xt, xte, gu, s_ex, s_r, s_in = sem("xt"), sem("xt_evac"), sem("gate_up"), sem("ex"), sem("rc"), sem("inter")
        it, ite, dn, yr = sem("it"), sem("it_evac"), sem("down"), sem("y_ready")
        idxs, passed, s_pos = sem("idx_copied"), sem("passed"), sem("positions")
        passed_sp = sem("passed_sync")
        PER = 16 // RING
        HALF = (RING - 1.0) / (2 * RING)
        SURE, TURNS = TOK * TOPK // P // RING, NT // RING

        def last_turn(engine):
            return engine.value_load(live[0:1, 0:1], min_val=SURE - 1, max_val=TURNS - 1)

        def walk(engine, four, end):
            with engine.Fori(1, SURE) as i:
                four(i)
            with engine.Fori(SURE, TURNS) as i:
                with engine.If(i < end + 1):
                    four(i)

        with nc.Block() as block:
            @block.vector
            def _(dve):
                V_ = nc.vector
                st = Steps(st_s)

                def do(ins, wait=True):
                    st.inc(ins)
                    if wait:
                        st.wait(dve)
                do(V_.tensor_tensor(more_than[:], bc(keep["counts"], 2, 16), bc(cst("tiles128"), 1, EXPERTS), ALU.is_gt))
                do(V_.tensor_reduce(nt[:], more_than[:], AX.X, ALU.add))
                do(V_.tensor_copy(cum[:, 0], nt[:]))
                a, s = 0, 1
                while s < EXPERTS:
                    do(V_.tensor_copy(cum[:, 1 - a, 0:s], cum[:, a, 0:s]), False)
                    do(V_.tensor_tensor(cum[:, 1 - a, s:], cum[:, a, s:], cum[:, a, 0:EXPERTS - s], ALU.add))
                    a, s = 1 - a, 2 * s
                incl = cum[:, a]
                do(V_.tensor_tensor(first[:], incl, nt[:], ALU.subtract))
                do(V_.tensor_scalar(first[:], first[:], float(P), None, ALU.mult))
                for g in range(2):
                    do(V_.tensor_scalar(tt[:, g:g + 1], cst("lane"), float(P * g), None, ALU.add))
                    do(V_.tensor_scalar(behind[:, g], incl, tt[:, g:g + 1], None, ALU.is_le))
                    do(V_.tensor_reduce(et[:, g:g + 1], behind[:, g], AX.X, ALU.add), False)
                    do(V_.tensor_tensor(behind[:, g], behind[:, g], nt[:], ALU.mult))
                    do(V_.tensor_reduce(bt[:, g:g + 1], behind[:, g], AX.X, ALU.add))
                do(V_.tensor_scalar(et[:], et[:], float(EXPERTS - 1), None, ALU.min))
                do(V_.tensor_tensor(tt[:], tt[:], bt[:], ALU.subtract))
                do(V_.scalar_tensor_tensor(rowf[:], et[:], 16.0, tt[:], ALU.mult, ALU.add))
                do(V_.tensor_scalar(rowi[:], rowf[:], float(EXPERTS * 16 - 1), None, ALU.min))
                assert st.n == ROWS, st.n
                for g in range(2):
                    dve.wait_ge(listg, 16 * (g + 1))
                    do(V_.tensor_copy(rowsf[:, g], rows[:, g]))
                assert st.n == ROWS + 2
                dve.wait_ge(turned, 2)
                do(V_.tensor_copy(idx[:], pX[:, 0, 0:2 * P]))
                do(V_.tensor_copy(erow[:], pG[0:1, 0, 0:2 * P]))
                do(V_.memset(turn[:, 0, 0:1], 1.0), False)
                do(V_.tensor_tensor(turn[:, 0, 1:], erow[:, 1:], erow[:, 0:2 * P - 1], ALU.not_equal))
                do(V_.tensor_copy(tab[:, 1], turn[:, 0]), False)
                do(V_.tensor_copy(tab[:, 0], erow[:]))
                a, s = 0, 1
                while s < 2 * P:
                    do(V_.tensor_copy(turn[:, 1 - a, 0:s], turn[:, a, 0:s]), False)
                    do(V_.tensor_tensor(turn[:, 1 - a, s:], turn[:, a, s:], turn[:, a, 0:2 * P - s], ALU.add))
                    a, s = 1 - a, 2 * s
                do(V_.tensor_scalar(livef[:, 0:1], incl[0:1, EXPERTS - 1:], 1.0 / RING, -1.0 / RING - HALF, ALU.mult, ALU.add))
                do(V_.tensor_scalar(livef[:, 1:2], livef[:, 0:1], ROUND, ROUND, ALU.add, ALU.subtract))
                do(V_.tensor_copy(live[:], livef[:, 1:2]))
                do(V_.tensor_scalar(turn[:, 1 - a], turn[:, a], 1.0 / RING, -HALF, ALU.mult, ALU.add))
                do(V_.tensor_scalar(turn[:, 1 - a], turn[:, 1 - a], ROUND, ROUND, ALU.add, ALU.subtract))
                do(V_.scalar_tensor_tensor(tab[:, 2], turn[:, 1 - a], -float(RING), turn[:, a], ALU.mult, ALU.add))
                V_.tensor_copy(tt[:, 0:1], tt[:, 1:2]).then_inc(ready, 1)

                def silu(t, u):
                    w = u % 2
                    dve.wait_ge(s_ex, t + 1)
                    if not (isinstance(t, int) and t < 2):
                        dve.wait_ge(it, t - 1)
                    V_.tensor_scalar(inter[:, w], ex[:], 1.0, None, ALU.add).then_inc(s_r, 1)
                    dve.wait_ge(s_r, t * 3 + 1)
                    V_.reciprocal(inter[:, w], inter[:, w]).then_inc(s_r, 1)
                    dve.wait_ge(s_r, t * 3 + 2)
                    V_.tensor_tensor(inter[:, w], inter[:, w], pG[:, w, 0:INTER], ALU.mult).then_inc(s_r, 1)
                    dve.wait_ge(s_r, t * 3 + 3)
                    V_.tensor_tensor(inter[:, w], inter[:, w], pG[:, w, INTER:2 * INTER], ALU.mult).then_inc(s_in, 1)

                def out(t, u, late=True):
                    dve.wait_ge(dn, t + (1 + RING))
                    if late:
                        dve.wait_ge(yl[u], (t - u) * PER)
                    V_.tensor_copy(Y[:, u], pY[:, u % 2]).then_inc(yr, 1)

                def place(i):
                    pairs = bass.ds(i * 3, 3)
                    V_.tensor_tensor(oneh[:], bc(cst("experts"), 1, 3), bc(keep["experts"][:, pairs], 2, EXPERTS), ALU.is_equal).then_inc(s_pos, 1)
                    dve.wait_ge(s_pos, i * 4 + 1)
                    V_.tensor_tensor(oneh[:], oneh[:], bc(first[:], 1, 3), ALU.mult).then_inc(s_pos, 1)
                    dve.wait_ge(s_pos, i * 4 + 2)
                    V_.tensor_reduce(base3[:], oneh[:], AX.X, ALU.add).then_inc(s_pos, 1)
                    dve.wait_ge(s_pos, i * 4 + 3)
                    V_.tensor_tensor(keep["slots"][:, pairs], keep["ranks"][:, pairs], base3[:], ALU.add).then_inc(s_pos, 1)

                def four(i, head=False):
                    for u in range(RING):
                        t = i * RING + u
                        silu(t, u)
                        if not (head and u < 2):
                            out(t - 2, (u - 2) % RING, late=not head)

                end = last_turn(dve)
                four(0, True)
                walk(V_, four, end)
                for u in (RING - 2, RING - 1):
                    out(end * RING + u, u)
                with V_.Fori(0, PAIRS // 3) as i:
                    place(i)

            @block.gpsimd
            def _(pool):
                G_ = nc.gpsimd
                pool.wait_ge(st_s, ROWS)
                rows_view = d["lists"].rearrange("(r n) a -> r (n a)", n=P)
                for g in range(2):
                    G_.indirect_dma_start(rows[:, g], None, rows_view,
                                          bass.IndirectOffsetOnAxis(ap=rowi[:, g:g + 1], axis=0)).then_inc(listg, 16)
                    pool.wait_ge(listg, 16 * (g + 1))
                pool.wait_ge(ready, 1)

                def four(i, par, head=False):
                    G_.tensor_copy(idxc[:, par], idx[:, bass.ds(i * RING, RING)]).then_inc(idxs, 1)
                    pool.wait_ge(idxs, i + 1)
                    pool.sem_inc(passed, 1)
                    for u in range(RING):
                        t = i * RING + u
                        if not head:
                            pool.wait_ge(xt, t - (RING - 1))
                            pool.sem_inc(passed, 1)
                        G_.indirect_dma_start(X[:, u], None, d["h1"],
                                              bass.IndirectOffsetOnAxis(ap=idxc[:, par, u:u + 1], axis=0)).then_inc(xl[u], 16)

                end = last_turn(pool)
                four(0, 0, True)
                four(1, 1)
                with G_.Fori(1, SURE // 2) as i:
                    four(i * 2, 0)
                    four(i * 2 + 1, 1)
                four(SURE, 0)
                with G_.Fori(SURE // 2, TURNS // 2) as i:
                    with G_.If(i * 2 < end + 1):
                        four(i * 2 + 1, 1)
                    with G_.If(i * 2 < end):
                        four(i * 2 + 2, 0)
                for u in range(RING):
                    pool.wait_ge(xl[u], end * 16 + 32)

            @block.sync
            def _(sp):
                sp.wait_ge(ready, 1)
                yv = d["slots"].rearrange("(t p) n -> p t n", p=P)

                def four(i, head=False):
                    for u in range(RING):
                        t = i * RING + u
                        e = sp.value_load(tab[0:1, 0, bass.ds(t, 1)], min_val=0, max_val=EXPERTS - 1)
                        new = sp.value_load(tab[0:1, 1, bass.ds(t, 1)], min_val=0, max_val=1)
                        at = sp.value_load(tab[0:1, 2, bass.ds(t, 1)], min_val=0, max_val=RING - 1)
                        if not head:
                            sp.wait_ge(dn, t + 1)
                        sp.dma_start(W[:, bass.ds(at, 1)].rearrange("p o n -> p (o n)"),
                                     d["w_experts"][bass.ds(e, 1)].rearrange("o p n -> p (o n)"), cond=new).then_inc(wl[u], 16)
                        if not head:
                            store(t - RING, u)

                def store(t, u):
                    sp.wait_ge(yr, t + 1)
                    sp.dma_start(yv[:, bass.ds(t, 1)].rearrange("p o n -> p (o n)"), Y[:, u]).then_inc(yl[u], 16)

                end = last_turn(sp)
                four(0, True)
                walk(nc.sync, four, end)
                for u in range(RING):
                    store(end * RING + u, u)
                for u in range(RING):
                    sp.wait_ge(yl[u], end * 16 + 16)
                    sp.sem_inc(passed_sp, 1)

            @block.scalar
            def _(act):
                A_ = nc.scalar

                def x_evac(t, u):
                    act.wait_ge(xt, t + 1)
                    A_.activation(XT[:, u % 2], pX[:, u % 2], ACT.Copy).then_inc(xte, 1)

                def exps(t, u):
                    act.wait_ge(gu, t + 1)
                    act.wait_ge(s_in, t)
                    A_.activation(ex[:], pG[:, u % 2, 0:INTER], ACT.Exp, scale=-1.0).then_inc(s_ex, 1)

                def i_evac(t, u):
                    act.wait_ge(it, t + 1)
                    A_.activation(interT[:, u % 2], pI[:, 0:P], ACT.Copy).then_inc(ite, 1)

                def four(i, head=False):
                    for u in range(RING):
                        t = i * RING + u
                        x_evac(t + 1, (u + 1) % RING)
                        exps(t, u)
                        if not (head and u == 0):
                            i_evac(t - 1, (u - 1) % RING)

                act.wait_ge(ready, 1)
                end = last_turn(act)
                x_evac(0, 0)
                four(0, head=True)
                walk(A_, four, end)
                i_evac(end * RING + (RING - 1), RING - 1)

            @block.tensor
            def _(pe):
                T_ = nc.tensor
                for g in range(2):
                    pe.wait_ge(st_s, ROWS + 1 + g)
                    T_.transpose(pX[:, 0, g * P:(g + 1) * P], rowsf[:, g], ident)
                    T_.matmul(pG[0:1, 0, g * P:(g + 1) * P], et[:, g:g + 1], ident, start=True, stop=True).then_inc(turned, 1)
                pe.wait_ge(ready, 1)
                pe.sem_inc(dn, RING)

                def x_turn(t, u):
                    pe.wait_ge(xl[u], ((t - u) * PER + 16))
                    if not (isinstance(t, int) and t < 2):
                        pe.wait_ge(xte, t - 1)
                    for j in range(FCH):
                        ins = T_.transpose(pX[:, u % 2, j * P:(j + 1) * P], X[:, u, j * P:(j + 1) * P], ident)
                    ins.then_inc(xt, 1)

                def gate_up(t, u, at):
                    pe.wait_ge(xte, t + 1)
                    pe.wait_ge(wl[u], (t - u) * PER + 16)
                    if not (isinstance(t, int) and t < 2):
                        pe.wait_ge(s_in, t - 1)
                    for j in range(FCH):
                        ins = T_.matmul(pG[:, u % 2, 0:2 * INTER], XT[:, u % 2, j * P:(j + 1) * P],
                                        W[:, bass.ds(at, 1), j * 2 * INTER:(j + 1) * 2 * INTER].rearrange("p o n -> p (o n)"),
                                        start=(j == 0), stop=(j == FCH - 1))
                    ins.then_inc(gu, 1)

                def i_turn(t, u):
                    pe.wait_ge(s_in, t + 1)
                    pe.wait_ge(ite, t)
                    T_.transpose(pI[:, 0:P], inter[:, u % 2], ident).then_inc(it, 1)

                def down(t, u, at):
                    pe.wait_ge(ite, t + 1)
                    if not (isinstance(t, int) and t < 2):
                        pe.wait_ge(yr, t - 1)
                    T_.matmul(pY[:, u % 2], interT[:, u % 2],
                              W[:, bass.ds(at, 1), FCH * 2 * INTER:WCOLS].rearrange("p o n -> p (o n)"), start=True, stop=True).then_inc(dn, 1)

                def place(t):
                    return pe.value_load(tab[0:1, 2, bass.ds(t, 1)], min_val=0, max_val=RING - 1)

                def four(i, head=False):
                    for u in range(RING):
                        t = i * RING + u
                        x_turn(t + 1, (u + 1) % RING)
                        gate_up(t, u, place(t))
                        if not (head and u < 2):
                            down(t - 2, (u - 2) % RING, place(t - 2))
                        if not (head and u == 0):
                            i_turn(t - 1, (u - 1) % RING)

                end = last_turn(pe)
                x_turn(0, 0)
                four(0, head=True)
                walk(T_, four, end)
                for u in (RING - 2, RING - 1):
                    t = end * RING + u
                    if u == RING - 1:
                        i_turn(t, u)
                    down(t, u, place(t))


ROWS = 3 + 12 + 2 + 10 + 4


def combine_phase(nc, y, keep, d, out, consts):
    with ExitStack() as ctx:
        sb = lambda n, s, dt=F32: ctx.enter_context(nc.sbuf_tensor("e_" + n, s, dt))
        sem = lambda n: ctx.enter_context(nc.semaphore("e_" + n))
        Gt = sb("G", [P, 2, TOPK, LEN])
        posi = sb("posi", [P, TILES * TOPK], I32)
        posc = sb("posc", [P, 2, TOPK], I32)
        rwc = sb("rwc", [P, 2, TOPK])
        acc = sb("acc", [P, 2, LEN])
        o = sb("o", [P, 2, LEN])
        bn, sta = sb("bn", [P, 6]), sb("sta", [P, 2, 6])
        s_posi, s_posc, passed, passed_v = sem("posi"), sem("posc"), sem("passed"), sem("passed_v")
        got = [sem(f"got{i}") for i in range(2 * TOPK)]
        sv, root, outr = sem("steps"), sem("root"), sem("out_ready")
        stored = [sem("stored0"), sem("stored1")]
        used = sem("used")
        PE_ = TOPK + 6
        with nc.Block() as block:
            @block.gpsimd
            def _(pool):
                G_ = nc.gpsimd
                pool.wait_ge(s_posi, 1)

                def tile(n, par, head):
                    if not head:
                        pool.wait_ge(used, n - 1)
                        pool.sem_inc(passed, 1)
                    G_.tensor_copy(posc[:, par], posi[:, bass.ds(n * TOPK, TOPK)]).then_inc(s_posc, 1)
                    pool.wait_ge(s_posc, n + 1)
                    pool.sem_inc(passed, 1)
                    for k in range(TOPK):
                        G_.indirect_dma_start(Gt[:, par, k], None, d["slots"],
                                              bass.IndirectOffsetOnAxis(ap=posc[:, par, k:k + 1], axis=0)).then_inc(got[par * TOPK + k], 16)
                tile(0, 0, True)
                tile(1, 1, True)
                with G_.Fori(1, TILES // 2) as i:
                    tile(i * 2, 0, False)
                    tile(i * 2 + 1, 1, False)

            @block.vector
            def _(dve):
                V_ = nc.vector
                V_.tensor_copy(posi[:], keep["slots"][:, 0:TILES * TOPK]).then_inc(s_posi, 1)
                st = Steps(sv)

                def do(ins, wait=True):
                    st.inc(ins)
                    if wait:
                        st.wait(dve)

                def tile(n, par, head):
                    st.start, st.n = n * PE_, 0
                    do(V_.tensor_copy(rwc[:, par], keep["rw"][:, bass.ds(n * TOPK, TOPK)]))
                    for k in range(TOPK):
                        dve.wait_ge(got[par * TOPK + k], (n - par) * 8 + 16)
                        before = y[:, bass.ds(n, 1)].rearrange("p o n -> p (o n)") if k == 0 else acc[:, par]
                        do(V_.scalar_tensor_tensor(acc[:, par], Gt[:, par, k], rwc[:, par, k:k + 1], before,
                                                   ALU.mult, ALU.add))
                    V_.tensor_copy(sta[:, par, 5:6], acc[:, par, 0:1]).then_inc(used, 1)
                    do(V_.bn_stats(bn[:], acc[:, par]))
                    dve.sem_inc(passed_v, 1)
                    do(V_.bn_aggr(sta[:, par, 0:2], bn[:]))
                    do(V_.tensor_scalar(sta[:, par, 2:3], sta[:, par, 1:2], EPS, None, ALU.add))
                    do(V_.reciprocal(sta[:, par, 3:4], sta[:, par, 2:3]))
                    dve.wait_ge(root, n + 1)
                    do(V_.scalar_tensor_tensor(sta[:, par, 5:6], sta[:, par, 0:1], -1.0, sta[:, par, 4:5], ALU.mult, ALU.mult), False)
                    assert st.n == PE_
                tile(0, 0, True)
                tile(1, 1, True)
                with V_.Fori(1, TILES // 2) as i:
                    tile(i * 2, 0, False)
                    tile(i * 2 + 1, 1, False)

            @block.scalar
            def _(act):
                def tile(n, par, head):
                    act.wait_ge(sv, n * PE_ + (TOPK + 5))
                    nc.scalar.activation(sta[:, par, 4:5], sta[:, par, 3:4], ACT.Sqrt).then_inc(root, 1)
                    act.wait_ge(sv, n * PE_ + PE_)
                    if not head:
                        act.wait_ge(stored[par], (n - par) * 8)
                    nc.scalar.activation(o[:, par], acc[:, par], ACT.Identity, bias=sta[:, par, 5:6], scale=sta[:, par, 4:5]).then_inc(outr, 1)
                tile(0, 0, True)
                tile(1, 1, True)
                with nc.scalar.Fori(1, TILES // 2) as i:
                    tile(i * 2, 0, False)
                    tile(i * 2 + 1, 1, False)

            @block.sync
            def _(sp):
                ov = out.rearrange("b (u p) n -> p (b u) n", p=P)
                with nc.sync.Fori(0, TILES // 2) as i:
                    for par in range(2):
                        n = i * 2 + par
                        sp.wait_ge(outr, n + 1)
                        sp.dma_start(ov[:, bass.ds(n, 1)].rearrange("p o n -> p (o n)"), o[:, par]).then_inc(stored[par], 16)
                for par in range(2):
                    sp.wait_ge(stored[par], 16 * TILES // 2)


def build(nc, d, out):
    with ExitStack() as ctx:
        consts_sb = ctx.enter_context(nc.sbuf_tensor("consts_sb", [P, d["consts"].shape[1]], F32))
        keep = keeps(nc, ctx)
        d["lists"] = nc.dram_tensor("lists", (EXPERTS * TOK, 1), I32, kind="Internal").ap()
        d["h1"] = nc.dram_tensor("h1", (TOK, LEN), F32, kind="Internal").ap()
        d["slots"] = nc.dram_tensor("slots", (MAX_TILES * P, LEN), F32, kind="Internal").ap()
        consts_loaded = ctx.enter_context(nc.semaphore("consts_loaded"))
        with nc.Block() as block:
            @block.sync
            def _(sp):
                sp.dma_start(consts_sb[:], d["consts"]).then_inc(consts_loaded, 16)
                sp.wait_ge(consts_loaded, 16)
        hT = ctx.enter_context(nc.sbuf_tensor("hT", [P, FCH, TOK], F32))
        tok_phase(nc, d["c"], d["log_dt"], d["log_w_real"], d["w_imag"], consts_sb, hT)
        y = ctx.enter_context(nc.sbuf_tensor("y", [P, TILES, LEN], F32))
        attention_phase(nc, hT, y, d["w_qkv"], [d["lq1"], d["lq2"], d["lk1"], d["lk2"]], consts_sb)
        mix_phase(nc, hT, y, keep, d, consts_sb)
        expert_phase(nc, keep, d, consts_sb)
        combine_phase(nc, y, keep, d, out, consts_sb)


def kernel(x, L0_tok_log_dt, L0_tok_log_w_real, L0_tok_w_imag, L0_attn_w_qkv, L0_attn_wo, L0_attn_lambda_q1,
           L0_attn_lambda_q2, L0_attn_lambda_k1, L0_attn_lambda_k2, L0_attn_gamma, L0_attn_beta, L0_ffn_gate_w,
           L0_ffn_gu_w, L0_ffn_dp_w, L0_ffn_sh_gate_w, L0_ffn_sh_up_w, L0_ffn_sh_down_w, L0_ffn_sh_gate1_w):
    import numpy as _np
    import concourse.bacc as _bacc
    from concourse import mybir as _mybir
    from concourse.bass_utils import run_bass_kernel_spmd as _run

    lay = _np.ascontiguousarray
    gu = _np.asarray(L0_ffn_gu_w).transpose(0, 2, 1).reshape(EXPERTS, FCH, P, 2 * INTER).transpose(0, 2, 1, 3)
    w_experts = _np.concatenate([gu.reshape(EXPERTS, P, FCH * 2 * INTER), _np.asarray(L0_ffn_dp_w).transpose(0, 2, 1)], 2)
    w_joint = _np.concatenate([_np.asarray(a) for a in (L0_ffn_gate_w, L0_ffn_sh_up_w, L0_ffn_sh_gate_w, L0_ffn_sh_gate1_w)], 0).T
    arrays = {
        "c": _np.asarray(x).transpose(3, 2, 1, 0), "log_dt": L0_tok_log_dt,
        "log_w_real": _np.asarray(L0_tok_log_w_real).T, "w_imag": _np.asarray(L0_tok_w_imag).T,
        "w_qkv": _np.asarray(L0_attn_w_qkv).T, "wo": _np.asarray(L0_attn_wo).T,
        "lq1": L0_attn_lambda_q1, "lq2": L0_attn_lambda_q2, "lk1": L0_attn_lambda_k1, "lk2": L0_attn_lambda_k2,
        "gamma": L0_attn_gamma, "beta": L0_attn_beta, "w_joint": w_joint, "sh_down": _np.asarray(L0_ffn_sh_down_w).T,
        "w_experts": w_experts, "consts": const_table(),
    }
    arrays = {"in_" + n: lay(_np.asarray(a)) for n, a in arrays.items()}
    nc = _bacc.Bacc("TRN2", target_bir_lowering=False, num_devices=1)
    d = {n[3:]: nc.dram_tensor(n, a.shape, _mybir.dt.from_np(a.dtype), kind="ExternalInput").ap() for n, a in arrays.items()}
    out = nc.dram_tensor("out", (BATCH, SEQ, LEN), _mybir.dt.float32, kind="ExternalOutput").ap()
    build(nc, d, out)
    r = _run(nc, [arrays], core_ids=[0])
    return r.results[0]["out"]
```

```python
import concourse.bass as bass
from concourse import mybir
from contextlib import ExitStack
import math
import numpy as np

F32 = mybir.dt.float32
F32R = mybir.dt.float32r
BF16 = mybir.dt.bfloat16
I32 = mybir.dt.int32
U32 = mybir.dt.uint32
ACT = mybir.ActivationFunctionType
ALU = mybir.AluOpType
AX = mybir.AxisListType

P = 128
BATCH, SEQ, MODES, LEN = 8, 256, 64, 512
TOK = BATCH * SEQ
TILES = TOK // P
FCH = LEN // P
FINE = 64
COARSE = LEN // FINE
ROUND = 1.5 * 2.0 ** 23
TURN = 6.2831845
INV_TURN = 1.0 / (2.0 * math.pi)

CONST = {}


def const_table():
    parts = {}
    p = np.arange(P)
    parts["ident"] = np.eye(P)
    parts["before"] = (p[:, None] < p[None, :]) * 1.0
    parts["ones"] = np.ones((P, P))
    parts["group"] = (p[:, None] // 16 == p[None, :] // 16) * (1.0 / 16)
    inv = np.float32(1.0) / np.power(np.float32(10000.0), np.arange(0, 32, 2, dtype=np.float32) / np.float32(32))
    ang = np.arange(SEQ, dtype=np.float32)[:, None] * inv[None, :].astype(np.float32)
    cos, sin = np.cos(ang), np.sin(ang)
    scaler = np.float32(32) ** np.float32(-0.5)
    for name, f in (("q", scaler), ("k", np.float32(1))):
        c = np.concatenate([cos, cos], 1) * f
        s = np.concatenate([-sin, sin], 1) * f
        for u in range(2):
            parts[f"cos_{name}{u}"] = c[u * P:(u + 1) * P]
            parts[f"sin_{name}{u}"] = s[u * P:(u + 1) * P]
    row = lambda v: np.broadcast_to(np.asarray(v, np.float64), (P, len(v)))
    parts["fine"] = row(np.arange(FINE))
    parts["coarse"] = row(np.arange(COARSE) * FINE)
    parts["experts"] = row(np.arange(64))
    parts["tiles128"] = row(np.arange(16) * 128)
    half = (p >= 64) * 1.0
    parts["phase_v"] = (0.25 - 0.25 * half)[:, None]
    parts["phase_a"] = (0.25 + 0.25 * half)[:, None]
    parts["phase_b"] = (0.50 + 0.25 * half)[:, None]
    parts["minus_half"] = np.full((P, 1), -0.5)
    parts["eps"] = np.full((P, 1), 1e-5)
    parts["lane"] = p[:, None] * 1.0
    at = 0
    for name, a in parts.items():
        CONST[name] = (at, a.shape[1])
        at += a.shape[1]
    return np.ascontiguousarray(np.concatenate(list(parts.values()), 1).astype(np.float32))


class Steps:

    def __init__(self, sem):
        self.sem, self.start, self.n = sem, 0, 0

    def inc(self, ins):
        ins.then_inc(self.sem, 1)
        self.n += 1
        return self.n

    def wait(self, engine, n=None):
        engine.wait_ge(self.sem, self.start + (self.n if n is None else n))


def bc(ap, axis, n):
    a = ap.unsqueeze(axis)
    shape = list(a.shape)
    shape[axis] = n
    return a.to_broadcast(shape)


def tok_phase(nc, w_qkv, wq, wq_loaded, c_in, log_dt, lwr, wim, consts_in, consts, hT):
    HB = 16
    NB = SEQ // HB
    with ExitStack() as ctx:
        sb = lambda n, s, d=F32: ctx.enter_context(nc.sbuf_tensor("a_" + n, s, d))
        sem = lambda n: ctx.enter_context(nc.semaphore("a_" + n))
        C = sb("C", [P, 2, SEQ, BATCH])
        ldt, lw, wi = sb("ldt", [P, SEQ]), sb("lw", [P, SEQ]), sb("wi", [P, SEQ])
        sm = sb("small", [P, 14, SEQ])
        dt, ew, dr, di, ti, e, th, rs, rc, s_, c_, qr, qi, tmp = [sm[:, i, :] for i in range(14)]
        tmpb, w2, wi2, er, ei = ldt[:], lw[:], tmp, th, dt
        U = sb("U", [P, 4, SEQ, COARSE])
        mag, ta, tb, work = [U[:, i] for i in range(4)]
        A, B = sb("A", [P, SEQ, COARSE]), sb("B", [P, SEQ, COARSE])
        EV = sb("EV", [P, SEQ, FINE])
        tT, t2, kk, V = [U[:, i].rearrange("p (t h x) a -> p t h (x a)", t=2, h=HB) for i in range(4)]
        G = sb("G", [P, 2, HB, COARSE, BATCH])
        G2 = sb("G2", [P, 2, HB, COARSE, BATCH])
        ps = ctx.enter_context(nc.psum_tensor("a_ps", [P, 2, HB, FCH, BATCH], F32))
        loaded, c_loaded = sem("loaded"), sem("c_loaded")
        dve_s, act_s, pool_s = sem("dve"), sem("act"), sem("pool")
        angle, phased, rounded, residue, sine = sem("angle"), sem("phased"), sem("rounded"), sem("residue"), sem("sine")
        v_ready, g2_ready, g_ready, products, evac = sem("v"), sem("g2"), sem("g"), sem("products"), sem("evac")
        exps_in, exps = sem("exps_in"), sem("exps")
        g1_free, b_steps = sem("g1"), sem("coarse_b")
        cst = lambda n: consts[:, CONST[n][0]:CONST[n][0] + CONST[n][1]]
        EB = 32
        with nc.Block() as block:
            @block.sync
            def _(sp):
                sp.dma_start(ldt[:], log_dt.partition_broadcast(P)).then_inc(loaded, 16)
                halves = (slice(0, P // 2), slice(P // 2, P))
                for half in halves:
                    sp.dma_start(lw[half, :], lwr).then_inc(loaded, 16)
                    sp.dma_start(wi[half, :], wim).then_inc(loaded, 16)
                sp.dma_start(consts[:], consts_in).then_inc(loaded, 16)
                for half in halves:
                    for r in range(2):
                        sp.dma_start(C[half, r], c_in[r]).then_inc(c_loaded, 16)
                loads_weights(sp, w_qkv, wq, 0).then_inc(wq_loaded, 16)

            @block.gpsimd
            def _(pool):
                pool.wait_ge(dve_s, 3)
                for i in range(SEQ // EB):
                    hs = slice(i * EB, (i + 1) * EB)
                    nc.gpsimd.tensor_tensor(EV[:, hs], bc(dr[:, hs], 2, FINE), bc(cst("fine"), 1, EB), ALU.mult).then_inc(exps_in, 1)
                bt = G2[:].rearrange("p t h a c -> p (t h a c)").rearrange("p (s a) -> p s a", a=COARSE)
                pool.wait_ge(dve_s, SCALED)
                nc.gpsimd.tensor_tensor(B[:], tb, bc(qr, 2, COARSE), ALU.mult).then_inc(b_steps, 1)
                nc.gpsimd.tensor_tensor(bt, ta, bc(qi, 2, COARSE), ALU.mult).then_inc(b_steps, 1)
                pool.wait_ge(b_steps, 2)
                nc.gpsimd.tensor_tensor(B[:], B[:], bt, ALU.subtract).then_inc(b_steps, 1)
                pool.wait_ge(b_steps, 3)
                pool.wait_ge(c_loaded, 64)
                pool.wait_ge(dve_s, TABLES)
                with nc.gpsimd.Fori(0, NB // 2) as i:
                    for par in range(2):
                        n = i * 2 + par
                        hs = bass.ds(n * HB, HB)
                        pool.wait_ge(phased, n + 1)
                        nc.gpsimd.tensor_tensor(tT[:, par], bc(di[:, hs], 2, FINE), bc(cst("fine"), 1, HB), ALU.mult).then_inc(angle, 1)
                        pool.wait_ge(g_ready, n + 1)
                        nc.gpsimd.tensor_tensor(G2[:, par], bc(C[:, 1, hs], 2, COARSE), bc(B[:, hs], 3, BATCH), ALU.mult).then_inc(g2_ready, 1)

            @block.vector
            def _(dve):
                st = Steps(dve_s)
                V_ = nc.vector

                def do(ins, wait=True):
                    st.inc(ins)
                    if wait:
                        st.wait(dve)

                dve.wait_ge(act_s, 2)
                do(V_.tensor_tensor(dr, ew, dt, ALU.mult), False)
                do(V_.tensor_tensor(di, wi[:], dt, ALU.mult))
                do(V_.tensor_scalar(di, di, INV_TURN, None, ALU.mult))
                do(V_.tensor_tensor(mag, bc(dr, 2, COARSE), bc(cst("coarse"), 1, SEQ), ALU.mult))
                do(V_.tensor_tensor(ta, bc(di, 2, COARSE), bc(cst("coarse"), 1, SEQ), ALU.mult))
                do(V_.tensor_scalar(ti, di, 0.5, None, ALU.mult))
                do(V_.tensor_scalar(tmp, ti, ROUND, ROUND, ALU.add, ALU.subtract))
                do(V_.tensor_tensor(rs, tmp, ti, ALU.subtract))
                do(V_.tensor_scalar(ti, ti, 0.25, None, ALU.add))
                do(V_.tensor_scalar(tmp, ti, ROUND, ROUND, ALU.add, ALU.subtract))
                do(V_.tensor_tensor(rc, tmp, ti, ALU.subtract))
                do(V_.tensor_scalar(tb, ta, cst("phase_b"), None, ALU.add))
                do(V_.tensor_scalar(ta, ta, cst("phase_a"), None, ALU.add))
                do(V_.tensor_scalar(work, ta, ROUND, ROUND, ALU.add, ALU.subtract))
                do(V_.tensor_tensor(ta, work, ta, ALU.subtract))
                do(V_.tensor_scalar(work, tb, ROUND, ROUND, ALU.add, ALU.subtract))
                do(V_.tensor_tensor(tb, work, tb, ALU.subtract))
                assert st.n == ANGLES
                do(V_.tensor_tensor(w2, ew, ew, ALU.mult), False)
                do(V_.tensor_tensor(wi2, wi[:], wi[:], ALU.mult))
                do(V_.tensor_tensor(w2, w2, wi2, ALU.add))
                do(V_.reciprocal(w2, w2))
                dve.wait_ge(act_s, 2 + 3)
                do(V_.scalar_tensor_tensor(th, e, 1.0, th, ALU.add, ALU.mult))
                dve.wait_ge(act_s, 2 + 3 + 2)
                do(V_.tensor_tensor(tmp, s_, s_, ALU.mult), False)
                do(V_.tensor_tensor(tmpb, s_, c_, ALU.mult))
                do(V_.scalar_tensor_tensor(tmp, tmp, -2.0, e, ALU.mult, ALU.mult), False)
                do(V_.scalar_tensor_tensor(ei, tmpb, 2.0, e, ALU.mult, ALU.mult))
                do(V_.tensor_tensor(er, th, tmp, ALU.add))
                do(V_.tensor_tensor(qr, ei, wi[:], ALU.mult), False)
                do(V_.tensor_tensor(tmpb, er, ew, ALU.mult))
                do(V_.tensor_tensor(qr, qr, tmpb, ALU.subtract))
                do(V_.tensor_tensor(qr, qr, w2, ALU.mult))
                do(V_.tensor_tensor(qi, er, wi[:], ALU.mult), False)
                do(V_.tensor_tensor(tmpb, ei, ew, ALU.mult))
                do(V_.tensor_tensor(qi, qi, tmpb, ALU.add))
                do(V_.scalar_tensor_tensor(qi, qi, -1.0, w2, ALU.mult, ALU.mult))
                dve.wait_ge(act_s, 2 + 3 + 2 + 2)
                do(V_.tensor_tensor(ta, ta, mag, ALU.mult), False)
                do(V_.tensor_tensor(tb, tb, mag, ALU.mult))
                assert st.n == SCALED, st.n
                do(V_.tensor_tensor(A[:], ta, bc(qr, 2, COARSE), ALU.mult), False)
                do(V_.tensor_tensor(work, tb, bc(qi, 2, COARSE), ALU.mult))
                do(V_.tensor_tensor(A[:], A[:], work, ALU.add))
                assert st.n == TABLES, st.n
                dve.wait_ge(c_loaded, 64)
                V_.tensor_copy(tmp, tmp).then_inc(g_ready, 1)
                V_.tensor_copy(tmpb, tmpb).then_inc(v_ready, 1)
                dve.wait_ge(exps, SEQ // EB)
                with V_.Fori(0, NB // 2) as i:
                    for par in range(2):
                        n = i * 2 + par
                        hs = bass.ds(n * HB, HB)
                        dve.wait_ge(rounded, n + 1)
                        V_.scalar_tensor_tensor(kk[:, par], kk[:, par], ROUND, t2[:, par], ALU.subtract, ALU.subtract).then_inc(residue, 1)
                        dve.wait_ge(products, n)
                        V_.tensor_tensor(G[:, par], bc(C[:, 0, hs], 2, COARSE), bc(A[:, hs], 3, BATCH), ALU.mult).then_inc(g1_free, 1)
                        dve.wait_ge(g1_free, n + 1)
                        dve.wait_ge(g2_ready, n + 1)
                        V_.tensor_tensor(G[:, par], G[:, par], G2[:, par], ALU.add).then_inc(g_ready, 1)
                        dve.wait_ge(sine, n + 1)
                        V_.tensor_tensor(V[:, par], kk[:, par], EV[:, hs], ALU.mult).then_inc(v_ready, 1)

            @block.scalar
            def _(act):
                A_ = nc.scalar
                act.wait_ge(loaded, 16 * 6)
                A_.activation(dt, ldt[:], ACT.Exp).then_inc(act_s, 1)
                A_.activation(ew, lw[:], ACT.Exp).then_inc(act_s, 1)
                act.wait_ge(dve_s, 1)
                A_.activation(e, dr, ACT.Exp, scale=-1.0).then_inc(act_s, 1)
                A_.activation(th, dr, ACT.Tanh, scale=-0.5).then_inc(act_s, 1)
                act.wait_ge(dve_s, 4)
                A_.activation(mag, mag, ACT.Exp, scale=-1.0).then_inc(act_s, 1)

                def magnitudes(i):
                    act.wait_ge(exps_in, i + 1)
                    A_.activation(EV[:, i * EB:(i + 1) * EB], EV[:, i * EB:(i + 1) * EB], ACT.Exp, scale=-1.0).then_inc(exps, 1)

                before = SEQ // EB // 2
                for i in range(before):
                    magnitudes(i)
                act.wait_ge(dve_s, ANGLES)
                A_.activation(s_, rs, ACT.Sin, scale=-TURN).then_inc(act_s, 1)
                A_.activation(c_, rc, ACT.Sin, scale=-TURN).then_inc(act_s, 1)
                A_.activation(ta, ta, ACT.Sin, scale=-TURN).then_inc(act_s, 1)
                A_.activation(tb, tb, ACT.Sin, scale=-TURN).then_inc(act_s, 1)
                for i in range(before, SEQ // EB):
                    magnitudes(i)
                A_.copy(rs, rs).then_inc(phased, 1)

                def sines(n, par):
                    act.wait_ge(angle, n + 1)
                    A_.activation(t2[:, par], tT[:, par], ACT.Identity, bias=cst("phase_v")).then_inc(phased, 1)
                    act.wait_ge(phased, n + 2)
                    act.wait_ge(v_ready, n)
                    A_.activation(kk[:, par], t2[:, par], ACT.Copy, bias=ROUND).then_inc(rounded, 1)
                    act.wait_ge(residue, n + 1)
                    A_.activation(kk[:, par], kk[:, par], ACT.Sin, scale=-TURN).then_inc(sine, 1)

                def evacuate(n, par):
                    act.wait_ge(products, n + 2)
                    out = hT[:].rearrange("p j (c s) -> p j c s", c=BATCH)[:, :, :, bass.ds(n * HB, HB)]
                    A_.activation(out, ps[:, par].rearrange("p h j c -> p j c h"), ACT.Copy, scale=2.0).then_inc(evac, 1)

                sines(0, 0)
                with A_.Fori(0, NB // 2 - 1) as i:
                    for par in range(2):
                        sines(i * 2 + par + 1, 1 - par)
                        evacuate(i * 2 + par, par)
                sines(NB - 1, 1)
                evacuate(NB - 2, 0)
                evacuate(NB - 1, 1)

            @block.tensor
            def _(pe):
                pe.sem_inc(products, 1)
                pe.sem_inc(evac, 1)
                with nc.tensor.Fori(0, NB // 2) as i:
                    for par in range(2):
                        n = i * 2 + par
                        pe.wait_ge(g_ready, n + 2)
                        pe.wait_ge(v_ready, n + 2)
                        pe.wait_ge(evac, n)
                        for h in range(HB):
                            for odd in range(2):
                                ins = nc.tensor.matmul(ps[64 * odd:64 * odd + 64, par, h], V[:, par, h],
                                                       G[:, par, h].rearrange("p (j o) c -> p o j c", o=2)[:, odd],
                                                       start=True, stop=True)
                        ins.then_inc(products, 1)


ANGLES, SCALED, TABLES = 17, 37, 40



HEADS, HD = 16, 32
INIT_LAMBDA = 0.8


def attention_phase(nc, hT, y, wq, wq_loaded, w_qkv, lambdas, consts):
    UN = 2 * HEADS
    with ExitStack() as ctx:
        sb = lambda n, s, d=F32: ctx.enter_context(nc.sbuf_tensor("b_" + n, s, d))
        sem = lambda n: ctx.enter_context(nc.semaphore("b_" + n))
        pb = lambda n, s: ctx.enter_context(nc.psum_tensor("b_" + n, s, F32))
        cst = lambda n: consts[:, CONST[n][0]:CONST[n][0] + CONST[n][1]]
        W = [wq, sb("wk", [P, FCH, LEN]), sb("wv", [P, FCH, LEN])]
        hc = sb("hc", [P, FCH, SEQ])
        mulc, muls = sb("mulc", [P, LEN]), sb("muls", [P, LEN])
        xr = sb("xr", [P, 2, LEN])
        stack = sb("stack", [P, UN, 4, 16], F32R)
        qk = [sb(f"qk{i}", [P, 2, HEADS, SEQ], F32R) for i in range(2)]
        Vb = sb("Vb", [P, 2, 2, LEN])
        E = sb("E", [P, 2, 2, 2, SEQ])
        D = sb("D", [P, 2, 2, SEQ])
        DT = sb("DT", [P, 2, 2, 2, P])
        negmax, sums, mixw = sb("negmax", [P, 2, 2, 2]), sb("sums", [P, 2, 2, 2]), sb("mixw", [P, 2, 2])
        recips = sb("recips", [P, 2, HEADS, 2])
        maskb, identb = sb("maskb", [P, SEQ], BF16), sb("identb", [P, P], BF16)
        identr = sb("identr", [P, P], F32R)
        lam = sb("lam", [P, 4, HD])
        lamw = sb("lamw", [P, 2, HD])
        lams = sb("lams", [P, 4])
        pq = pb("pq", [P, LEN])
        pS = pb("pS", [P, 2, 2, 2, SEQ])
        pT = pb("pT", [P, 2, 2, P])
        pK = ctx.enter_context(nc.psum_tensor("b_pK", [P, 4, P], F32R))
        pO = pb("pO", [P, LEN])

        wkv_loaded, lam_loaded, setup = [sem("wk_loaded"), sem("wv_loaded")], sem("lam_loaded"), sem("setup")
        s_hc, s_qkv, s_rm, s_xr, s_hi, s_lo = (sem(n) for n in ("hc", "qkv", "rope_mul", "roped", "hi", "lo"))
        s_qkb, s_qke, s_v = sem("qk_transposed"), sem("qk_evac"), sem("v_evac")
        s_scores, s_max, s_exp, s_small, s_d = (sem(n) for n in ("scores", "max", "exp", "small", "mixed"))
        s_t, s_dt, s_pv, s_y = (sem(n) for n in ("mixed_t", "mixed_t_evac", "pv", "y"))


        def first_bank(t, x):
            return pO[:] if (t, x) == (1, 2) else pq[:] if x == 2 else pS[:, t, x].rearrange("p s n -> p (s n)")

        def walk(engine, slot):
            for j in range(LAG):
                slot(0, 0, j)
            with engine.Fori(0, BATCH // 2 - 1) as i:
                for j in range(LAG, PAIRS_):
                    slot(i * 2, 0, j)
                for j in range(PAIRS_):
                    slot(i * 2 + 1, 1, j)
                for j in range(LAG):
                    slot(i * 2 + 2, 0, j)
            for j in range(LAG, PAIRS_):
                slot(BATCH - 2, 0, j)
            for j in range(PAIRS_ + LAG):
                slot(BATCH - 1, 1, j)

        def behind(c, par, j, lag):
            j -= lag
            if j < 0:
                if isinstance(c, int) and c == 0:
                    return None
                c, par, j = c - 1, 1 - par, j + PAIRS_
            return (c, par, j, c * PAIRS_ + j) if j < PAIRS_ else None

        def pieces(table, c, j):
            more = j < PAIRS_ and not (isinstance(c, int) and c == BATCH - 1)
            return [table.get((j, place), ()) if more else () for place in (START, MID, END)]

        with nc.Block() as block:
            @block.sync
            def _(sp):
                for x in (1, 2):
                    load = loads_weights(sp, w_qkv, W[x], x)
                    load.then_inc(wkv_loaded[x - 1], 16)
                    if x == 1:
                        for i, l in enumerate(lambdas):
                            sp.dma_start(lam[:, i, :], l.partition_broadcast(P)).then_inc(lam_loaded, 16)

            @block.gpsimd
            def _(pool):
                def prepare(b, t):
                    for x in range(2):
                        r = b * 4 + (2 * t + x)
                        pool.wait_ge(s_rm, r + 1)
                        nc.gpsimd.tensor_tensor(xr[:, x], mulc[:], muls[:], ALU.add).then_inc(s_xr, 1)
                        pool.wait_ge(s_hi, r + 1)
                        src = xr[:, x].rearrange("p (m d) -> p m d", d=16)
                        for half in range(2):
                            ms = slice(half * HEADS, (half + 1) * HEADS)
                            if x == 0:
                                out = stack[:].rearrange("p m (a r) d -> p m a r d", r=2)[:, ms, :, 1]
                            else:
                                out = stack[:, ms, 2:4]
                            nc.gpsimd.tensor_tensor(out, bc(src[:, ms], 2, 2), bc(stack[:, ms, 0].bitcast(F32), 2, 2),
                                                    ALU.subtract).then_inc(s_lo, 1)

                prepare(0, 0)
                prepare(0, 1)
                with nc.gpsimd.Fori(1, BATCH) as b:
                    prepare(b, 0)
                    prepare(b, 1)

            @block.vector
            def _(dve):
                V_ = nc.vector
                V_.tensor_copy(maskb[:, 0:P], cst("before")).then_inc(setup, 1)
                V_.tensor_copy(maskb[:, P:SEQ], cst("ones")).then_inc(setup, 1)
                V_.tensor_copy(identb[:], cst("ident")).then_inc(setup, 1)
                V_.tensor_copy(identr[:], cst("ident")).then_inc(setup, 1)
                dve.wait_ge(lam_loaded, 64)
                V_.tensor_tensor(lamw[:], lam[:, 0:2], lam[:, 2:4], ALU.mult).then_inc(setup, 1)
                dve.wait_ge(setup, 5)
                V_.reduce_sum(lams[:, 0:2], lamw[:], AX.X).then_inc(setup, 1)
                dve.wait_ge(setup, 7)
                V_.tensor_tensor(lams[:, 2:3], lams[:, 1:2], lams[:, 0:1], ALU.subtract).then_inc(setup, 1)
                dve.wait_ge(setup, 8)
                V_.tensor_scalar(lams[:, 3:4], lams[:, 2:3], -INIT_LAMBDA, None, ALU.add).then_inc(setup, 1)
                dve.wait_ge(setup, 9)
                dve.sem_inc(s_d, 4)

                def rope(b, t, x, bank=None):
                    r = b * 4 + (2 * t + x)
                    name = "qk"[x]
                    dve.wait_ge(s_qkv, b * 6 + (3 * t + x + 1) if bank is None else AHEAD.index((t, x)) + 1)
                    dve.wait_ge(s_xr, r)
                    src = (pq[:] if bank is None else bank).rearrange("p (h s d) -> p s h d", s=2, d=16)
                    cos = cst(f"cos_{name}{t}")[:, 0:16]
                    sin = cst(f"sin_{name}{t}")
                    V_.tensor_tensor(mulc[:].rearrange("p (s h d) -> p s h d", s=2, d=16), src,
                                     bc(bc(cos, 1, HEADS), 1, 2), ALU.mult)
                    ms = muls[:].rearrange("p (s h d) -> p s h d", s=2, d=16)
                    V_.tensor_tensor(ms[:, 0], src[:, 1], bc(sin[:, 0:16], 1, HEADS), ALU.mult)
                    V_.tensor_tensor(ms[:, 1], src[:, 0], bc(sin[:, 16:32], 1, HEADS), ALU.mult).then_inc(s_rm, 1)

                def evac(b, t, x, i, par):
                    w = b * 16 + (8 * t + 4 * x + i)
                    dve.wait_ge(s_qkb, w + 1)
                    V_.tensor_copy(qk[par][:, x, 4 * i:4 * i + 4, t * P:(t + 1) * P], pK[:]).then_inc(s_qke, 1)

                def negmax_of(m, j, g):
                    dve.wait_ge(s_scores, m * 2 + (g + 1))
                    V_.tensor_reduce(negmax[:, j % 2, g], pS[:, j % 2, g], AX.X, ALU.max, negate=True).then_inc(s_max, 1)

                def slot(c, par, j):
                    now, last = behind(c, par, j, 0), behind(c, par, j, 1)
                    begin, mid, _ = pieces(DVE_PIECES, c, j)

                    def piece(p):
                        rope(c + 1, *p[1:]) if p[0] == "rope" else evac(c + 1, *p[1:], 1 - par)
                    for p in begin:
                        piece(p)
                    if now:
                        negmax_of(now[3], j, 0)
                    if last:
                        _, _, jl, ml = last
                        u, h = divmod(2 * jl, HEADS)
                        l2 = jl % 2
                        dve.wait_ge(s_exp, ml * 2 + 6)
                        V_.reciprocal(recips[:, u, h:h + 2], sums[:, l2]).then_inc(s_small, 1)
                    if now:
                        negmax_of(now[3], j, 1)
                    for p in mid:
                        piece(p)
                    if last:
                        dve.wait_ge(s_small, ml * 2 + 1)
                        V_.scalar_tensor_tensor(mixw[:, l2], sums[:, l2, :, 0], lams[:, 3:4], recips[:, u, h:h + 2, 1],
                                                ALU.mult, ALU.mult).then_inc(s_small, 1)
                        dve.wait_ge(s_small, ml * 2 + 2)
                        dve.wait_ge(s_t, ml + 1)
                        for g in range(2):
                            V_.scalar_tensor_tensor(D[:, l2, g], E[:, l2, g, 1], mixw[:, l2, g:g + 1], E[:, l2, g, 0],
                                                    ALU.mult, ALU.add).then_inc(s_d, 1)
                    done = behind(c, par, j, LAG)
                    if done and done[2] % (PAIRS_ // 2) == PAIRS_ // 2 - 1:
                        cd, _, jd, md = done
                        u = jd // (PAIRS_ // 2)
                        dve.wait_ge(s_pv, md + (1 + 2))
                        V_.tensor_tensor(y[:, bass.ds(cd * 2 + u, 1)].rearrange("p o (h d) -> p (o h) d", d=HD),
                                         pO[:].rearrange("p (h d) -> p h d", d=HD),
                                         bc(recips[:, u, :, 0], 2, HD), ALU.mult).then_inc(s_y, 1)

                rope(0, 0, 0, first_bank(0, 0))
                for t, x in ((0, 0), (0, 1), (1, 0), (1, 1)):
                    if (t, x) != (1, 1):
                        ahead = (t, 1) if x == 0 else (1, 0)
                        rope(0, *ahead, first_bank(*ahead))
                    for i in range(4):
                        evac(0, t, x, i, 0)
                walk(V_, slot)

            @block.scalar
            def _(act):
                A_ = nc.scalar
                act.wait_ge(setup, 6)
                A_.activation(lams[:, 0:2], lams[:, 0:2], ACT.Exp).then_inc(setup, 1)
                act.sem_inc(s_exp, 4)

                def take(b):
                    act.wait_ge(s_qkv, b * 6)
                    A_.activation(hc[:], hT[:, :, bass.ds(b * SEQ, SEQ)], ACT.Copy).then_inc(s_hc, 1)

                def high(b, t, x):
                    r = b * 4 + (2 * t + x)
                    act.wait_ge(s_xr, r + 1)
                    act.wait_ge(s_qkb, r * 4)
                    if x == 0:
                        out = stack[:].rearrange("p m (a r) d -> p m a r d", r=2)[:, :, :, 0]
                    else:
                        out = stack[:, :, 0:2]
                    A_.activation(out, bc(xr[:, x].rearrange("p (m d) -> p m d", d=16), 2, 2), ACT.Copy).then_inc(s_hi, 1)

                def values(b, t, par, bank=None):
                    act.wait_ge(s_qkv, b * 6 + (3 * t + 3) if bank is None else AHEAD.index((t, 2)) + 1)
                    A_.activation(Vb[:, par, t], (pq[:] if bank is None else bank), ACT.Copy).then_inc(s_v, 1)

                def slot(c, par, j):
                    now, turned = behind(c, par, j, 0), behind(c, par, j, 2)
                    begin, mid, _ = pieces(ACT_PIECES, c, j)

                    def piece(p):
                        if p[0] == "take":
                            take(c + 1)
                        elif p[0] == "high":
                            high(c + 1, *p[1:])
                        else:
                            values(c + 1, p[1], 1 - par)
                    for p in begin:
                        piece(p)
                    if now:
                        for g in range(2):
                            act.wait_ge(s_max, now[3] * 2 + (g + 1))
                            act.wait_ge(s_d, now[3] * 2 + (g + 1))
                            for s in range(2):
                                ins = A_.activation(E[:, j % 2, g, s], pS[:, j % 2, g, s], ACT.Exp,
                                                    bias=negmax[:, j % 2, g, s:s + 1], accum_out=sums[:, j % 2, g, s:s + 1])
                            ins.then_inc(s_exp, 1)
                    for p in mid:
                        piece(p)
                    if turned:
                        _, _, jt, mt = turned
                        act.wait_ge(s_t, mt + 3)
                        act.wait_ge(s_pv, mt + 1)
                        A_.activation(DT[:, jt % 2], pT[:], ACT.Copy).then_inc(s_dt, 1)

                take(0)
                for t in range(2):
                    for x in range(2):
                        high(0, t, x)
                for t in range(2):
                    values(0, t, 0, first_bank(t, 2))
                walk(A_, slot)

            @block.tensor
            def _(pe):
                T_ = nc.tensor
                pe.wait_ge(setup, 4)
                pe.sem_inc(s_t, 2)
                pe.sem_inc(s_pv, 2)

                def project(b, t, x, f, bank=None):
                    if f is None:
                        pe.wait_ge(s_hc, 1)
                    elif f == 0:
                        pe.wait_ge(s_hc, b + 1)
                        if x == 0:
                            pe.wait_ge(s_v, b * 2 + t)
                        else:
                            pe.wait_ge(s_rm, b * 4 + (2 * t + x))
                    for f in (range(FCH) if f is None else (f,)):
                        ins = T_.matmul((pq[:] if bank is None else bank), hc[:, f, t * P:(t + 1) * P], W[x][:, f],
                                        start=(f == 0), stop=(f == FCH - 1))
                    if f == FCH - 1:
                        ins.then_inc(s_qkv, 1)

                def turn(b, t, x, i):
                    w = b * 16 + (8 * t + 4 * x + i)
                    pe.wait_ge(s_lo, b * 8 + (2 * (2 * t + x) + i // 2 + 1))
                    pe.wait_ge(s_qke, w)
                    for q in range(4):
                        m = (4 * i + q) * 2
                        ins = T_.transpose(pK[:, q], stack[:, m:m + 2].rearrange("p m r d -> p (m r d)"), identr[:])
                    ins.then_inc(s_qkb, 1)

                def scores(m, j, g, par):
                    u, h = divmod(2 * j + g, HEADS)
                    hp = h // 2
                    pe.wait_ge(s_exp, m * 2 + (g + 1))
                    rows = slice(64 * g, 64 * g + 64)
                    for s in range(2):
                        T_.matmul(pS[:, j % 2, g, s], qk[par][rows, 0, s * 8 + hp, u * P:(u + 1) * P],
                                  qk[par][rows, 1, s * 8 + hp, :], start=(s == 0), stop=False, skip_group_check=True)
                    out, mask = (pS[:, j % 2, g], maskb[:]) if u == 0 else (pS[:, j % 2, g, :, P:SEQ], maskb[:, 0:P])
                    T_.matmul(out, identb[:], bc(mask, 1, 2), start=False, stop=True, skip_group_check=True).then_inc(s_scores, 1)

                def slot(c, par, j):
                    now, mixed, turned = behind(c, par, j, 0), behind(c, par, j, 2), behind(c, par, j, LAG)
                    begin, mid, end = pieces(PE_PIECES, c, j)

                    def piece(p):
                        (project if p[0] == "project" else turn)(c + 1, *p[1:])
                    for p in begin:
                        piece(p)
                    if now:
                        if j == 0:
                            pe.wait_ge(s_qke, c * 16 + 16)
                        for g in range(2):
                            scores(now[3], j, g, par)
                    if mixed:
                        _, _, jm, mm = mixed
                        pe.wait_ge(s_d, mm * 2 + 6)
                        pe.wait_ge(s_dt, mm)
                        for g in range(2):
                            for kt in range(2):
                                ins = T_.transpose(pT[:, g, kt], D[:, jm % 2, g, kt * P:(kt + 1) * P], cst("ident"))
                        ins.then_inc(s_t, 1)
                    for p in mid:
                        piece(p)
                    if turned:
                        ct, pt, jt, mt = turned
                        u, h = divmod(2 * jt, HEADS)
                        pe.wait_ge(s_dt, mt + 1)
                        if jt == 0:
                            pe.wait_ge(s_v, ct * 2 + 2)
                        if h == 0:
                            pe.wait_ge(s_y, ct * 2 + u)
                        for g in range(2):
                            for kt in range(2):
                                cols = slice((h + g) * HD, (h + g + 1) * HD)
                                ins = T_.matmul(pO[:, cols], DT[:, jt % 2, g, kt], Vb[:, pt, kt, cols],
                                                start=(kt == 0), stop=(kt == 1))
                        ins.then_inc(s_pv, 1)
                    for p in end:
                        piece(p)

                for t, x in AHEAD:
                    if t == 0:
                        pe.wait_ge(*((wq_loaded, 16) if x == 0 else (wkv_loaded[x - 1], 16)))
                    project(0, t, x, None, first_bank(t, x))
                    for i in range(4) if (t, x) in TURN_BEHIND else ():
                        turn(0, *TURN_BEHIND[t, x], i)
                walk(T_, slot)


AHEAD = ((0, 0), (0, 1), (1, 0), (1, 1), (0, 2), (1, 2))
TURN_BEHIND = {(0, 1): (0, 0), (1, 0): (0, 1), (1, 1): (1, 0), (1, 2): (1, 1)}


def loads_weights(sp, w_qkv, to, x):
    return sp.dma_start(to[:], w_qkv.rearrange("(j p) n -> p j n", p=P)[:, :, x * LEN:(x + 1) * LEN])


LAG, PAIRS_ = 3, HEADS
START, MID, END = 0, 1, 2
PLAN = dict(
    chunks=((2, 4, 5, 5), (8, 10, 11, 11), (14, 16, 17, 17), (23, 25, 26, 26), (29, 31, 32, 32), (35, 37, 38, 38)),
    read=(6, 12, 18, 27, 33, 39),
    high=(9, 15, 30, 36),
    turns=((11, 13, 14, 16), (17, 19, 20, 22), (32, 34, 35, 37), (41, 43, 44, 46)),
    fetch=((12, 13, 15, 16), (18, 19, 21, 22), (33, 34, 36, 37), (42, 43, 45, 46)),
)
PE_PIECES, DVE_PIECES, ACT_PIECES = {}, {}, {(0, START): [("take",)]}


def put(table, at, *piece):
    table.setdefault(divmod(at, 3), []).append(piece)


for _n in range(4):
    _t, _x = divmod(_n, 2)
    put(ACT_PIECES, PLAN["high"][_n], "high", _t, _x)
    for _i in range(4):
        put(DVE_PIECES, PLAN["fetch"][_n][_i], "evac", _t, _x, _i)
for _n in range(6):
    _t, _x = divmod(_n, 3)
    put(ACT_PIECES if _x == 2 else DVE_PIECES, PLAN["read"][_n], *(("values", _t) if _x == 2 else ("rope", _t, _x)))
    for _i in range(4):
        put(PE_PIECES, PLAN["chunks"][_n][_i], "project", _t, _x, _i)
for _n in range(4):
    for _i in range(4):
        put(PE_PIECES, PLAN["turns"][_n][_i], "turn", *divmod(_n, 2), _i)



EXPERTS, TOPK, INTER = 64, 8, 128
EPS = 1e-5
UP, GATE, GATE1 = 64, 192, 320
JOINT = 321


def mix_phase(nc, hT, y, keep, d, consts):
    with ExitStack() as ctx:
        sb = lambda n, s, dt=F32: ctx.enter_context(nc.sbuf_tensor("c_" + n, s, dt))
        sem = lambda n: ctx.enter_context(nc.semaphore("c_" + n))
        pb = lambda n, s: ctx.enter_context(nc.psum_tensor("c_" + n, s, F32))
        cst = lambda n: consts[:, CONST[n][0]:CONST[n][0] + CONST[n][1]]
        Wo = sb("Wo", [P, FCH, LEN])
        Wj = sb("Wj", [P, FCH, JOINT])
        Wd = sb("Wd", [P, LEN])
        gb = sb("gb", [P, 2, 2, 2])
        bna = sb("bna", [P, TILES, 6])
        tok_mv = sb("tok_mv", [P, TILES, 2])
        gmean, diff, gvar, grstd = (sb(n, [P, TILES]) for n in ("gmean", "diff", "gvar", "grstd"))
        ab = sb("ab", [P, 2, TILES // 2, 2, 2])
        am = sb("am", [P, TILES // 2, 2, 2])
        abn = sb("abn", [P, 2, 2])
        hs = sb("hs", [P, 2, FCH, P])
        z = sb("z", [P, LEN])
        zT = sb("zT", [P, FCH, P])
        h1 = sb("h1", [P, LEN])
        h1T = sb("h1T", [P, FCH, P])
        bn, mv, rstd = sb("bn", [P, 6]), sb("mv", [P, 2]), sb("rstd", [P, 2])
        top, topi, topf = sb("top", [P, TOPK]), sb("topi", [P, TOPK], U32), sb("topf", [P, TOPK])
        negtop, wsum = sb("negtop", [P, 1]), sb("wsum", [P, 2])
        onehot, picked = sb("onehot", [P, TOPK, EXPERTS]), sb("picked", [P, TOPK, EXPERTS])
        chosen = sb("chosen", [P, EXPERTS], BF16)
        R = sb("R", [P, EXPERTS])
        posf, pos = sb("posf", [P, TOPK]), sb("pos", [P, 2, TOPK], I32)
        tok = sb("tok", [P, TILES], I32)
        tokc = sb("tokc", [P, 2, 1], I32)
        ex, rc, inter = sb("ex", [P, INTER + 1]), sb("rc", [P, 2, INTER + 1]), sb("inter", [P, INTER])
        interT = sb("interT", [P, INTER])
        beforeb, onesb = sb("beforeb", [P, P], BF16), sb("onesb", [P, P], BF16)
        zero = sb("zero", [P, EXPERTS * TOK // P], I32)
        pA = pb("pA", [P, 2, LEN])
        pZ, pX, pR, pC, pI, pD = (pb(n, [P, LEN]) for n in ("pZ", "pX", "pR", "pC", "pI", "pD"))
        rw, ranks, experts, carry = keep["rw"], keep["ranks"], keep["experts"], keep["counts"]

        loaded, gb_loaded, setup, group, grooted = sem("loaded"), sem("gb_loaded"), sem("setup"), sem("group"), sem("group_rstd")
        zeroed, listed0, spared = sem("zeroed"), sem("list_zero"), sem("spare_zero")
        s_z, s_ln, s_rt, s_si, s_rk = (sem("dve_" + n) for n in ("z", "norm", "route", "silu", "rank"))
        Z, LN, RT, SI, RK = 2, 4, 6, 4, 7
        z_turned, z_taken, hs_taken, joined = sem("z_turned"), sem("z_taken"), sem("hs_taken"), sem("wo")
        rooted, h1_kept, h1_turned, h1_taken, joint = (sem(n) for n in ("root", "h1_kept", "h1_turned", "h1_taken", "joint"))
        s_ex, s_w8, counted, i_turned, i_taken, down, ended = (
            sem(n) for n in ("ex", "w8", "counted", "i_turned", "i_taken", "down", "ended"))
        h1_stored, listed = [sem("h1_stored0"), sem("h1_stored1")], [sem("listed0"), sem("listed1")]
        passed, passed_p, passed_s = sem("passed"), sem("passed_pool"), sem("passed_sync")
        LOADS = 16 * 3
        FIRST, LAST, RAMP = -1, TILES + 2, 5

        def walk(engine, step):
            turns = (TILES - 2 - (FIRST + RAMP)) // 2
            for c in range(FIRST, FIRST + RAMP):
                step(0, c)
            with engine.Fori(0, turns) as i:
                for c in (FIRST + RAMP, FIRST + RAMP + 1):
                    step(i * 2, c)
            for c in range(FIRST + RAMP + 2 * turns, LAST + 1):
                step(0, c)

        def tile(base, c, off):
            n = c + off
            if isinstance(base, int) and not 0 <= n < TILES:
                return None
            return base + n, n % 2, (not isinstance(base, int)) or n >= 2

        with nc.Block() as block:
            @block.sync
            def _(sp):
                sp.dma_start(Wo[:], d["wo"].rearrange("(j p) n -> p j n", p=P)).then_inc(loaded, 16)
                for i, n in enumerate(("gamma", "beta")):
                    for u in range(2):
                        sp.dma_start(gb[:, i, u], d[n].rearrange("(u p a) -> u p a", p=P, a=2)[u]).then_inc(gb_loaded, 16)
                sp.dma_start(Wj[:], d["w_joint"].rearrange("(j p) n -> p j n", p=P)).then_inc(loaded, 16)
                sp.dma_start(Wd[:], d["sh_down"]).then_inc(loaded, 16)
                sp.wait_ge(zeroed, 1)
                sp.dma_start(d["lists"].rearrange("(p n) a -> p (n a)", p=P), zero[:]).then_inc(listed0, 16)
                sp.wait_ge(listed0, 16)
                spare = d["slots"].rearrange("(t p) n -> p t n", p=P)[:, TOK * TOPK // P:]
                sp.dma_start(spare, bc(zero[:, 0:LEN].bitcast(F32), 1, EXPERTS)).then_inc(spared, 16)
                h1_out = d["h1"].rearrange("(t p) n -> p t n", p=P)

                def store(n, par, late):
                    sp.wait_ge(s_ln, n * LN + LN)
                    sp.sem_inc(passed_s, 1)
                    if late:
                        sp.wait_ge(h1_stored[par], (n - par) * 8)
                    sp.dma_start(h1_out[:, bass.ds(n, 1)], y[:, bass.ds(n, 1)]).then_inc(h1_stored[par], 16)
                store(0, 0, False)
                store(1, 1, False)
                with nc.sync.Fori(1, TILES // 2) as i:
                    for par in range(2):
                        store(i * 2 + par, par, True)
                for par in range(2):
                    sp.wait_ge(h1_stored[par], 16 * TILES // 2)
                sp.wait_ge(spared, 16)

            @block.gpsimd
            def _(pool):
                nc.gpsimd.memset(zero[:], 0).then_inc(zeroed, 1)
                pool.wait_ge(setup, GVAR)
                nc.gpsimd.tensor_tensor(grstd[:], gvar[:], cst("minus_half").to_broadcast([P, TILES]), ALU.pow).then_inc(grooted, 1)
                pool.wait_ge(listed0, 16)

                def step(base, c):
                    if t := tile(base, c, 0):
                        n, _, _ = t
                        pool.wait_ge(s_ln, n * LN + 3)
                        nc.gpsimd.tensor_tensor(rstd[:, 1:2], rstd[:, 0:1], cst("minus_half"), ALU.pow).then_inc(rooted, 1)
                    if t := tile(base, c, -2):
                        n, par, _ = t
                        pool.wait_ge(s_rk, n * RK + RK)
                        pool.sem_inc(passed_p, 1)
                        for k in range(TOPK):
                            nc.gpsimd.indirect_dma_start(
                                d["lists"], bass.IndirectOffsetOnAxis(ap=pos[:, par, k:k + 1], axis=0),
                                tokc[:, par], None).then_inc(listed[par], 16)
                walk(nc.gpsimd, step)
                for par in range(2):
                    pool.wait_ge(listed[par], 16 * TOPK * TILES // 2)

            @block.vector
            def _(dve):
                V_ = nc.vector
                st = Steps(setup)

                def do(s, ins, wait=True, alone=False):
                    s.inc(ins)
                    if wait:
                        s.wait(dve)
                    if alone:
                        dve.sem_inc(passed, 1)
                do(st, V_.tensor_copy(beforeb[:], cst("before")), False)
                do(st, V_.tensor_copy(onesb[:], cst("ones")), False)
                do(st, V_.memset(carry, 0.0), False)
                for t in range(TILES):
                    do(st, V_.tensor_scalar(tok[:, t:t + 1], cst("lane"), float(P * t), None, ALU.add), False)
                for t in range(TILES):
                    do(st, V_.bn_stats(bna[:, t], y[:, t]), False)
                st.wait(dve)
                dve.sem_inc(passed, 1)
                for t in range(TILES):
                    do(st, V_.bn_aggr(tok_mv[:, t], bna[:, t]), False)
                assert st.n == TOKEN_STATS
                st.wait(dve)
                dve.wait_ge(group, 1)
                do(st, V_.tensor_copy(gmean[:], pC[:, 0:2 * TILES].rearrange("p (t a) -> p t a", a=2)[:, :, 0]))
                do(st, V_.tensor_tensor(diff[:], tok_mv[:, :, 0], gmean[:], ALU.subtract))
                do(st, V_.tensor_tensor(diff[:], diff[:], diff[:], ALU.mult))
                do(st, V_.tensor_tensor(diff[:], diff[:], tok_mv[:, :, 1], ALU.add), False)
                assert st.n == SPREAD
                dve.wait_ge(group, 2)
                do(st, V_.tensor_scalar(gvar[:], pC[:, 0:TILES], EPS, None, ALU.add), False)
                assert st.n == GVAR
                dve.wait_ge(gb_loaded, 64)
                do(st, V_.tensor_scalar(gb[:], gb[:], 1.0 - INIT_LAMBDA, None, ALU.mult))
                dve.wait_ge(grooted, 1)
                by_tile = lambda x: bc(x[:].rearrange("p (t u) -> p t u", u=2), 3, 2)
                do(st, V_.tensor_tensor(ab[:, 0], bc(gb[:, 0], 1, TILES // 2), by_tile(grstd), ALU.mult))
                do(st, V_.tensor_tensor(am[:], ab[:, 0], by_tile(gmean), ALU.mult))
                do(st, V_.tensor_tensor(ab[:, 1], bc(gb[:, 1], 1, TILES // 2), am[:], ALU.subtract))

                def step(base, c):
                    if t := tile(base, c, -2):
                        n, _, _ = t
                        q = Steps(s_rt)
                        q.start = n * RT
                        dve.wait_ge(joint, n + 1)
                        dve.sem_inc(passed, 1)
                        logits = pR[:, 0:EXPERTS]
                        do(q, V_.max(top[:], logits), alone=True)
                        do(q, V_.max_index(topi[:], top[:], logits), False)
                        do(q, V_.tensor_scalar(negtop[:], top[:, 0:1], -1.0, None, ALU.mult))
                        do(q, V_.tensor_copy(topf[:], topi[:]))
                        do(q, V_.tensor_tensor(onehot[:], bc(cst("experts"), 1, TOPK), bc(topf[:], 2, EXPERTS), ALU.is_equal))
                        with nc.allow_low_precision(reason="zeros and ones"):
                            do(q, V_.tensor_reduce(chosen[:], onehot[:].rearrange("p k e -> p e k"), AX.X, ALU.add), False)
                        assert q.n == RT
                    if t := tile(base, c, 1):
                        n, _, _ = t
                        q = Steps(s_z)
                        q.start = n * Z
                        if c >= 0 or not isinstance(base, int):
                            dve.wait_ge(z_turned, n)
                        do(q, V_.tensor_copy(abn[:], ab[:].rearrange("p i t u f -> p i (t u) f")[:, :, bass.ds(n, 1)].rearrange("p i o f -> p i (o f)")))
                        yt = y[:, bass.ds(n, 1)].rearrange("p o n -> p (o n)")
                        for f in range(2):
                            half = slice(f * 256, (f + 1) * 256)
                            ins = V_.tensor_scalar(z[:, half], yt[:, half], abn[:, 0, f:f + 1], abn[:, 1, f:f + 1], ALU.mult, ALU.add)
                        do(q, ins, False)
                        assert q.n == Z
                    if t := tile(base, c, -2):
                        n, par, late = t
                        q = Steps(s_si)
                        q.start = n * SI
                        dve.wait_ge(s_ex, n + 1)
                        do(q, V_.tensor_scalar(rc[:, par], ex[:], 1.0, None, ALU.add))
                        do(q, V_.reciprocal(rc[:, par], rc[:, par]))
                        if c > 2 or not isinstance(base, int):
                            dve.wait_ge(i_turned, n)
                        do(q, V_.tensor_tensor(inter[:], rc[:, par, 0:INTER], pR[:, GATE:GATE1], ALU.mult))
                        do(q, V_.tensor_tensor(inter[:], inter[:], pR[:, UP:GATE], ALU.mult), False)
                        assert q.n == SI
                    if t := tile(base, c, 0):
                        n, par, _ = t
                        q = Steps(s_ln)
                        q.start = n * LN
                        dve.wait_ge(joined, n + 1)
                        do(q, V_.bn_stats(bn[:], pA[:, par]), alone=True)
                        do(q, V_.bn_aggr(mv[:], bn[:]))
                        do(q, V_.tensor_scalar(rstd[:, 0:1], mv[:, 1:2], EPS, None, ALU.add), False)
                    if t := tile(base, c, -2):
                        n, par, late = t
                        q = Steps(s_rk)
                        q.start = n * RK
                        kept = lambda x: x[:, bass.ds(n * TOPK, TOPK)]
                        dve.wait_ge(counted, n + 1)
                        do(q, V_.tensor_tensor(R[:], pC[:, 0:EXPERTS], carry, ALU.add))
                        do(q, V_.tensor_tensor(carry, pC[:, EXPERTS:2 * EXPERTS], carry, ALU.add), False)
                        do(q, V_.tensor_tensor(picked[:], onehot[:], bc(R[:], 1, TOPK), ALU.mult))
                        do(q, V_.tensor_reduce(posf[:], picked[:], AX.X, ALU.add))
                        V_.tensor_copy(kept(ranks), posf[:])
                        V_.tensor_copy(kept(experts), topf[:])
                        if late:
                            dve.wait_ge(listed[par], (n - par) * 8 * TOPK)
                        do(q, V_.tensor_copy(tokc[:, par], tok[:, bass.ds(n, 1)]), False)
                        dve.wait_ge(s_w8, n + 1)
                        do(q, V_.reciprocal(wsum[:, 1:2], wsum[:, 0:1]), False)
                        do(q, V_.scalar_tensor_tensor(pos[:, par], topf[:], float(TOK), posf[:], ALU.mult, ALU.add))
                        assert q.n == RK
                        V_.tensor_scalar(kept(rw), kept(rw), wsum[:, 1:2], None, ALU.mult)
                    if t := tile(base, c, 0):
                        n, par, _ = t
                        q = Steps(s_ln)
                        q.start, q.n = n * LN, 3
                        dve.wait_ge(rooted, n + 1)
                        do(q, V_.tensor_scalar(y[:, bass.ds(n, 1)].rearrange("p o n -> p (o n)"), pA[:, par], mv[:, 0:1], rstd[:, 1:2],
                                               ALU.subtract, ALU.mult), False)
                        assert q.n == LN
                    if t := tile(base, c, -3):
                        n, par, _ = t
                        dve.wait_ge(down, n + 1)
                        dve.wait_ge(h1_stored[par], (n - par) * 8 + 16)
                        yt = y[:, bass.ds(n, 1)].rearrange("p o n -> p (o n)")
                        V_.scalar_tensor_tensor(yt, pD[:], rc[:, par, INTER:INTER + 1], yt, ALU.mult, ALU.add).then_inc(ended, 1)
                walk(V_, step)

            @block.scalar
            def _(act):
                A_ = nc.scalar

                def residual(n, par, late):
                    if late:
                        act.wait_ge(joined, n - 1)
                    A_.activation(hs[:, par], hT[:, :, bass.ds(n * P, P)], ACT.Copy).then_inc(hs_taken, 1)

                def step(base, c):
                    first = isinstance(base, int)
                    if t := tile(base, c, -1):
                        n, _, _ = t
                        act.wait_ge(s_ln, n * LN + LN)
                        if not (first and c < 2):
                            act.wait_ge(h1_turned, n)
                        A_.activation(h1[:], y[:, bass.ds(n, 1)].rearrange("p o n -> p (o n)"), ACT.Copy).then_inc(h1_kept, 1)
                    if t := tile(base, c, -2):
                        n, _, _ = t
                        act.wait_ge(s_rt, n * RT + 2)
                        if not (first and c < 3):
                            act.wait_ge(s_si, n * SI)
                        A_.activation(ex[:], pR[:, GATE:JOINT], ACT.Exp, scale=-1.0).then_inc(s_ex, 1)
                        act.wait_ge(s_rt, n * RT + 3)
                        if not (first and c < 3):
                            act.wait_ge(s_rk, n * RK)
                        A_.activation(rw[:, bass.ds(n * TOPK, TOPK)], top[:], ACT.Exp, bias=negtop[:], accum_out=wsum[:, 0:1]).then_inc(s_w8, 1)
                    if t := tile(base, c, 1):
                        residual(*t)
                        n, _, _ = t
                        act.wait_ge(z_turned, n + 1)
                        if not (first and c < 0):
                            act.wait_ge(joined, n)
                        A_.activation(zT[:].rearrange("p j n -> p (j n)"), pZ[:], ACT.Copy).then_inc(z_taken, 1)
                    if t := tile(base, c, -1):
                        n, _, _ = t
                        act.wait_ge(h1_turned, n + 1)
                        if not (first and c < 2):
                            act.wait_ge(joint, n)
                        A_.activation(h1T[:].rearrange("p j n -> p (j n)"), pX[:], ACT.Copy).then_inc(h1_taken, 1)
                    if t := tile(base, c, -2):
                        n, _, _ = t
                        act.wait_ge(i_turned, n + 1)
                        if not (first and c < 3):
                            act.wait_ge(down, n)
                        A_.activation(interT[:], pI[:, 0:P], ACT.Copy).then_inc(i_taken, 1)
                walk(A_, step)

            @block.tensor
            def _(pe):
                T_ = nc.tensor
                ident = cst("ident")
                pe.wait_ge(setup, TOKEN_STATS)
                T_.matmul(pC[:, 0:2 * TILES], cst("group"), tok_mv[:].rearrange("p t a -> p (t a)"), start=True, stop=True).then_inc(group, 1)
                pe.wait_ge(setup, SPREAD)
                T_.matmul(pC[:, 0:TILES], cst("group"), diff[:], start=True, stop=True).then_inc(group, 1)
                pe.wait_ge(loaded, LOADS)

                def step(base, c):
                    first = isinstance(base, int)
                    if t := tile(base, c, 0):
                        n, par, late = t
                        pe.wait_ge(z_taken, n + 1)
                        pe.wait_ge(hs_taken, n + 1)
                        if late:
                            pe.wait_ge(s_ln, (n - 1) * LN)
                        for j in range(FCH):
                            T_.matmul(pA[:, par], zT[:, j], Wo[:, j], start=(j == 0), stop=False, skip_group_check=True)
                        for j in range(FCH):
                            ins = T_.matmul(pA[:, par, j * P:(j + 1) * P], hs[:, par, j], ident, start=False, stop=True, skip_group_check=True)
                        ins.then_inc(joined, 1)
                    if t := tile(base, c, 1):
                        n, _, _ = t
                        pe.wait_ge(s_z, n * Z + Z)
                        if not (first and c < 0):
                            pe.wait_ge(z_taken, n)
                        for j in range(FCH):
                            ins = T_.transpose(pZ[:, j * P:(j + 1) * P], z[:, j * P:(j + 1) * P], ident)
                        ins.then_inc(z_turned, 1)
                    if t := tile(base, c, -1):
                        n, _, _ = t
                        pe.wait_ge(h1_kept, n + 1)
                        if not (first and c < 2):
                            pe.wait_ge(h1_taken, n)
                        for j in range(FCH):
                            ins = T_.transpose(pX[:, j * P:(j + 1) * P], h1[:, j * P:(j + 1) * P], ident)
                        ins.then_inc(h1_turned, 1)
                    if t := tile(base, c, -2):
                        n, _, _ = t
                        pe.wait_ge(s_rt, n * RT + RT)
                        if not (first and c < 3):
                            pe.wait_ge(s_rk, (n - 1) * RK + 2)
                        T_.matmul(pC[:, 0:EXPERTS], beforeb[:], chosen[:], start=True, stop=True)
                        T_.matmul(pC[:, EXPERTS:2 * EXPERTS], onesb[:], chosen[:], start=True, stop=True).then_inc(counted, 1)
                        pe.wait_ge(s_si, n * SI + SI)
                        if not (first and c < 3):
                            pe.wait_ge(i_taken, n)
                        T_.transpose(pI[:, 0:P], inter[:], ident).then_inc(i_turned, 1)
                    if t := tile(base, c, -3):
                        n, _, _ = t
                        pe.wait_ge(i_taken, n + 1)
                        if not (first and c < 4):
                            pe.wait_ge(ended, n)
                        T_.matmul(pD[:], interT[:], Wd[:], start=True, stop=True).then_inc(down, 1)
                    if t := tile(base, c, -1):
                        n, _, _ = t
                        pe.wait_ge(h1_taken, n + 1)
                        if not (first and c < 2):
                            pe.wait_ge(s_si, n * SI)
                        for j in range(FCH):
                            ins = T_.matmul(pR[:, 0:JOINT], h1T[:, j], Wj[:, j], start=(j == 0), stop=(j == FCH - 1))
                        ins.then_inc(joint, 1)
                walk(T_, step)


TOKEN_STATS = 3 + 3 * TILES
SPREAD, GVAR = TOKEN_STATS + 4, TOKEN_STATS + 5


def keeps(nc, ctx):
    sb = lambda n, s, dt=F32: ctx.enter_context(nc.sbuf_tensor("k_" + n, s, dt))
    return dict(rw=sb("rw", [P, TILES * TOPK])[:], ranks=sb("ranks", [P, TILES * TOPK])[:],
                experts=sb("experts", [P, TILES * TOPK])[:], slots=sb("slots", [P, TILES * TOPK])[:], counts=sb("counts", [P, EXPERTS])[:])



MAX_TILES = TOK * TOPK // P + EXPERTS
RING = 8
PAIRS = TILES * TOPK
EACH = PAIRS // (TOK * TOPK // P // RING)
WCOLS = FCH * 2 * INTER + LEN


def expert_phase(nc, keep, d, consts):
    NT = MAX_TILES
    with ExitStack() as ctx:
        sb = lambda n, s, dt=F32: ctx.enter_context(nc.sbuf_tensor("d_" + n, s, dt))
        sem = lambda n: ctx.enter_context(nc.semaphore("d_" + n))
        pb = lambda n, s: ctx.enter_context(nc.psum_tensor("d_" + n, s, F32))
        cst = lambda n: consts[:, CONST[n][0]:CONST[n][0] + CONST[n][1]]
        ident = cst("ident")
        more_than = sb("more_than", [P, EXPERTS, 16])
        nt, cum, first = sb("nt", [P, EXPERTS]), sb("cum", [P, 2, EXPERTS]), sb("first", [P, EXPERTS])
        behind = sb("behind", [P, 2, EXPERTS])
        et, bt, tt, rowf, rowi = (sb(n, [P, 2]) for n in ("et", "bt", "tt", "rowf", "rowi_f"))
        rowi = sb("rowi", [P, 2], I32)
        rows = sb("rows", [P, 2, P], I32)
        rowsf = sb("rowsf", [P, 2, P])
        idx = sb("idx", [P, 2 * P], I32)
        idxc = sb("idxc", [P, 2, RING], I32)
        erow = sb("erow", [1, 2 * P])
        turn = sb("turn", [1, 2, 2 * P])
        livef, live = sb("livef", [1, 2]), sb("live", [1, 1], I32)
        tab = sb("tab", [1, 3, 2 * P], I32)
        W = sb("W", [P, RING, WCOLS])
        X = sb("X", [P, RING, LEN])
        XT = sb("XT", [P, 2, LEN])
        ex, inter = sb("ex", [P, INTER]), sb("inter", [P, 2, INTER])
        interT = sb("interT", [P, 2, INTER])
        Y = sb("Y", [P, RING, LEN])
        oneh = sb("oneh", [P, EACH, EXPERTS])
        base = sb("base", [P, EACH])
        pX, pG, pY = pb("pX", [P, 2, LEN]), pb("pG", [P, 2, LEN]), pb("pY", [P, 2, LEN])
        pI = pb("pI", [P, LEN])
        st_s = sem("setup")
        listg, turned, tabbed, ready = sem("list_rows"), sem("rows_turned"), sem("erow"), sem("tables")
        wl = [sem(f"weights{u}") for u in range(RING)]
        xl = [sem(f"gathered{u}") for u in range(RING)]
        yl = [sem(f"stored{u}") for u in range(RING)]
        xt, xte, gu, s_ex, s_r, s_in = sem("xt"), sem("xt_evac"), sem("gate_up"), sem("ex"), sem("rc"), sem("inter")
        it, ite, dn, yr = sem("it"), sem("it_evac"), sem("down"), sem("y_ready")
        idxs, passed, s_pos = sem("idx_copied"), sem("passed"), sem("positions")
        passed_sp = sem("passed_sync")
        PER = 16 // RING
        HALF = (RING - 1.0) / (2 * RING)
        SURE, TURNS = TOK * TOPK // P // RING, NT // RING

        def last_turn(engine):
            return engine.value_load(live[0:1, 0:1], min_val=SURE - 1, max_val=TURNS - 1)

        def walk(engine, four, end, sure=None):
            with engine.Fori(1, SURE) as i:
                (sure or four)(i)
            with engine.Fori(SURE, TURNS) as i:
                with engine.If(i < end + 1):
                    four(i)

        with nc.Block() as block:
            @block.vector
            def _(dve):
                V_ = nc.vector
                st = Steps(st_s)

                def do(ins, wait=True):
                    st.inc(ins)
                    if wait:
                        st.wait(dve)
                do(V_.tensor_tensor(more_than[:], bc(keep["counts"], 2, 16), bc(cst("tiles128"), 1, EXPERTS), ALU.is_gt))
                do(V_.tensor_reduce(nt[:], more_than[:], AX.X, ALU.add))
                do(V_.tensor_copy(cum[:, 0], nt[:]))
                a, s = 0, 1
                while s < EXPERTS:
                    do(V_.tensor_copy(cum[:, 1 - a, 0:s], cum[:, a, 0:s]), False)
                    do(V_.tensor_tensor(cum[:, 1 - a, s:], cum[:, a, s:], cum[:, a, 0:EXPERTS - s], ALU.add))
                    a, s = 1 - a, 2 * s
                incl = cum[:, a]
                do(V_.tensor_tensor(first[:], incl, nt[:], ALU.subtract))
                do(V_.tensor_scalar(first[:], first[:], float(P), None, ALU.mult))
                for g in range(2):
                    do(V_.tensor_scalar(tt[:, g:g + 1], cst("lane"), float(P * g), None, ALU.add))
                    do(V_.tensor_scalar(behind[:, g], incl, tt[:, g:g + 1], None, ALU.is_le))
                    do(V_.tensor_reduce(et[:, g:g + 1], behind[:, g], AX.X, ALU.add), False)
                    do(V_.tensor_tensor(behind[:, g], behind[:, g], nt[:], ALU.mult))
                    do(V_.tensor_reduce(bt[:, g:g + 1], behind[:, g], AX.X, ALU.add))
                do(V_.tensor_scalar(et[:], et[:], float(EXPERTS - 1), None, ALU.min))
                do(V_.tensor_tensor(tt[:], tt[:], bt[:], ALU.subtract))
                do(V_.scalar_tensor_tensor(rowf[:], et[:], 16.0, tt[:], ALU.mult, ALU.add))
                do(V_.tensor_scalar(rowi[:], rowf[:], float(EXPERTS * 16 - 1), None, ALU.min))
                assert st.n == ROWS, st.n
                for g in range(2):
                    dve.wait_ge(listg, 16 * (g + 1))
                    do(V_.tensor_copy(rowsf[:, g], rows[:, g]))
                assert st.n == ROWS + 2
                dve.wait_ge(turned, 2)
                do(V_.tensor_copy(idx[:], pX[:, 0, 0:2 * P]))
                do(V_.tensor_copy(erow[:], pG[0:1, 0, 0:2 * P]))
                do(V_.memset(turn[:, 0, 0:1], 1.0), False)
                do(V_.tensor_tensor(turn[:, 0, 1:], erow[:, 1:], erow[:, 0:2 * P - 1], ALU.not_equal))
                do(V_.tensor_copy(tab[:, 1], turn[:, 0]), False)
                do(V_.tensor_copy(tab[:, 0], erow[:]))
                a, s = 0, 1
                while s < 2 * P:
                    do(V_.tensor_copy(turn[:, 1 - a, 0:s], turn[:, a, 0:s]), False)
                    do(V_.tensor_tensor(turn[:, 1 - a, s:], turn[:, a, s:], turn[:, a, 0:2 * P - s], ALU.add))
                    a, s = 1 - a, 2 * s
                do(V_.tensor_scalar(livef[:, 0:1], incl[0:1, EXPERTS - 1:], 1.0 / RING, -1.0 / RING - HALF, ALU.mult, ALU.add))
                do(V_.tensor_scalar(livef[:, 1:2], livef[:, 0:1], ROUND, ROUND, ALU.add, ALU.subtract))
                do(V_.tensor_copy(live[:], livef[:, 1:2]))
                do(V_.tensor_scalar(turn[:, 1 - a], turn[:, a], 1.0 / RING, -HALF, ALU.mult, ALU.add))
                do(V_.tensor_scalar(turn[:, 1 - a], turn[:, 1 - a], ROUND, ROUND, ALU.add, ALU.subtract))
                do(V_.scalar_tensor_tensor(tab[:, 2], turn[:, 1 - a], -float(RING), turn[:, a], ALU.mult, ALU.add))
                V_.tensor_copy(tt[:, 0:1], tt[:, 1:2]).then_inc(ready, 1)

                def silu(t, u):
                    w = u % 2
                    dve.wait_ge(s_ex, t + 1)
                    if not (isinstance(t, int) and t < 2):
                        dve.wait_ge(it, t - 1)
                    V_.tensor_scalar(inter[:, w], ex[:], 1.0, None, ALU.add).then_inc(s_r, 1)
                    dve.wait_ge(s_r, t * 3 + 1)
                    V_.reciprocal(inter[:, w], inter[:, w]).then_inc(s_r, 1)
                    dve.wait_ge(s_r, t * 3 + 2)
                    V_.tensor_tensor(inter[:, w], inter[:, w], pG[:, w, 0:INTER], ALU.mult).then_inc(s_r, 1)
                    dve.wait_ge(s_r, t * 3 + 3)
                    V_.tensor_tensor(inter[:, w], inter[:, w], pG[:, w, INTER:2 * INTER], ALU.mult).then_inc(s_in, 1)

                def out(t, u, late=True):
                    dve.wait_ge(dn, t + (1 + RING))
                    if late:
                        dve.wait_ge(yl[u], (t - u) * PER)
                    V_.tensor_copy(Y[:, u], pY[:, u % 2]).then_inc(yr, 1)

                def place(i):
                    pairs = bass.ds(i * EACH, EACH)
                    V_.tensor_tensor(oneh[:], bc(cst("experts"), 1, EACH), bc(keep["experts"][:, pairs], 2, EXPERTS), ALU.is_equal).then_inc(s_pos, 1)
                    dve.wait_ge(s_pos, i * 4 + 1)
                    V_.tensor_tensor(oneh[:], oneh[:], bc(first[:], 1, EACH), ALU.mult).then_inc(s_pos, 1)
                    dve.wait_ge(s_pos, i * 4 + 2)
                    V_.tensor_reduce(base[:], oneh[:], AX.X, ALU.add).then_inc(s_pos, 1)
                    dve.wait_ge(s_pos, i * 4 + 3)
                    V_.tensor_tensor(keep["slots"][:, pairs], keep["ranks"][:, pairs], base[:], ALU.add).then_inc(s_pos, 1)

                def four(i, head=False, placing=False):
                    for u in range(RING):
                        t = i * RING + u
                        silu(t, u)
                        if not (head and u < 2):
                            out(t - 2, (u - 2) % RING, late=not head)
                        if placing and u == RING // 2:
                            place(i)

                end = last_turn(dve)
                four(0, True, placing=True)
                walk(V_, four, end, lambda i: four(i, placing=True))
                for u in (RING - 2, RING - 1):
                    out(end * RING + u, u)

            @block.gpsimd
            def _(pool):
                G_ = nc.gpsimd
                pool.wait_ge(st_s, ROWS)
                rows_view = d["lists"].rearrange("(r n) a -> r (n a)", n=P)
                for g in range(2):
                    G_.indirect_dma_start(rows[:, g], None, rows_view,
                                          bass.IndirectOffsetOnAxis(ap=rowi[:, g:g + 1], axis=0)).then_inc(listg, 16)
                    pool.wait_ge(listg, 16 * (g + 1))
                pool.wait_ge(ready, 1)

                def four(i, par, head=False):
                    G_.tensor_copy(idxc[:, par], idx[:, bass.ds(i * RING, RING)]).then_inc(idxs, 1)
                    pool.wait_ge(idxs, i + 1)
                    pool.sem_inc(passed, 1)
                    for u in range(RING):
                        t = i * RING + u
                        if not head:
                            pool.wait_ge(xt, t - (RING - 1))
                            pool.sem_inc(passed, 1)
                        G_.indirect_dma_start(X[:, u], None, d["h1"],
                                              bass.IndirectOffsetOnAxis(ap=idxc[:, par, u:u + 1], axis=0)).then_inc(xl[u], 16)

                end = last_turn(pool)
                four(0, 0, True)
                four(1, 1)
                with G_.Fori(1, SURE // 2) as i:
                    four(i * 2, 0)
                    four(i * 2 + 1, 1)
                four(SURE, 0)
                with G_.Fori(SURE // 2, TURNS // 2) as i:
                    with G_.If(i * 2 < end + 1):
                        four(i * 2 + 1, 1)
                    with G_.If(i * 2 < end):
                        four(i * 2 + 2, 0)
                for u in range(RING):
                    pool.wait_ge(xl[u], end * 16 + 32)

            @block.sync
            def _(sp):
                sp.wait_ge(ready, 1)
                yv = d["slots"].rearrange("(t p) n -> p t n", p=P)

                def four(i, head=False):
                    for u in range(RING):
                        t = i * RING + u
                        e = sp.value_load(tab[0:1, 0, bass.ds(t, 1)], min_val=0, max_val=EXPERTS - 1)
                        new = sp.value_load(tab[0:1, 1, bass.ds(t, 1)], min_val=0, max_val=1)
                        at = sp.value_load(tab[0:1, 2, bass.ds(t, 1)], min_val=0, max_val=RING - 1)
                        if not head:
                            sp.wait_ge(dn, t + 1)
                        sp.dma_start(W[:, bass.ds(at, 1)].rearrange("p o n -> p (o n)"),
                                     d["w_experts"][bass.ds(e, 1)].rearrange("o p n -> p (o n)"), cond=new).then_inc(wl[u], 16)
                        if not head:
                            store(t - RING, u)

                def store(t, u):
                    sp.wait_ge(yr, t + 1)
                    sp.dma_start(yv[:, bass.ds(t, 1)].rearrange("p o n -> p (o n)"), Y[:, u]).then_inc(yl[u], 16)

                end = last_turn(sp)
                four(0, True)
                walk(nc.sync, four, end)
                for u in range(RING):
                    store(end * RING + u, u)
                for u in range(RING):
                    sp.wait_ge(yl[u], end * 16 + 16)
                    sp.sem_inc(passed_sp, 1)

            @block.scalar
            def _(act):
                A_ = nc.scalar

                def x_evac(t, u):
                    act.wait_ge(xt, t + 1)
                    A_.activation(XT[:, u % 2], pX[:, u % 2], ACT.Copy).then_inc(xte, 1)

                def exps(t, u):
                    act.wait_ge(gu, t + 1)
                    act.wait_ge(s_in, t)
                    A_.activation(ex[:], pG[:, u % 2, 0:INTER], ACT.Exp, scale=-1.0).then_inc(s_ex, 1)

                def i_evac(t, u):
                    act.wait_ge(it, t + 1)
                    A_.activation(interT[:, u % 2], pI[:, 0:P], ACT.Copy).then_inc(ite, 1)

                def four(i, head=False):
                    for u in range(RING):
                        t = i * RING + u
                        x_evac(t + 1, (u + 1) % RING)
                        exps(t, u)
                        if not (head and u == 0):
                            i_evac(t - 1, (u - 1) % RING)

                act.wait_ge(ready, 1)
                end = last_turn(act)
                x_evac(0, 0)
                four(0, head=True)
                walk(A_, four, end)
                i_evac(end * RING + (RING - 1), RING - 1)

            @block.tensor
            def _(pe):
                T_ = nc.tensor
                for g in range(2):
                    pe.wait_ge(st_s, ROWS + 1 + g)
                    T_.transpose(pX[:, 0, g * P:(g + 1) * P], rowsf[:, g], ident)
                    T_.matmul(pG[0:1, 0, g * P:(g + 1) * P], et[:, g:g + 1], ident, start=True, stop=True).then_inc(turned, 1)
                pe.wait_ge(ready, 1)
                pe.sem_inc(dn, RING)

                def x_turn(t, u):
                    pe.wait_ge(xl[u], ((t - u) * PER + 16))
                    if not (isinstance(t, int) and t < 2):
                        pe.wait_ge(xte, t - 1)
                    for j in range(FCH):
                        ins = T_.transpose(pX[:, u % 2, j * P:(j + 1) * P], X[:, u, j * P:(j + 1) * P], ident)
                    ins.then_inc(xt, 1)

                def gate_up(t, u, at):
                    pe.wait_ge(xte, t + 1)
                    pe.wait_ge(wl[u], (t - u) * PER + 16)
                    if not (isinstance(t, int) and t < 2):
                        pe.wait_ge(s_in, t - 1)
                    for j in range(FCH):
                        ins = T_.matmul(pG[:, u % 2, 0:2 * INTER], XT[:, u % 2, j * P:(j + 1) * P],
                                        W[:, bass.ds(at, 1), j * 2 * INTER:(j + 1) * 2 * INTER].rearrange("p o n -> p (o n)"),
                                        start=(j == 0), stop=(j == FCH - 1))
                    ins.then_inc(gu, 1)

                def i_turn(t, u):
                    pe.wait_ge(s_in, t + 1)
                    pe.wait_ge(ite, t)
                    T_.transpose(pI[:, 0:P], inter[:, u % 2], ident).then_inc(it, 1)

                def down(t, u, at):
                    pe.wait_ge(ite, t + 1)
                    if not (isinstance(t, int) and t < 2):
                        pe.wait_ge(yr, t - 1)
                    T_.matmul(pY[:, u % 2], interT[:, u % 2],
                              W[:, bass.ds(at, 1), FCH * 2 * INTER:WCOLS].rearrange("p o n -> p (o n)"), start=True, stop=True).then_inc(dn, 1)

                def place(t):
                    return pe.value_load(tab[0:1, 2, bass.ds(t, 1)], min_val=0, max_val=RING - 1)

                def four(i, head=False):
                    for u in range(RING):
                        t = i * RING + u
                        x_turn(t + 1, (u + 1) % RING)
                        gate_up(t, u, place(t))
                        if not (head and u < 2):
                            down(t - 2, (u - 2) % RING, place(t - 2))
                        if not (head and u == 0):
                            i_turn(t - 1, (u - 1) % RING)

                end = last_turn(pe)
                x_turn(0, 0)
                four(0, head=True)
                walk(T_, four, end)
                for u in (RING - 2, RING - 1):
                    t = end * RING + u
                    if u == RING - 1:
                        i_turn(t, u)
                    down(t, u, place(t))


ROWS = 3 + 12 + 2 + 10 + 4


def combine_phase(nc, y, keep, d, out, consts):
    with ExitStack() as ctx:
        sb = lambda n, s, dt=F32: ctx.enter_context(nc.sbuf_tensor("e_" + n, s, dt))
        sem = lambda n: ctx.enter_context(nc.semaphore("e_" + n))
        Gt = sb("G", [P, 2, TOPK, LEN])
        posi = sb("posi", [P, TILES * TOPK], I32)
        posc = sb("posc", [P, 2, TOPK], I32)
        rwc = sb("rwc", [P, 2, TOPK])
        acc = sb("acc", [P, 2, LEN])
        o = sb("o", [P, 2, LEN])
        bn, sta = sb("bn", [P, 6]), sb("sta", [P, 2, 6])
        s_posi, s_posc, passed, passed_v = sem("posi"), sem("posc"), sem("passed"), sem("passed_v")
        got = [sem(f"got{i}") for i in range(2 * TOPK)]
        sv, root, outr = sem("steps"), sem("root"), sem("out_ready")
        stored = [sem("stored0"), sem("stored1")]
        used = sem("used")
        PE_ = TOPK + 6
        with nc.Block() as block:
            @block.gpsimd
            def _(pool):
                G_ = nc.gpsimd
                pool.wait_ge(s_posi, 1)

                def tile(n, par, head):
                    if not head:
                        pool.wait_ge(used, n - 1)
                        pool.sem_inc(passed, 1)
                    G_.tensor_copy(posc[:, par], posi[:, bass.ds(n * TOPK, TOPK)]).then_inc(s_posc, 1)
                    pool.wait_ge(s_posc, n + 1)
                    pool.sem_inc(passed, 1)
                    for k in range(TOPK):
                        G_.indirect_dma_start(Gt[:, par, k], None, d["slots"],
                                              bass.IndirectOffsetOnAxis(ap=posc[:, par, k:k + 1], axis=0)).then_inc(got[par * TOPK + k], 16)
                tile(0, 0, True)
                tile(1, 1, True)
                with G_.Fori(1, TILES // 2) as i:
                    tile(i * 2, 0, False)
                    tile(i * 2 + 1, 1, False)

            @block.vector
            def _(dve):
                V_ = nc.vector
                V_.tensor_copy(posi[:], keep["slots"][:, 0:TILES * TOPK]).then_inc(s_posi, 1)
                st = Steps(sv)

                def do(ins, wait=True):
                    st.inc(ins)
                    if wait:
                        st.wait(dve)

                def tile(n, par, head):
                    st.start, st.n = n * PE_, 0
                    do(V_.tensor_copy(rwc[:, par], keep["rw"][:, bass.ds(n * TOPK, TOPK)]))
                    for k in range(TOPK):
                        dve.wait_ge(got[par * TOPK + k], (n - par) * 8 + 16)
                        before = y[:, bass.ds(n, 1)].rearrange("p o n -> p (o n)") if k == 0 else acc[:, par]
                        do(V_.scalar_tensor_tensor(acc[:, par], Gt[:, par, k], rwc[:, par, k:k + 1], before,
                                                   ALU.mult, ALU.add))
                    V_.tensor_copy(sta[:, par, 5:6], acc[:, par, 0:1]).then_inc(used, 1)
                    do(V_.bn_stats(bn[:], acc[:, par]))
                    dve.sem_inc(passed_v, 1)
                    do(V_.bn_aggr(sta[:, par, 0:2], bn[:]))
                    do(V_.tensor_scalar(sta[:, par, 2:3], sta[:, par, 1:2], EPS, None, ALU.add))
                    do(V_.reciprocal(sta[:, par, 3:4], sta[:, par, 2:3]))
                    dve.wait_ge(root, n + 1)
                    do(V_.scalar_tensor_tensor(sta[:, par, 5:6], sta[:, par, 0:1], -1.0, sta[:, par, 4:5], ALU.mult, ALU.mult), False)
                    assert st.n == PE_
                tile(0, 0, True)
                tile(1, 1, True)
                with V_.Fori(1, TILES // 2) as i:
                    tile(i * 2, 0, False)
                    tile(i * 2 + 1, 1, False)

            @block.scalar
            def _(act):
                def tile(n, par, head):
                    act.wait_ge(sv, n * PE_ + (TOPK + 5))
                    nc.scalar.activation(sta[:, par, 4:5], sta[:, par, 3:4], ACT.Sqrt).then_inc(root, 1)
                    act.wait_ge(sv, n * PE_ + PE_)
                    if not head:
                        act.wait_ge(stored[par], (n - par) * 8)
                    nc.scalar.activation(o[:, par], acc[:, par], ACT.Identity, bias=sta[:, par, 5:6], scale=sta[:, par, 4:5]).then_inc(outr, 1)
                tile(0, 0, True)
                tile(1, 1, True)
                with nc.scalar.Fori(1, TILES // 2) as i:
                    tile(i * 2, 0, False)
                    tile(i * 2 + 1, 1, False)

            @block.sync
            def _(sp):
                ov = out.rearrange("b (u p) n -> p (b u) n", p=P)
                with nc.sync.Fori(0, TILES // 2) as i:
                    for par in range(2):
                        n = i * 2 + par
                        sp.wait_ge(outr, n + 1)
                        sp.dma_start(ov[:, bass.ds(n, 1)].rearrange("p o n -> p (o n)"), o[:, par]).then_inc(stored[par], 16)
                for par in range(2):
                    sp.wait_ge(stored[par], 16 * TILES // 2)


def build(nc, d, out):
    with ExitStack() as ctx:
        consts_sb = ctx.enter_context(nc.sbuf_tensor("consts_sb", [P, d["consts"].shape[1]], F32))
        keep = keeps(nc, ctx)
        d["lists"] = nc.dram_tensor("lists", (EXPERTS * TOK, 1), I32, kind="Internal").ap()
        d["h1"] = nc.dram_tensor("h1", (TOK, LEN), F32, kind="Internal").ap()
        d["slots"] = nc.dram_tensor("slots", (MAX_TILES * P, LEN), F32, kind="Internal").ap()
        hT = ctx.enter_context(nc.sbuf_tensor("hT", [P, FCH, TOK], F32))
        wq = ctx.enter_context(nc.sbuf_tensor("wq", [P, FCH, LEN], F32))
        wq_loaded = ctx.enter_context(nc.semaphore("wq_loaded"))
        tok_phase(nc, d["w_qkv"], wq, wq_loaded, d["c"], d["log_dt"], d["log_w_real"], d["w_imag"], d["consts"], consts_sb, hT)
        y = ctx.enter_context(nc.sbuf_tensor("y", [P, TILES, LEN], F32))
        attention_phase(nc, hT, y, wq, wq_loaded, d["w_qkv"], [d["lq1"], d["lq2"], d["lk1"], d["lk2"]], consts_sb)
        mix_phase(nc, hT, y, keep, d, consts_sb)
        expert_phase(nc, keep, d, consts_sb)
        combine_phase(nc, y, keep, d, out, consts_sb)


def kernel(x, L0_tok_log_dt, L0_tok_log_w_real, L0_tok_w_imag, L0_attn_w_qkv, L0_attn_wo, L0_attn_lambda_q1,
           L0_attn_lambda_q2, L0_attn_lambda_k1, L0_attn_lambda_k2, L0_attn_gamma, L0_attn_beta, L0_ffn_gate_w,
           L0_ffn_gu_w, L0_ffn_dp_w, L0_ffn_sh_gate_w, L0_ffn_sh_up_w, L0_ffn_sh_down_w, L0_ffn_sh_gate1_w):
    import numpy as _np
    import concourse.bacc as _bacc
    from concourse import mybir as _mybir
    from concourse.bass_utils import run_bass_kernel_spmd as _run

    lay = _np.ascontiguousarray
    gu = _np.asarray(L0_ffn_gu_w).transpose(0, 2, 1).reshape(EXPERTS, FCH, P, 2 * INTER).transpose(0, 2, 1, 3)
    w_experts = _np.concatenate([gu.reshape(EXPERTS, P, FCH * 2 * INTER), _np.asarray(L0_ffn_dp_w).transpose(0, 2, 1)], 2)
    w_joint = _np.concatenate([_np.asarray(a) for a in (L0_ffn_gate_w, L0_ffn_sh_up_w, L0_ffn_sh_gate_w, L0_ffn_sh_gate1_w)], 0).T
    arrays = {
        "c": _np.asarray(x).transpose(3, 2, 1, 0), "log_dt": L0_tok_log_dt,
        "log_w_real": _np.asarray(L0_tok_log_w_real).T, "w_imag": _np.asarray(L0_tok_w_imag).T,
        "w_qkv": _np.asarray(L0_attn_w_qkv).T, "wo": _np.asarray(L0_attn_wo).T,
        "lq1": L0_attn_lambda_q1, "lq2": L0_attn_lambda_q2, "lk1": L0_attn_lambda_k1, "lk2": L0_attn_lambda_k2,
        "gamma": L0_attn_gamma, "beta": L0_attn_beta, "w_joint": w_joint, "sh_down": _np.asarray(L0_ffn_sh_down_w).T,
        "w_experts": w_experts, "consts": const_table(),
    }
    arrays = {"in_" + n: lay(_np.asarray(a)) for n, a in arrays.items()}
    nc = _bacc.Bacc("TRN2", target_bir_lowering=False, num_devices=1)
    d = {n[3:]: nc.dram_tensor(n, a.shape, _mybir.dt.from_np(a.dtype), kind="ExternalInput").ap() for n, a in arrays.items()}
    out = nc.dram_tensor("out", (BATCH, SEQ, LEN), _mybir.dt.float32, kind="ExternalOutput").ap()
    build(nc, d, out)
    r = _run(nc, [arrays], core_ids=[0])
    return r.results[0]["out"]
```
